# Optimizing a Trainium2 kernel written in Bass

```python
import numpy as np
import jax
import jax.numpy as jnp

def _softmax(x, axis=-1):
    return jax.nn.softmax(x, axis=axis)

def _gelu(x):
    return jax.nn.gelu(x, approximate=True)

def _silu(x):
    return jax.nn.silu(x)

def _sigmoid(x):
    return jax.nn.sigmoid(x)

def _layernorm(x, axis=-1, eps=1e-05):
    m = jnp.mean(x, axis=axis, keepdims=True)
    v = jnp.var(x, axis=axis, keepdims=True)
    return (x - m) / jnp.sqrt(v + eps)

def _scatter_add(tgt, idx, src, axis=0):
    return tgt.at[idx].add(src)

def _segment_sum(src, seg, n):
    return jax.ops.segment_sum(src, seg, n)
kernel_name = 'mk_lm_tower_d1_tok_ids2048_r4_dfc9c4'

def setup_inputs(seed: int=0):
    np.random.seed(seed)
    _w = jnp.asarray

    def _rec_inputs():
        import jax
        import jax.numpy as jnp
        _rk = jax.random.key(seed)
        x = jax.random.randint(jax.random.fold_in(_rk, 1), (4, 1024), 0, 127990, jnp.int32)
        return x
    x = _rec_inputs()

    def _L0_tok_setup():
        import jax, jax.numpy as jnp
        import numpy as np
        VOCAB = 32000
        EMBED = 512
        N_TRAIN = 64
        BATCH, SEQ = (4, 1024)
        key = jax.random.key(seed)
        k1, k2, k3, k4 = jax.random.split(key, 4)
        x = jax.random.randint(k1, (BATCH, SEQ), 0, VOCAB, dtype=jnp.int64 if jax.config.jax_enable_x64 else jnp.int32)
        W = jax.random.normal(k2, (VOCAB, EMBED), dtype=jnp.float32)
        delta_values = jax.random.normal(k3, (N_TRAIN * EMBED,), dtype=jnp.float32)
        token_indices = jnp.sort(jax.random.randint(k4, (N_TRAIN,), 0, VOCAB, dtype=jnp.int32))
        return {'x': x, 'W': W, 'delta_values': delta_values, 'token_indices': token_indices}
    _L0_tok_all = _L0_tok_setup()
    _L0_tok_in = {k: v for k, v in _L0_tok_all.items() if k in ('W', 'delta_values', 'token_indices')}
    del _L0_tok_all

    def _L0_attn_setup():
        import jax, jax.numpy as jnp
        import numpy as np
        HIDDEN = 512
        NUM_HEADS = 32
        NUM_KV_HEADS = 8
        HEAD_DIM = HIDDEN // NUM_HEADS
        key = jax.random.key(seed)
        ks = jax.random.split(key, 5)
        s = 0.02
        x = jax.random.normal(ks[0], (2, 512, HIDDEN), dtype=jnp.float32)
        Wq = jax.random.normal(ks[1], (HIDDEN, NUM_HEADS * HEAD_DIM), dtype=jnp.float32) * s
        Wk = jax.random.normal(ks[2], (HIDDEN, NUM_KV_HEADS * HEAD_DIM), dtype=jnp.float32) * s
        Wv = jax.random.normal(ks[3], (HIDDEN, NUM_KV_HEADS * HEAD_DIM), dtype=jnp.float32) * s
        Wo = jax.random.normal(ks[4], (NUM_HEADS * HEAD_DIM, HIDDEN), dtype=jnp.float32) * s
        return {'x': x, 'Wq': Wq, 'Wk': Wk, 'Wv': Wv, 'Wo': Wo}
    _L0_attn_all = _L0_attn_setup()
    _L0_attn_in = {k: v for k, v in _L0_attn_all.items() if k in ('Wq', 'Wk', 'Wv', 'Wo')}
    del _L0_attn_all

    def _L0_ffn_setup():
        import jax, jax.numpy as jnp
        import numpy as np
        EPS = 1e-05

        def rms_norm(x):
            return x * jax.lax.rsqrt(jnp.mean(x * x, axis=-1, keepdims=True) + EPS)

        def act_quant(x):
            scale = 127.0 / jnp.clip(jnp.max(jnp.abs(x), axis=-1, keepdims=True), 1e-05)
            q = jnp.clip(jnp.round(x * scale), -128.0, 127.0) / scale
            return x + jax.lax.stop_gradient(q - x)

        def weight_quant(w):
            scale = 1.0 / jnp.clip(jnp.mean(jnp.abs(w)), 1e-05)
            q = jnp.clip(jnp.round(w * scale), -1.0, 1.0) / scale
            return w + jax.lax.stop_gradient(q - w)

        def bitlinear158(x, w, b):
            xq = act_quant(rms_norm(x))
            wq = weight_quant(w)
            return jnp.einsum('bsd,od->bso', xq, wq) + b

        def layer_norm(x, g, b):
            mu = jnp.mean(x, axis=-1, keepdims=True)
            var = jnp.mean((x - mu) ** 2, axis=-1, keepdims=True)
            return (x - mu) * jax.lax.rsqrt(var + EPS) * g + b
        key = jax.random.key(seed)
        ks = jax.random.split(key, 3)
        d, inner = (512, 2048)
        x = jax.random.normal(ks[0], (4, 512, d), dtype=jnp.float32)
        w1 = jax.random.normal(ks[1], (inner, d), dtype=jnp.float32) * 0.02
        b1 = jnp.zeros((inner,), jnp.float32)
        ln_g = jnp.ones((inner,), jnp.float32)
        ln_b = jnp.zeros((inner,), jnp.float32)
        w2 = jax.random.normal(ks[2], (d, inner), dtype=jnp.float32) * 0.02
        b2 = jnp.zeros((d,), jnp.float32)
        return {'x': x, 'w1': w1, 'b1': b1, 'ln_g': ln_g, 'ln_b': ln_b, 'w2': w2, 'b2': b2}
    _L0_ffn_all = _L0_ffn_setup()
    _L0_ffn_in = {k: v for k, v in _L0_ffn_all.items() if k in ('w1', 'b1', 'ln_g', 'ln_b', 'w2', 'b2')}
    del _L0_ffn_all
    return {'x': x, 'L0_tok_W': _L0_tok_in['W'], 'L0_tok_delta_values': _L0_tok_in['delta_values'], 'L0_tok_token_indices': _L0_tok_in['token_indices'], 'L0_attn_Wq': _L0_attn_in['Wq'], 'L0_attn_Wk': _L0_attn_in['Wk'], 'L0_attn_Wv': _L0_attn_in['Wv'], 'L0_attn_Wo': _L0_attn_in['Wo'], 'L0_ffn_w1': _L0_ffn_in['w1'], 'L0_ffn_b1': _L0_ffn_in['b1'], 'L0_ffn_ln_g': _L0_ffn_in['ln_g'], 'L0_ffn_ln_b': _L0_ffn_in['ln_b'], 'L0_ffn_w2': _L0_ffn_in['w2'], 'L0_ffn_b2': _L0_ffn_in['b2']}

def reference(x, L0_tok_W, L0_tok_delta_values, L0_tok_token_indices, L0_attn_Wq, L0_attn_Wk, L0_attn_Wv, L0_attn_Wo, L0_ffn_w1, L0_ffn_b1, L0_ffn_ln_g, L0_ffn_ln_b, L0_ffn_w2, L0_ffn_b2):
    import jax
    import jax.numpy as jnp

    def _L0_tok_ref(x, W, delta_values, token_indices):
        import jax, jax.numpy as jnp
        import numpy as np
        VOCAB = 32000
        EMBED = 512
        N_TRAIN = 64
        BATCH, SEQ = (4, 1024)
        delta = delta_values.reshape(EMBED, N_TRAIN).T
        W_eff = W.at[token_indices].add(delta)
        return W_eff[x]

    def _L0_attn_ref(x, Wq, Wk, Wv, Wo):
        import jax, jax.numpy as jnp
        import numpy as np
        HIDDEN = 512
        NUM_HEADS = 32
        NUM_KV_HEADS = 8
        HEAD_DIM = HIDDEN // NUM_HEADS
        b, s, _ = x.shape
        q = (x @ Wq).reshape(b, s, NUM_HEADS, HEAD_DIM).transpose(0, 2, 1, 3)
        k = (x @ Wk).reshape(b, s, NUM_KV_HEADS, HEAD_DIM).transpose(0, 2, 1, 3)
        v = (x @ Wv).reshape(b, s, NUM_KV_HEADS, HEAD_DIM).transpose(0, 2, 1, 3)
        rep = NUM_HEADS // NUM_KV_HEADS
        k = jnp.repeat(k, rep, axis=1)
        v = jnp.repeat(v, rep, axis=1)
        scale = HEAD_DIM ** (-0.5)
        attn = jnp.einsum('bhqd,bhkd->bhqk', q, k) * scale
        attn = jax.nn.softmax(attn, axis=-1)
        out = jnp.einsum('bhqk,bhkd->bhqd', attn, v)
        out = out.transpose(0, 2, 1, 3).reshape(b, s, NUM_HEADS * HEAD_DIM)
        return out @ Wo

    def _L0_ffn_ref(x, w1, b1, ln_g, ln_b, w2, b2):
        import jax, jax.numpy as jnp
        import numpy as np
        EPS = 1e-05

        def rms_norm(x):
            return x * jax.lax.rsqrt(jnp.mean(x * x, axis=-1, keepdims=True) + EPS)

        def act_quant(x):
            scale = 127.0 / jnp.clip(jnp.max(jnp.abs(x), axis=-1, keepdims=True), 1e-05)
            q = jnp.clip(jnp.round(x * scale), -128.0, 127.0) / scale
            return x + jax.lax.stop_gradient(q - x)

        def weight_quant(w):
            scale = 1.0 / jnp.clip(jnp.mean(jnp.abs(w)), 1e-05)
            q = jnp.clip(jnp.round(w * scale), -1.0, 1.0) / scale
            return w + jax.lax.stop_gradient(q - w)

        def bitlinear158(x, w, b):
            xq = act_quant(rms_norm(x))
            wq = weight_quant(w)
            return jnp.einsum('bsd,od->bso', xq, wq) + b

        def layer_norm(x, g, b):
            mu = jnp.mean(x, axis=-1, keepdims=True)
            var = jnp.mean((x - mu) ** 2, axis=-1, keepdims=True)
            return (x - mu) * jax.lax.rsqrt(var + EPS) * g + b
        h = jax.nn.silu(bitlinear158(x, w1, b1))
        h = jax.nn.gelu(h, approximate=False)
        h = layer_norm(h, ln_g, ln_b)
        return bitlinear158(h, w2, b2)
    h = _L0_tok_ref(x, L0_tok_W, L0_tok_delta_values, L0_tok_token_indices)
    h = h + _L0_attn_ref(_layernorm(h, axis=-1), L0_attn_Wq, L0_attn_Wk, L0_attn_Wv, L0_attn_Wo)
    h = h + _L0_ffn_ref(_layernorm(h, axis=-1), L0_ffn_w1, L0_ffn_b1, L0_ffn_ln_g, L0_ffn_ln_b, L0_ffn_w2, L0_ffn_b2)
    return h

_drawn_inputs = setup_inputs


def setup_inputs(seed=0):
    import zlib

    import numpy as np

    out = dict(_drawn_inputs(seed))
    spreads = {'L0_ffn_b1': (0.0, 0.1),
     'L0_ffn_ln_g': (1.0, 0.2),
     'L0_ffn_ln_b': (0.0, 0.1),
     'L0_ffn_b2': (0.0, 0.1)}
    factors = {'L0_attn_Wq': 5.52, 'L0_attn_Wk': 4.837}
    for name, (base, spread) in spreads.items():
        noise = np.random.default_rng([zlib.crc32(name.encode()), seed]).standard_normal(out[name].shape)
        drawn = base * np.exp(spread * noise) if base else spread * noise
        out[name] = jnp.asarray(drawn.astype(out[name].dtype))
    for name, factor in factors.items():
        out[name] = (out[name] * factor).astype(out[name].dtype)
    return out
```

```python
from contextlib import ExitStack

import concourse.bass as bass
from concourse import mybir

F32 = mybir.dt.float32
BF16 = mybir.dt.bfloat16
I32 = mybir.dt.int32
U32 = mybir.dt.uint32
ALU = mybir.AluOpType
ACT = mybir.ActivationFunctionType
AX = mybir.AxisListType.X

P = 128
BATCH, SEQ = 4, 1024
TOKENS = BATCH * SEQ
VOCAB, D = 32000, 512
N_TRAIN = 64
HEADS, KV_HEADS, HD = 32, 8, 16
REP = HEADS // KV_HEADS
INNER = 2048
EPS = 1e-5
ROUND = 1.5 * 2.0 ** 23

DC = D // P
TB = SEQ // P
NT = TOKENS // P
IC = INNER // P
HC = HEADS * HD // P
BANK = 512
QH = SEQ // BANK
UC = INNER // BANK

Q_PARTS = (0, 0, 0, 1, 1, 2)
K_PARTS = (0, 1, 2, 0, 1, 0)
PART_ROWS = len(Q_PARTS) * HD
MAX_ROWS = 2
SCORE_ROWS = PART_ROWS + MAX_ROWS
VW = 32
QK_SLOTS = 3

GROUP_SCORES = REP * TB
S1_BLOCKS = REP * TB * QH
S1_USES = S1_BLOCKS + 1
S1_SPREAD = 24


class Names:
    pass


def semaphores(nc, stack):
    def sem(name):
        return stack.enter_context(nc.semaphore(name))

    setup = Names()
    setup.small = sem("small_loaded")
    setup.proj_w = sem("proj_weights_loaded")
    setup.ffn_w = [sem("w1_staged"), sem("w2_staged")]
    setup.const = sem("constants_set")
    setup.vec = sem("setup_vector_chain")
    setup.abs_sum = sem("abs_sum_ready")
    setup.abs_tot = sem("abs_total_ready")
    setup.w1_read = sem("w1_stage_read")
    gather = [sem(f"gathered{t}") for t in range(TB)]
    first = sem("batch_first")
    batch = Names()
    batch.gather = gather
    batch.x_row = sem("x_row_loaded")
    batch.idx = sem("indices_copied")
    batch.hot = sem("one_hot_ready")
    batch.delta = sem("delta_in_psum")
    batch.h0 = sem("h0_ready")
    batch.h0_stored = sem("h0_stored")
    batch.p_vec = sem("project_vector_chain")
    batch.p_var = sem("variance_ready")
    batch.p_rstd = sem("rstd_ready")
    batch.p_norm = sem("normalised_ready")
    batch.x_tr = sem("x_transposes_in_psum")
    batch.x_t = sem("x_t_ready")
    batch.v_ps = sem("v_in_psum")
    batch.v_sb = sem("v_ready")
    batch.v_const = sem("v_ones_set")
    batch.qk_ps = sem("qk_in_psum")
    batch.qk_hi = sem("qk_high_ready")
    batch.qk_r1 = sem("qk_remainder_ready")
    batch.qk_mid = sem("qk_middle_ready")
    batch.qk_lo = sem("qk_low_ready")
    batch.part_st = [sem(f"qk_parts_stored{i}") for i in range(2)]
    batch.qk_load = [sem(f"qk_parts_loaded{i}") for i in range(QK_SLOTS)]
    batch.ones = sem("score_ones_set")
    batch.s1 = sem("stage1_in_psum")
    batch.s1_read = sem("stage1_read")
    batch.a_vec = sem("attend_vector_chain")
    batch.negmax = sem("negmax_ready")
    batch.mrow = sem("max_rows_ready")
    batch.mrow_st = sem("max_rows_stored")
    batch.mrow_ld = sem("max_rows_loaded")
    batch.s2 = sem("stage2_in_psum")
    batch.exp = sem("exp_ready")
    batch.pv = sem("pv_done")
    batch.o = sem("outputs_ready")
    batch.sum_st = sem("sums_stored")
    batch.sum_ld = sem("sums_loaded")
    batch.rec = sem("reciprocals_ready")
    batch.rec_st = sem("reciprocals_stored")
    batch.rec_ld = sem("reciprocals_loaded")
    batch.on = sem("outputs_normalised")
    batch.at = sem("attn_t_landed")
    batch.f_h = [sem(f"h0_loaded{t}") for t in range(TB)]
    batch.wo = sem("wo_in_psum")
    batch.h1 = sem("h1_ready")
    batch.f_vec = sem("ffn_vector_chain")
    batch.f_pool = sem("ffn_pool_chain")
    batch.f_var = sem("h1_variance_ready")
    batch.f_r0 = sem("h1_rstd_ready")
    batch.x2 = sem("x2_ready")
    batch.x2_ss = sem("x2_squares_ready")
    batch.x2_r = sem("x2_rms_ready")
    batch.xq = sem("xq_ready")
    batch.xq_tr = sem("xq_transposes_in_psum")
    batch.xq_t = sem("xq_t_ready")
    batch.u_ps = sem("u_in_psum")
    batch.u = sem("u_ready")
    batch.silu = sem("silu_ready")
    batch.gelu = sem("gelu_ready")
    batch.g_var = sem("g_variance_ready")
    batch.g_scaled = sem("g_scaled_ready")
    batch.y = sem("y_ready")
    batch.y_ss = sem("y_squares_ready")
    batch.y_r = sem("y_rms_ready")
    batch.y_qs = sem("y_scale_ready")
    batch.y_shift = sem("y_shifted_ready")
    batch.yq = sem("yq_ready")
    batch.yq_tr = sem("yq_transposes_in_psum")
    batch.yq_t = sem("yq_t_ready")
    batch.o_ps = sem("ffn_out_in_psum")
    batch.f_o = sem("ffn_out_ready")
    batch.out_st = [sem(f"out_stored{i}") for i in range(4)]
    last = sem("batch_last")
    return setup, batch, range(first.num, last.num + 1)


def rows_of(weights):
    return weights.rearrange("(c p) n -> p c n", p=P)


def set_up(nc, S, M, A):
    with ExitStack() as ctx:
        def sb(name, shape, dt=F32):
            return ctx.enter_context(nc.sbuf_tensor(name, shape, dt))

        xc_i = sb("xc_i", [P, NT], I32)
        xc_f = sb("xc_f", [P, NT])
        xc_n = sb("xc_n", [P, NT])
        t_i = sb("t_i", [P, 1], I32)
        t_n = sb("t_n", [P, 1])
        dl = sb("dl", [P, D])
        dl_bf = sb("dl_bf", [P, D], BF16)
        dl_r1 = sb("dl_r1", [P, D])
        dl_r2 = sb("dl_r2", [P, D])
        stage = sb("stage", [P, DC * INNER])
        abs_part = sb("abs_part", [P, 16])
        abs_sum = sb("abs_sum", [P, 2])
        abs_tot = sb("abs_tot", [P, 2])
        w_scale = sb("w_scale", [P, 2])
        block = ctx.enter_context(nc.Block())

        @block.sync
        def _(sp):
            sp.dma_start(rows_of_stage(stage, DC), rows_of(A.w1t)).then_inc(S.ffn_w[0], 16)
            sp.dma_start(xc_i[:], A.x_col).then_inc(S.small, 16)
            for half in range(2):
                rows = slice(half * N_TRAIN, (half + 1) * N_TRAIN)
                sp.dma_start(t_i[rows, :], A.tokens).then_inc(S.small, 16)
                sp.dma_start(dl[rows, :], A.delta_t).then_inc(S.small, 16)
            for dst, src in ((M.wq, A.wq), (M.wk, A.wk), (M.wv, A.wv), (M.wo, A.wo)):
                sp.dma_start(dst[:], rows_of(src)).then_inc(S.proj_w, 16)
            for dst, src in ((M.b1, A.b1), (M.ln_g, A.ln_g), (M.ln_b, A.ln_b), (M.b2, A.b2)):
                sp.dma_start(dst[:], src.partition_broadcast(P)).then_inc(S.proj_w, 16)
            sp.wait_ge(S.w1_read, 1)
            sp.dma_start(rows_of_stage(stage, IC), rows_of(A.w2t)).then_inc(S.ffn_w[1], 16)
            sp.wait_ge(S.proj_w, 8 * 16)

        @block.gpsimd
        def _(pool):
            pool.memset(M.ident[:], 0.0).then_inc(S.const, 1)
            pool.memset(M.neg_half[:], -0.5).then_inc(S.const, 1)
            pool.memset(M.round_c[:], ROUND).then_inc(S.const, 1)
            pool.wait_ge(S.const, 3)
            pool.affine_select(out=M.ident[:], in_=M.ident[:], compare_op=ALU.not_equal, fill=1.0, base=0,
                               pattern=[[-1, P]], channel_multiplier=1).then_inc(S.const, 1)
            for w in range(2):
                pool.wait_ge(S.abs_sum, w + 1)
                pool.partition_all_reduce(abs_tot[:, w:w + 1], abs_sum[:, w:w + 1], P,
                                          bass.bass_isa.ReduceOp.add).then_inc(S.abs_tot, 1)

        @block.vector
        def _(dve):
            n = [0]

            def link(ins):
                n[0] += 1
                ins.then_inc(S.vec, 1)
                dve.wait_ge(S.vec, n[0])

            dve.wait_ge(S.const, 4)
            link(dve.tensor_copy(M.ident_bf[:], M.ident[:]))
            dve.wait_ge(S.small, 5 * 16)

            link(dve.tensor_copy(xc_f[:], xc_i[:]))
            link(dve.tensor_scalar(xc_n[:], xc_f[:], 0.0, float(VOCAB), ALU.is_lt, ALU.mult))
            link(dve.tensor_tensor(xc_f[:], xc_f[:], xc_n[:], ALU.add))
            link(dve.tensor_scalar(xc_f[:], xc_f[:], 0.0, float(VOCAB - 1), ALU.max, ALU.min))
            link(dve.tensor_copy(M.idx_all[:], xc_f[:]))
            link(dve.tensor_copy(M.tok[:], t_i[:]))
            link(dve.tensor_scalar(t_n[:], M.tok[:], 0.0, float(VOCAB), ALU.is_lt, ALU.mult))
            link(dve.tensor_tensor(M.tok[:], M.tok[:], t_n[:], ALU.add))
            lower, upper = slice(0, N_TRAIN), slice(N_TRAIN, P)
            link(dve.tensor_copy(dl_bf[:], dl[:]))
            link(dve.tensor_tensor(dl_r1[:], dl[:], dl_bf[:], ALU.subtract))
            link(dve.tensor_copy(M.d_hm[lower, :], dl_bf[lower, :]))
            link(dve.tensor_copy(M.d_hm[upper, :], dl_r1[upper, :]))
            link(dve.tensor_copy(dl_bf[:], dl_r1[:]))
            link(dve.tensor_tensor(dl_r2[:], dl_r1[:], dl_bf[:], ALU.subtract))
            link(dve.memset(M.d_lo[:], 0.0))
            link(dve.tensor_copy(M.d_lo[lower, :], dl_r2[lower, :]))

            for w, dst in enumerate((M.w1q, M.w2q)):
                dve.wait_ge(S.ffn_w[w], 16)
                link(dve.tensor_reduce(abs_part[:], stage[:].rearrange("p (c n) -> p c n", c=16), AX,
                                       ALU.add, apply_absolute_value=True))
                dve.tensor_reduce(abs_sum[:, w:w + 1], abs_part[:], AX, ALU.add).then_inc(S.abs_sum, 1)
                dve.wait_ge(S.abs_tot, w + 1)
                link(dve.tensor_scalar(M.w_mean[:, w:w + 1], abs_tot[:, w:w + 1], 1.0 / (D * INNER), 1e-5,
                                       ALU.mult, ALU.max))
                link(dve.reciprocal(w_scale[:, w:w + 1], M.w_mean[:, w:w + 1]))
                link(dve.tensor_scalar(M.w_dq[:, w:w + 1], M.w_mean[:, w:w + 1], 1.0 / 127.0, None, ALU.mult))
                link(dve.tensor_scalar(stage[:], stage[:], w_scale[:, w:w + 1], 1.0, ALU.mult, ALU.min))
                link(dve.tensor_scalar(stage[:], stage[:], -1.0, ROUND, ALU.max, ALU.add))
                last = dve.tensor_scalar(dst[:].rearrange("p c n -> p (c n)"), stage[:], ROUND, None,
                                         ALU.subtract)
                last.then_inc(S.w1_read, 1)


def rows_of_stage(stage, chunks):
    return stage[:].rearrange("p (c n) -> p c n", c=chunks)


def project(nc, S, M, A, b):
    with ExitStack() as ctx:
        def sb(name, shape, dt=F32):
            return ctx.enter_context(nc.sbuf_tensor(name, shape, dt))

        def ps(name, shape, dt=F32):
            return ctx.enter_context(nc.psum_tensor(name, shape, dt))

        x_i = sb("x_i", [P, SEQ], I32)
        x_f = sb("x_f", [P, SEQ])
        x_n = sb("x_n", [P, SEQ])
        hot = sb("hot", [P, SEQ], BF16)
        h = sb("h", [P, TB, D])
        stats = sb("p_stats", [P, TB, 6])
        mv = sb("p_mv", [P, TB, 2])
        veps = sb("p_veps", [P, TB])
        rstd = sb("p_rstd_sb", [P, TB])
        xn = sb("xn", [P, 2, D])
        x_t = sb("x_t", [P, DC, SEQ])
        r1 = sb("r1", [P, 2, BANK])
        parts = sb("parts", [P, 2, 3, BANK], BF16)
        ps_d = ps("ps_d", [P, 2, BANK])
        ps_t = ps("ps_t", [P, 2, BANK])
        ps_v = ps("ps_v", [P, BANK])
        ps_q = ps("ps_q", [P, 2, BANK])
        block = ctx.enter_context(nc.Block())
        qk_items = [(half, m) for half in range(QH) for m in range(HC + 1)]
        half_tiles = TB // QH

        @block.sync
        def _(sp):
            sp.dma_start(x_i[:], A.x_row[bass.ds(b * SEQ, SEQ)].partition_broadcast(P)).then_inc(S.x_row, 16)
            for t in range(TB):
                sp.wait_ge(S.h0, t + 1)
                sp.dma_start(A.h_dram[bass.ds(b * SEQ + t * P, P), :], h[:, t, :]).then_inc(S.h0_stored, 16)
            for n, (half, m) in enumerate(qk_items):
                sp.wait_ge(S.qk_lo, n + 1)
                cols = slice(half * BANK, (half + 1) * BANK)
                dst = A.q_dram[:, m, :, cols] if m < HC else A.k_dram[:, :, cols]
                sp.dma_start(dst.rearrange("s p t -> p s t"), parts[:, n % 2]).then_inc(S.part_st[n % 2], 16)
            sp.wait_ge(S.h0_stored, TB * 16)
            for i in range(2):
                sp.wait_ge(S.part_st[i], len(qk_items) // 2 * 16)

        @block.gpsimd
        def _(pool):
            pool.tensor_copy(M.idx_b[:], M.idx_all[:, bass.ds(b * TB, TB)]).then_inc(S.idx, 1)
            pool.wait_ge(S.idx, 1)
            for t in range(TB):
                pool.indirect_dma_start(out=h[:, t, :], out_offset=None, in_=A.W,
                                        in_offset=bass.IndirectOffsetOnAxis(ap=M.idx_b[:, t:t + 1], axis=0),
                                        ).then_inc(S.gather[t], 16)
            pool.memset(M.v[:], 0.0).then_inc(S.v_const, 1)
            pool.wait_ge(S.v_const, 1)
            pool.memset(M.v[:, :, :, 0:1], 1.0).then_inc(S.v_const, 1)
            for t in range(TB):
                pool.wait_ge(S.p_var, t + 1)
                pool.tensor_tensor(rstd[:, t:t + 1], veps[:, t:t + 1], M.neg_half[:], ALU.pow).then_inc(S.p_rstd, 1)
            for n in range(len(qk_items)):
                pool.wait_ge(S.qk_mid, n + 1)
                if n >= 2:
                    pool.wait_ge(S.part_st[n % 2], n // 2 * 16)
                pool.tensor_tensor(parts[:, n % 2, 2, :], r1[:, n % 2, :], parts[:, n % 2, 1, :],
                                   ALU.subtract).then_inc(S.qk_lo, 1)

        @block.vector
        def _(dve):
            n = [0]

            def link(ins):
                n[0] += 1
                ins.then_inc(S.p_vec, 1)
                dve.wait_ge(S.p_vec, n[0])

            dve.wait_ge(S.x_row, 16)
            link(dve.tensor_copy(x_f[:], x_i[:]))
            link(dve.tensor_scalar(x_n[:], x_f[:], 0.0, float(VOCAB), ALU.is_lt, ALU.mult))
            link(dve.tensor_tensor(x_f[:], x_f[:], x_n[:], ALU.add))
            link(dve.tensor_scalar(x_f[:], x_f[:], 0.0, float(VOCAB - 1), ALU.max, ALU.min))
            dve.tensor_scalar(hot[:], x_f[:], M.tok[:], None, ALU.is_equal).then_inc(S.hot, 1)

            def embed(t):
                dve.wait_ge(S.gather[t], b * 16 + 16)
                dve.wait_ge(S.delta, t + 1)
                dve.tensor_tensor(h[:, t, :], h[:, t, :], ps_d[:, t % 2, :], ALU.add).then_inc(S.h0, 1)
                dve.wait_ge(S.h0, t + 1)
                link(dve.bn_stats(stats[:, t, :], h[:, t, :]))
                link(dve.bn_aggr(mv[:, t, :], stats[:, t, :]))
                dve.tensor_scalar(veps[:, t:t + 1], mv[:, t, 1:2], EPS, None, ALU.add).then_inc(S.p_var, 1)

            def normalise(t):
                dve.wait_ge(S.p_rstd, t + 1)
                if t >= 2:
                    dve.wait_ge(S.x_tr, t - 1)
                dve.tensor_scalar(xn[:, t % 2, :], h[:, t, :], mv[:, t, 0:1], rstd[:, t:t + 1],
                                  ALU.subtract, ALU.mult).then_inc(S.p_norm, 1)

            def remainder(i):
                scale = HD ** -0.5 if qk_items[i][1] < HC else 1.0
                dve.wait_ge(S.qk_hi, i + 1)
                if i >= 2:
                    dve.wait_ge(S.qk_lo, i - 1)
                dve.scalar_tensor_tensor(out=r1[:, i % 2, :], in0=ps_q[:, i % 2, :], scalar=scale,
                                         in1=parts[:, i % 2, 0, :], op0=ALU.mult,
                                         op1=ALU.subtract).then_inc(S.qk_r1, 1)

            for t in range(TB + 1):
                if t < TB:
                    embed(t)
                if t >= 1:
                    normalise(t - 1)
            for i in range(len(qk_items)):
                remainder(i)

        @block.scalar
        def _(act):
            def copy_x_t(t):
                act.wait_ge(S.x_tr, t + 1)
                act.activation(x_t[:, :, t * P:(t + 1) * P],
                               ps_t[:, t % 2, :].rearrange("p (c t) -> p c t", c=DC), ACT.Copy).then_inc(S.x_t, 1)

            def copy_v(t):
                act.wait_ge(S.v_ps, t + 1)
                if t == 0:
                    act.wait_ge(S.v_const, 2)
                act.activation(M.v[:, t, :, 1:1 + HD],
                               ps_v[:, 0:KV_HEADS * HD].rearrange("p (g d) -> p g d", g=KV_HEADS),
                               ACT.Copy).then_inc(S.v_sb, 1)

            def split(i):
                scale = HD ** -0.5 if qk_items[i][1] < HC else 1.0
                act.wait_ge(S.qk_ps, i + 1)
                if i >= 2:
                    act.wait_ge(S.part_st[i % 2], i // 2 * 16)
                act.activation(parts[:, i % 2, 0, :], ps_q[:, i % 2, :], ACT.Copy, scale=scale).then_inc(S.qk_hi, 1)
                act.wait_ge(S.qk_r1, i + 1)
                act.activation(parts[:, i % 2, 1, :], r1[:, i % 2, :], ACT.Copy).then_inc(S.qk_mid, 1)

            for t in range(TB):
                copy_x_t(t)
                copy_v(t)
            for i in range(len(qk_items)):
                split(i)

        @block.tensor
        def _(pe):
            def add_delta(t):
                if t >= 2:
                    pe.wait_ge(S.h0, t - 1)
                pe.matmul(ps_d[:, t % 2, :], hot[:, t * P:(t + 1) * P], M.d_hm[:], start=True, stop=False)
                pe.matmul(ps_d[:, t % 2, :], hot[:, t * P:(t + 1) * P], M.d_lo[:], start=False,
                          stop=True).then_inc(S.delta, 1)

            def transposes(t):
                pe.wait_ge(S.p_norm, t + 1)
                if t >= 2:
                    pe.wait_ge(S.x_t, t - 1)
                for c in range(DC):
                    last = pe.transpose(ps_t[:, t % 2, c * P:(c + 1) * P], xn[:, t % 2, c * P:(c + 1) * P],
                                        M.ident[:])
                last.then_inc(S.x_tr, 1)

            def values(t):
                pe.wait_ge(S.x_t, t + 1)
                if t >= 1:
                    pe.wait_ge(S.v_sb, t)
                for c in range(DC):
                    last = pe.matmul(ps_v[:, 0:KV_HEADS * HD], x_t[:, c, t * P:(t + 1) * P], M.wv[:, c, :],
                                     start=(c == 0), stop=(c == DC - 1))
                last.then_inc(S.v_ps, 1)

            def queries_keys(i):
                half, m = qk_items[i]
                w = M.wq[:, :, m * P:(m + 1) * P] if m < HC else M.wk[:]
                if i >= 2:
                    pe.wait_ge(S.qk_r1, i - 1)
                for c in range(DC):
                    last = pe.matmul(ps_q[:, i % 2, :], w[:, c, :], x_t[:, c, half * BANK:(half + 1) * BANK],
                                     start=(c == 0), stop=(c == DC - 1))
                last.then_inc(S.qk_ps, 1)

            pe.wait_ge(S.hot, 1)
            add_delta(0)
            for t in range(TB):
                if t + 1 < TB:
                    add_delta(t + 1)
                transposes(t)
                values(t)
            for i in range(len(qk_items)):
                queries_keys(i)


def attend(nc, S, M, A, b):
    with ExitStack() as ctx:
        def sb(name, shape, dt=F32):
            return ctx.enter_context(nc.sbuf_tensor(name, shape, dt))

        def ps(name, shape, dt=F32):
            return ctx.enter_context(nc.psum_tensor(name, shape, dt))

        q6 = [sb(f"q6_{i}", [SCORE_ROWS, REP, SEQ], BF16) for i in range(QK_SLOTS)]
        k6 = [sb(f"k6_{i}", [SCORE_ROWS, SEQ], BF16) for i in range(QK_SLOTS)]
        half_max = sb("half_max", [P, S1_BLOCKS])
        neg_max = sb("neg_max", [P, REP * TB])
        neg_max_bf = sb("neg_max_bf", [P, MAX_ROWS * REP * TB], BF16)
        max_rows = sb("max_rows", [MAX_ROWS * REP * TB, P], BF16)
        probs = sb("probs", [P, 2, REP, SEQ])
        o = sb("o", [P, 2, SEQ])
        on = sb("on", [P, SEQ])
        sums = sb("sums", [P, REP * SEQ // P])
        rec = sb("rec", [P, REP * SEQ // P])
        rec_rows = sb("rec_rows", [P, SEQ])
        ps_s1 = ps("ps_s1", [P, 2, BANK])
        ps_s2 = ps("ps_s2", [P, 2, SEQ])
        ps_o = ps("ps_o", [P, SEQ])
        block = ctx.enter_context(nc.Block())
        LOADS = len(Q_PARTS) * 2 * 16

        @block.sync
        def _(sp):
            def load_qk(g):
                slot = g % QK_SLOTS
                if g >= QK_SLOTS:
                    sp.wait_ge(S.s2, GROUP_SCORES * (g - QK_SLOTS + 1))
                m, r0 = g // 2, (g % 2) * REP * HD
                for i in range(len(Q_PARTS)):
                    rows = slice(i * HD, (i + 1) * HD)
                    src = A.q_dram[Q_PARTS[i], m, r0:r0 + REP * HD, :].rearrange("(j d) t -> d j t", j=REP)
                    sp.dma_start(q6[slot][rows], src).then_inc(S.qk_load[slot], 16)
                    sp.dma_start(k6[slot][rows], A.k_dram[K_PARTS[i], g * HD:(g + 1) * HD, :],
                                 ).then_inc(S.qk_load[slot], 16)

            def place_max(g):
                sp.wait_ge(S.mrow, g + 1)
                sp.dma_start(A.max_dram.rearrange("r (a t) -> (r a) t", t=P), max_rows[:]).then_inc(S.mrow_st, 16)
                sp.wait_ge(S.mrow_st, 16 * (g + 1))
                sp.dma_start(q6[g % QK_SLOTS][PART_ROWS:SCORE_ROWS].rearrange("r j t -> r (j t)"),
                             A.max_dram).then_inc(S.mrow_ld, 16)

            def spread_sums(g):
                sp.wait_ge(S.o, g + 1)
                sp.dma_start(A.sum_dram.rearrange("(j t) -> j t", j=REP), o[0:P:VW, g % 2, :]).then_inc(S.sum_st, 16)
                sp.wait_ge(S.sum_st, 16 * (g + 1))
                sp.dma_start(sums[:], A.sum_dram.rearrange("(p n) -> p n", p=P)).then_inc(S.sum_ld, 16)

            def place_reciprocals(g):
                sp.wait_ge(S.rec, g + 1)
                sp.dma_start(A.rec_dram.rearrange("(p n) -> p n", p=P), rec[:]).then_inc(S.rec_st, 16)
                sp.wait_ge(S.rec_st, 16 * (g + 1))
                if g >= 1:
                    sp.wait_ge(S.on, g)
                for j in range(REP):
                    sp.dma_start(rec_rows[j * VW:(j + 1) * VW, :],
                                 A.rec_dram[j * SEQ:(j + 1) * SEQ].partition_broadcast(VW)).then_inc(S.rec_ld, 16)

            def place_outputs(g):
                sp.wait_ge(S.on, g + 1)
                for j in range(REP):
                    row = (g % 2) * REP * HD + j * HD
                    sp.dma_start(M.attn_t[row:row + HD, g // 2, :],
                                 on[j * VW + 1:j * VW + 1 + HD, :]).then_inc(S.at, 16)

            load_qk(0)
            load_qk(1)
            place_max(0)
            for g in range(KV_HEADS):
                if g >= 1:
                    spread_sums(g - 1)
                if g + 2 < KV_HEADS:
                    load_qk(g + 2)
                if g >= 1:
                    place_reciprocals(g - 1)
                    place_outputs(g - 1)
                if g + 1 < KV_HEADS:
                    place_max(g + 1)
            spread_sums(KV_HEADS - 1)
            place_reciprocals(KV_HEADS - 1)
            place_outputs(KV_HEADS - 1)
            sp.wait_ge(S.at, 16 * REP * KV_HEADS)

        @block.gpsimd
        def _(pool):
            for slot in range(QK_SLOTS):
                pool.memset(k6[slot][PART_ROWS:SCORE_ROWS, :], 1.0).then_inc(S.ones, 1)
            for g in range(KV_HEADS):
                pool.wait_ge(S.rec_ld, 16 * REP * (g + 1))
                if g >= 1:
                    pool.wait_ge(S.at, 16 * REP * g)
                pool.tensor_tensor(on[:], o[:, g % 2, :], rec_rows[:], ALU.mult).then_inc(S.on, 1)

        @block.vector
        def _(dve):
            n = [0]

            def link(ins):
                n[0] += 1
                ins.then_inc(S.a_vec, 1)
                dve.wait_ge(S.a_vec, n[0])

            def maxima(g, blocks):
                for i in blocks:
                    dve.wait_ge(S.s1, g * S1_USES + i + 1)
                    last = dve.tensor_reduce(half_max[:, i:i + 1], ps_s1[:, (g * S1_USES + i) % 2, :], AX, ALU.max)
                    last.then_inc(S.s1_read, 1)

            def negate(g):
                dve.wait_ge(S.s1_read, (g + 1) * S1_BLOCKS)
                link(dve.tensor_reduce(neg_max[:], half_max[:].rearrange("p (a h) -> p a h", h=QH), AX,
                                       ALU.max, negate=True))
                if g >= 1:
                    dve.wait_ge(S.s1, g * S1_USES)
                link(dve.tensor_copy(neg_max_bf[:, 0:REP * TB], neg_max[:]))
                dve.tensor_tensor(neg_max_bf[:, REP * TB:], neg_max[:], neg_max_bf[:, 0:REP * TB],
                                  ALU.subtract).then_inc(S.negmax, 1)
                dve.wait_ge(S.s1, (g + 1) * S1_USES)
                if g >= 1:
                    dve.wait_ge(S.mrow_st, 16 * g)
                bank = ps_s1[:, ((g + 1) * S1_USES - 1) % 2, :].bitcast(BF16)
                dve.tensor_copy(max_rows[:], bank[0:MAX_ROWS * REP * TB, 0:P]).then_inc(S.mrow, 1)

            def reciprocals(g):
                dve.wait_ge(S.sum_ld, 16 * (g + 1))
                if g >= 1:
                    dve.wait_ge(S.rec_st, 16 * g)
                dve.reciprocal(rec[:], sums[:]).then_inc(S.rec, 1)

            maxima(0, range(S1_BLOCKS))
            negate(0)
            for g in range(KV_HEADS):
                if g + 1 < KV_HEADS:
                    maxima(g + 1, range(S1_BLOCKS // 2))
                if g >= 1:
                    reciprocals(g - 1)
                if g + 1 < KV_HEADS:
                    maxima(g + 1, range(S1_BLOCKS // 2, S1_BLOCKS))
                    negate(g + 1)
            reciprocals(KV_HEADS - 1)

        @block.scalar
        def _(act):
            def outputs(g):
                act.wait_ge(S.pv, TB * (g + 1))
                if g >= 2:
                    act.wait_ge(S.on, g - 1)
                act.activation(o[:, g % 2, :], ps_o[:], ACT.Copy).then_inc(S.o, 1)

            for g in range(KV_HEADS):
                for kt in range(TB):
                    tile = g * TB + kt
                    if tile >= 2:
                        act.wait_ge(S.pv, tile - 1)
                    for j in range(REP):
                        item = tile * REP + j
                        act.wait_ge(S.s2, item + 1)
                        act.activation(probs[:, tile % 2, j, :], ps_s2[:, item % 2, :], ACT.Exp).then_inc(S.exp, 1)
                        if g >= 1 and kt == 0 and j == 1:
                            outputs(g - 1)
            outputs(KV_HEADS - 1)

        @block.tensor
        def _(pe):
            def stage1(g, i):
                use = g * S1_USES + i
                if use >= 2:
                    last_g, last_i = divmod(use - 2, S1_USES)
                    if last_i == S1_BLOCKS:
                        pe.wait_ge(S.mrow, last_g + 1)
                    else:
                        pe.wait_ge(S.s1_read, last_g * S1_BLOCKS + last_i + 1)
                j, t, half = i // (TB * QH), i // QH % TB, i % QH
                pe.matmul(ps_s1[:, use % 2, :], q6[g % QK_SLOTS][0:PART_ROWS, j, t * P:(t + 1) * P],
                          k6[g % QK_SLOTS][0:PART_ROWS, half * BANK:(half + 1) * BANK],
                          start=True, stop=True).then_inc(S.s1, 1)

            def transpose_max(g):
                pe.wait_ge(S.negmax, g + 1)
                use = (g + 1) * S1_USES - 1
                pe.transpose(ps_s1[:, use % 2, :].bitcast(BF16)[0:MAX_ROWS * REP * TB, 0:P], neg_max_bf[:],
                             M.ident_bf[:]).then_inc(S.s1, 1)

            def stage2(g, kt, j):
                item = (g * TB + kt) * REP + j
                if item >= 2:
                    pe.wait_ge(S.exp, item - 1)
                for half in range(QH):
                    last = pe.matmul(ps_s2[:, item % 2, half * BANK:(half + 1) * BANK],
                                     k6[g % QK_SLOTS][:, kt * P:(kt + 1) * P],
                                     q6[g % QK_SLOTS][:, j, half * BANK:(half + 1) * BANK], start=True, stop=True)
                last.then_inc(S.s2, 1)

            def weigh(g, kt, half):
                if half == 0:
                    pe.wait_ge(S.exp, (g * TB + kt + 1) * REP)
                    if kt == 0 and g >= 1:
                        pe.wait_ge(S.o, g)
                for j in range(REP):
                    last = pe.matmul(ps_o[j * VW:(j + 1) * VW, half * BANK:(half + 1) * BANK], M.v[:, kt, g, :],
                                     probs[:, (g * TB + kt) % 2, j, half * BANK:(half + 1) * BANK],
                                     start=(kt == 0), stop=(kt == TB - 1), skip_group_check=True)
                if half == QH - 1:
                    last.then_inc(S.pv, 1)

            pe.wait_ge(S.qk_load[0], LOADS)
            for i in range(S1_BLOCKS):
                stage1(0, i)
            transpose_max(0)
            pe.wait_ge(S.ones, QK_SLOTS)
            for g in range(KV_HEADS):
                pe.wait_ge(S.mrow_ld, 16 * (g + 1))
                ahead = g + 1 < KV_HEADS
                if ahead:
                    pe.wait_ge(S.qk_load[(g + 1) % QK_SLOTS], LOADS * ((g + 1) // QK_SLOTS + 1))
                for x in range(GROUP_SCORES):
                    kt, j = x // REP, x % REP
                    stage2(g, kt, j)
                    if ahead:
                        for i in range(x * S1_BLOCKS // S1_SPREAD, min((x + 1) * S1_BLOCKS // S1_SPREAD, S1_BLOCKS)):
                            stage1(g + 1, i)
                        if x == S1_SPREAD + 2:
                            transpose_max(g + 1)
                    if kt >= 1 and j in (1, 3):
                        weigh(g, kt - 1, j // 2)
                for half in range(QH):
                    weigh(g, TB - 1, half)


def feed_forward(nc, S, M, A, b):
    with ExitStack() as ctx:
        def sb(name, shape, dt=F32):
            return ctx.enter_context(nc.sbuf_tensor(name, shape, dt))

        def ps(name, shape, dt=F32):
            return ctx.enter_context(nc.psum_tensor(name, shape, dt))

        HS, XS, US = 8, 3, 5
        h1 = sb("h1", [P, HS, D])
        x2 = sb("x2", [P, XS, D])
        xq = sb("xq", [P, 2, D], BF16)
        xq_t = sb("xq_t", [P, 2, D], BF16)
        u = sb("u", [P, US, INNER])
        yq = sb("yq", [P, 2, INNER], BF16)
        yq_t = sb("yq_t", [P, 2, INNER], BF16)
        fo = sb("fo", [P, 2, D])
        x_sq = sb("x_sq", [P, D], BF16)
        y_sq = sb("y_sq", [P, INNER], BF16)
        st = sb("f_st", [P, TB, 6])
        gst = sb("f_gst", [P, TB, UC * 6])
        C = Names()
        C.veps = sb("c_veps", [P, TB])
        C.r0 = sb("c_r0", [P, TB])
        C.ss = sb("c_ss", [P, TB])
        C.mx = sb("c_mx", [P, TB])
        C.ms = sb("c_ms", [P, TB])
        C.r1 = sb("c_r1", [P, TB])
        C.am = sb("c_am", [P, TB])
        C.rc = sb("c_rc", [P, TB])
        C.qs = sb("c_qs", [P, TB])
        C.a1 = sb("c_a1", [P, TB])
        C.gveps = sb("c_gveps", [P, TB])
        C.gr = sb("c_gr", [P, TB])
        C.nb = sb("c_nb", [P, TB])
        C.yss = sb("c_yss", [P, TB])
        C.ymx = sb("c_ymx", [P, TB])
        C.yms = sb("c_yms", [P, TB])
        C.yr = sb("c_yr", [P, TB])
        C.yam = sb("c_yam", [P, TB])
        C.yrc = sb("c_yrc", [P, TB])
        C.yqs = sb("c_yqs", [P, TB])
        C.a2 = sb("c_a2", [P, TB])
        mv = sb("f_mv", [P, TB, 2])
        gmv = sb("f_gmv", [P, TB, 2])
        ps_a = ps("ps_a", [P, BANK])
        ps_x = ps("ps_x", [P, 2 * BANK], BF16)
        ps_u = ps("ps_u", [P, 3, BANK])
        ps_y = ps("ps_y", [P, 2, 2 * BANK], BF16)
        ps_f = ps("ps_f", [P, BANK])
        block = ctx.enter_context(nc.Block())

        def col(c, t):
            return c[:, t:t + 1]

        def steps(*stages):
            for s in range(TB + max(lag for _, lag in stages)):
                for stage, lag in stages:
                    if 0 <= s - lag < TB:
                        stage(s - lag)

        @block.sync
        def _(sp):
            def load(t):
                sp.dma_start(h1[:, t % HS, :], A.h_dram[bass.ds(b * SEQ + t * P, P), :]).then_inc(S.f_h[t], 16)

            def store(t):
                sp.wait_ge(S.f_o, t + 1)
                sp.dma_start(A.out[bass.ds(b * SEQ + t * P, P), :], fo[:, t % 2, :]).then_inc(S.out_st[t % 4], 16)

            for t in range(TB):
                load(t)
            for t in range(TB):
                store(t)
            for i in range(4):
                sp.wait_ge(S.out_st[i], TB // 4 * 16)

        @block.gpsimd
        def _(pool):
            n = [0]

            def link(ins):
                n[0] += 1
                ins.then_inc(S.f_pool, 1)
                pool.wait_ge(S.f_pool, n[0])

            def rstd_h1(t):
                pool.wait_ge(S.f_var, t + 1)
                pool.tensor_tensor(col(C.r0, t), col(C.veps, t), M.neg_half[:], ALU.pow).then_inc(S.f_r0, 1)

            def rms_x2(t):
                pool.wait_ge(S.x2_ss, t + 1)
                link(pool.tensor_scalar(col(C.ms, t), col(C.ss, t), 1.0 / D, EPS, ALU.mult, ALU.add))
                pool.tensor_tensor(col(C.r1, t), col(C.ms, t), M.neg_half[:], ALU.pow).then_inc(S.x2_r, 1)

            def scale_g(t):
                pool.wait_ge(S.g_var, t + 1)
                link(pool.tensor_tensor(col(C.gr, t), col(C.gveps, t), M.neg_half[:], ALU.pow))
                link(pool.tensor_scalar(u[:, t % US, :], u[:, t % US, :], gmv[:, t, 0:1], col(C.gr, t),
                                        ALU.subtract, ALU.mult))
                pool.tensor_tensor(u[:, t % US, :], u[:, t % US, :], M.ln_g[:], ALU.mult).then_inc(S.g_scaled, 1)

            def rms_y(t):
                pool.wait_ge(S.y_ss, t + 1)
                link(pool.tensor_scalar(col(C.yms, t), col(C.yss, t), 1.0 / INNER, EPS, ALU.mult, ALU.add))
                pool.tensor_tensor(col(C.yr, t), col(C.yms, t), M.neg_half[:], ALU.pow).then_inc(S.y_r, 1)

            steps((rstd_h1, 0), (rms_x2, 1), (scale_g, 4), (rms_y, 5))

        @block.vector
        def _(dve):
            n = [0]

            def link(ins):
                n[0] += 1
                ins.then_inc(S.f_vec, 1)
                dve.wait_ge(S.f_vec, n[0])

            def residual(t):
                dve.wait_ge(S.f_h[t], 16)
                dve.wait_ge(S.wo, t + 1)
                dve.tensor_tensor(h1[:, t % HS, :], ps_a[:], h1[:, t % HS, :], ALU.add).then_inc(S.h1, 1)
                dve.wait_ge(S.h1, t + 1)
                link(dve.bn_stats(st[:, t, :], h1[:, t % HS, :]))
                link(dve.bn_aggr(mv[:, t, :], st[:, t, :]))
                dve.tensor_scalar(col(C.veps, t), mv[:, t, 1:2], EPS, None, ALU.add).then_inc(S.f_var, 1)

            def norm_x2(t):
                dve.wait_ge(S.f_r0, t + 1)
                if t >= XS:
                    dve.wait_ge(S.x2_ss, t - XS + 1)
                dve.tensor_scalar(x2[:, t % XS, :], h1[:, t % HS, :], mv[:, t, 0:1], col(C.r0, t),
                                  ALU.subtract, ALU.mult).then_inc(S.x2, 1)
                dve.wait_ge(S.x2, t + 1)
                link(dve.tensor_reduce(col(C.mx, t), x2[:, t % XS, :], AX, ALU.max, apply_absolute_value=True))
                link(dve.tensor_tensor(h1[:, t % HS, :], h1[:, t % HS, :], M.b2[:], ALU.add))

            def scales(am, rc, qs, a, mx, r, w, t):
                link(dve.tensor_scalar(col(am, t), col(mx, t), col(r, t), 1e-5, ALU.mult, ALU.max))
                link(dve.reciprocal(col(rc, t), col(am, t)))
                link(dve.tensor_scalar(col(a, t), col(am, t), M.w_dq[:, w:w + 1], None, ALU.mult))
                return dve.tensor_scalar(col(qs, t), col(rc, t), 127.0, col(r, t), ALU.mult, ALU.mult)

            def quantise_x2(t):
                dve.wait_ge(S.x2_r, t + 1)
                link(scales(C.am, C.rc, C.qs, C.a1, C.mx, C.r1, 0, t))
                link(dve.tensor_scalar(x2[:, t % XS, :], x2[:, t % XS, :], col(C.qs, t), ROUND, ALU.mult, ALU.add))
                if t >= 2:
                    dve.wait_ge(S.xq_tr, t - 1)
                dve.tensor_scalar(xq[:, t % 2, :], x2[:, t % XS, :], ROUND, 127.0, ALU.subtract,
                                  ALU.min).then_inc(S.xq, 1)

            def dequantise_u(t):
                for c in range(UC):
                    dve.wait_ge(S.u_ps, t * UC + c + 1)
                    if t >= US and c == 0:
                        dve.wait_ge(S.yq, t - US + 1)
                    cs = slice(c * BANK, (c + 1) * BANK)
                    dve.scalar_tensor_tensor(out=u[:, t % US, cs], in0=ps_u[:, (t * UC + c) % 3, :],
                                             scalar=col(C.a1, t), in1=M.b1[:, cs], op0=ALU.mult,
                                             op1=ALU.add).then_inc(S.u, 1)

            def stats_g(t):
                dve.wait_ge(S.gelu, t + 1)
                for c in range(UC):
                    last = dve.bn_stats(gst[:, t, 6 * c:6 * c + 6], u[:, t % US, c * BANK:(c + 1) * BANK])
                link(last)
                link(dve.bn_aggr(gmv[:, t, :], gst[:, t, :]))
                dve.tensor_scalar(col(C.gveps, t), gmv[:, t, 1:2], EPS, None, ALU.add).then_inc(S.g_var, 1)

            def shift_y(t):
                dve.wait_ge(S.g_scaled, t + 1)
                dve.tensor_tensor(u[:, t % US, :], u[:, t % US, :], M.ln_b[:], ALU.add).then_inc(S.y, 1)
                dve.wait_ge(S.y, t + 1)
                link(dve.tensor_reduce(col(C.ymx, t), u[:, t % US, :], AX, ALU.max, apply_absolute_value=True))

            def scale_y(t):
                dve.wait_ge(S.y_r, t + 1)
                scales(C.yam, C.yrc, C.yqs, C.a2, C.ymx, C.yr, 1, t).then_inc(S.y_qs, 1)

            def quantise_y(t):
                dve.wait_ge(S.y_shift, t + 1)
                if t >= 2:
                    dve.wait_ge(S.yq_tr, 2 * (t - 1))
                dve.tensor_scalar(yq[:, t % 2, :], u[:, t % US, :], ROUND, 127.0, ALU.subtract,
                                  ALU.min).then_inc(S.yq, 1)

            def finish(t):
                dve.wait_ge(S.o_ps, t + 1)
                if t >= 2:
                    dve.wait_ge(S.out_st[(t - 2) % 4], 16 * ((t - 2) // 4 + 1))
                dve.scalar_tensor_tensor(out=fo[:, t % 2, :], in0=ps_f[:], scalar=col(C.a2, t),
                                         in1=h1[:, t % HS, :], op0=ALU.mult, op1=ALU.add).then_inc(S.f_o, 1)

            steps((residual, 0), (norm_x2, 1), (quantise_x2, 2), (dequantise_u, 2), (stats_g, 3),
                  (scale_y, 5), (shift_y, 4), (quantise_y, 5), (finish, 6))

        @block.scalar
        def _(act):
            def square_x2(t):
                act.wait_ge(S.x2, t + 1)
                if t >= 1:
                    act.wait_ge(S.x2_ss, t)
                act.activation(x_sq[:], x2[:, t % XS, :], ACT.Square,
                               accum_out=col(C.ss, t)).then_inc(S.x2_ss, 1)

            def copy_xq_t(t):
                act.wait_ge(S.xq_tr, t + 1)
                if t >= 2:
                    act.wait_ge(S.u_ps, UC * (t - 1))
                act.activation(xq_t[:, t % 2, :], ps_x[:, 0:D], ACT.Copy).then_inc(S.xq_t, 1)

            def silu_gelu(t):
                act.wait_ge(S.u, UC * (t + 1))
                act.activation(u[:, t % US, :], u[:, t % US, :], ACT.Silu).then_inc(S.silu, 1)
                act.wait_ge(S.silu, t + 1)
                act.activation(u[:, t % US, :], u[:, t % US, :], ACT.Gelu).then_inc(S.gelu, 1)

            def square_y(t):
                act.wait_ge(S.y, t + 1)
                if t >= 1:
                    act.wait_ge(S.y_ss, t)
                act.activation(y_sq[:], u[:, t % US, :], ACT.Square, accum_out=col(C.yss, t)).then_inc(S.y_ss, 1)

            def round_y(t):
                act.wait_ge(S.y_qs, t + 1)
                act.activation(u[:, t % US, :], u[:, t % US, :], ACT.Identity, bias=M.round_c[:],
                               scale=col(C.yqs, t)).then_inc(S.y_shift, 1)

            def copy_yq_t(t):
                for half in range(2):
                    act.wait_ge(S.yq_tr, 2 * t + half + 1)
                    if t >= 2 and half == 0:
                        act.wait_ge(S.o_ps, t - 1)
                    act.activation(yq_t[:, t % 2, half * 2 * BANK:(half + 1) * 2 * BANK], ps_y[:, half, :],
                                   ACT.Copy).then_inc(S.yq_t, 1)

            steps((square_x2, 1), (copy_xq_t, 2), (silu_gelu, 2), (square_y, 4), (round_y, 5), (copy_yq_t, 5))

        @block.tensor
        def _(pe):
            def project_out(t):
                if t >= 1:
                    pe.wait_ge(S.h1, t)
                for c in range(HC):
                    last = pe.matmul(ps_a[:], M.attn_t[:, c, t * P:(t + 1) * P], M.wo[:, c, :],
                                     start=(c == 0), stop=(c == HC - 1))
                last.then_inc(S.wo, 1)

            def transpose_xq(t):
                pe.wait_ge(S.xq, t + 1)
                if t >= 1:
                    pe.wait_ge(S.xq_t, t)
                for c in range(DC):
                    last = pe.transpose(ps_x[:, c * P:(c + 1) * P], xq[:, t % 2, c * P:(c + 1) * P], M.ident_bf[:])
                last.then_inc(S.xq_tr, 1)

            def product_1(t):
                pe.wait_ge(S.xq_t, t + 1)
                for n in range(UC):
                    use = t * UC + n
                    if use >= 3:
                        pe.wait_ge(S.u, use - 2)
                    for c in range(DC):
                        last = pe.matmul(ps_u[:, use % 3, :], xq_t[:, t % 2, c * P:(c + 1) * P],
                                         M.w1q[:, c, n * BANK:(n + 1) * BANK], start=(c == 0), stop=(c == DC - 1))
                    last.then_inc(S.u_ps, 1)

            def transpose_yq(t):
                pe.wait_ge(S.yq, t + 1)
                for half in range(2):
                    if t >= 1:
                        pe.wait_ge(S.yq_t, 2 * (t - 1) + half + 1)
                    for c in range(IC // 2):
                        ic = half * IC // 2 + c
                        last = pe.transpose(ps_y[:, half, c * P:(c + 1) * P], yq[:, t % 2, ic * P:(ic + 1) * P],
                                            M.ident_bf[:])
                    last.then_inc(S.yq_tr, 1)

            def product_2(t):
                if t >= 1:
                    pe.wait_ge(S.f_o, t)
                for c in range(IC):
                    if c % (IC // 2) == 0:
                        pe.wait_ge(S.yq_t, 2 * t + c // (IC // 2) + 1)
                    last = pe.matmul(ps_f[:], yq_t[:, t % 2, c * P:(c + 1) * P], M.w2q[:, c, :],
                                     start=(c == 0), stop=(c == IC - 1))
                last.then_inc(S.o_ps, 1)

            steps((project_out, 0), (transpose_xq, 2), (product_1, 2), (transpose_yq, 5), (product_2, 5))


def lm_tower(nc, x_row, x_col, W, delta_t, tokens, wq, wk, wv, wo, w1t, b1, ln_g, ln_b, w2t, b2, out):
    with ExitStack() as ctx:
        setup, batch, batch_range = semaphores(nc, ctx)

        def sb(name, shape, dt=F32):
            return ctx.enter_context(nc.sbuf_tensor(name, shape, dt))

        def dram(name, shape, dt=F32):
            return nc.dram_tensor(name, shape, dt, kind="Internal").ap()

        A = Names()
        A.x_row = x_row
        A.x_col = x_col
        A.W = W
        A.delta_t = delta_t
        A.tokens = tokens
        A.wq = wq
        A.wk = wk
        A.wv = wv
        A.wo = wo
        A.w1t = w1t
        A.b1 = b1
        A.ln_g = ln_g
        A.ln_b = ln_b
        A.w2t = w2t
        A.b2 = b2
        A.out = out
        A.h_dram = dram("h_dram", [TOKENS, D])
        A.q_dram = dram("q_dram", [3, HC, P, SEQ], BF16)
        A.k_dram = dram("k_dram", [3, P, SEQ], BF16)
        A.max_dram = dram("max_dram", [MAX_ROWS, REP * SEQ], BF16)
        A.sum_dram = dram("sum_dram", [REP * SEQ])
        A.rec_dram = dram("rec_dram", [REP * SEQ])
        M = Names()
        M.ident = sb("ident", [P, P])
        M.ident_bf = sb("ident_bf", [P, P], BF16)
        M.neg_half = sb("neg_half", [P, 1])
        M.round_c = sb("round_c", [P, 1])
        M.idx_all = sb("idx_all", [P, NT], U32)
        M.idx_b = sb("idx_b", [P, TB], U32)
        M.tok = sb("tok", [P, 1])
        M.d_hm = sb("d_hm", [P, D], BF16)
        M.d_lo = sb("d_lo", [P, D], BF16)
        M.wq = sb("wq_sb", [P, DC, HEADS * HD])
        M.wk = sb("wk_sb", [P, DC, KV_HEADS * HD])
        M.wv = sb("wv_sb", [P, DC, KV_HEADS * HD])
        M.wo = sb("wo_sb", [P, HC, D])
        M.b1 = sb("b1_sb", [P, INNER])
        M.ln_g = sb("ln_g_sb", [P, INNER])
        M.ln_b = sb("ln_b_sb", [P, INNER])
        M.b2 = sb("b2_sb", [P, D])
        M.w1q = sb("w1q", [P, DC, INNER], BF16)
        M.w2q = sb("w2q", [P, IC, D], BF16)
        M.w_mean = sb("w_mean", [P, 2])
        M.w_dq = sb("w_dq", [P, 2])
        M.v = sb("v", [P, TB, KV_HEADS, VW])
        M.attn_t = sb("attn_t", [P, HC, SEQ])

        set_up(nc, setup, M, A)
        with nc.Fori(0, BATCH) as b:
            project(nc, batch, M, A, b)
            attend(nc, batch, M, A, b)
            feed_forward(nc, batch, M, A, b)
            nc.all_engine_barrier(sems_to_clear=batch_range)


def kernel(**inputs):
    import numpy as _np
    import concourse.bacc as _bacc
    from concourse import mybir as _mybir
    from concourse.bass_utils import run_bass_kernel_spmd as _run

    a = {k: _np.asarray(v) for k, v in inputs.items()}
    x = a["x"]
    n_train, dim = a["L0_tok_token_indices"].shape[0], a["L0_tok_W"].shape[1]
    laid_out = {
        "x_row": x.reshape(-1),
        "x_col": x.reshape(-1, 128).T,
        "W": a["L0_tok_W"],
        "delta_t": a["L0_tok_delta_values"].reshape(dim, n_train).T,
        "tokens": a["L0_tok_token_indices"].reshape(n_train, 1),
        "wq": a["L0_attn_Wq"], "wk": a["L0_attn_Wk"], "wv": a["L0_attn_Wv"], "wo": a["L0_attn_Wo"],
        "w1t": a["L0_ffn_w1"].T, "b1": a["L0_ffn_b1"], "ln_g": a["L0_ffn_ln_g"], "ln_b": a["L0_ffn_ln_b"],
        "w2t": a["L0_ffn_w2"].T, "b2": a["L0_ffn_b2"],
    }
    nc = _bacc.Bacc("TRN2", target_bir_lowering=False, num_devices=1)
    arrays, args = {}, []
    for name, v in laid_out.items():
        v = _np.ascontiguousarray(v)
        arrays[f"in_{name}"] = v
        args.append(nc.dram_tensor(f"in_{name}", v.shape, _mybir.dt.from_np(v.dtype), kind="ExternalInput").ap())
    out = nc.dram_tensor("out_0", (x.size, dim), _mybir.dt.from_np(_np.dtype("float32")), kind="ExternalOutput").ap()
    lm_tower(nc, *args, out)
    r = _run(nc, [arrays], core_ids=[0])
    return r.results[0]["out_0"].reshape(*x.shape, dim)
```

```python
from contextlib import ExitStack

import concourse.bass as bass
from concourse import mybir

F32 = mybir.dt.float32
BF16 = mybir.dt.bfloat16
I32 = mybir.dt.int32
U32 = mybir.dt.uint32
ALU = mybir.AluOpType
ACT = mybir.ActivationFunctionType
AX = mybir.AxisListType.X

P = 128
BATCH, SEQ = 4, 1024
TOKENS = BATCH * SEQ
VOCAB, D = 32000, 512
N_TRAIN = 64
HEADS, KV_HEADS, HD = 32, 8, 16
REP = HEADS // KV_HEADS
INNER = 2048
EPS = 1e-5
ROUND = 1.5 * 2.0 ** 23

DC = D // P
TB = SEQ // P
NT = TOKENS // P
IC = INNER // P
HC = HEADS * HD // P
BANK = 512
QH = SEQ // BANK
UC = INNER // BANK

Q_PARTS = (0, 0, 0, 1, 1, 2)
K_PARTS = (0, 1, 2, 0, 1, 0)
PART_ROWS = len(Q_PARTS) * HD
MAX_ROWS = 2
SCORE_ROWS = PART_ROWS + MAX_ROWS
VW = 32
QK_SLOTS = 3
K_RUNS = ((0, 3), (3, 2), (5, 1))
QK_LOADS = (len(Q_PARTS) + len(K_RUNS)) * 16

SEG_ITEMS = TB * REP // 2
GROUP_ITEMS = QH * SEG_ITEMS
ITEMS = KV_HEADS * GROUP_ITEMS
S1_BLOCKS = REP * TB * QH
S1_LEAD = 6


def plan_stage1(share):
    last = (KV_HEADS - 1) * GROUP_ITEMS - S1_LEAD
    rate = S1_BLOCKS * (KV_HEADS - 1) / (sum(share(x) for x in range(last)) or 1)
    done, total = [], 0.0
    for x in range(last):
        total += rate * share(x)
        done.append(total)
    ahead = max(S1_BLOCKS * g - done[g * GROUP_ITEMS - S1_LEAD - 1] for g in range(1, KV_HEADS))
    order, at, used = [], {}, 0
    pending = []
    for x in range(-1, last + 3):
        until = S1_BLOCKS * KV_HEADS if x >= last else int(S1_BLOCKS + ahead + (done[x] if x >= 0 else 0) + 0.999)
        events = [("max", g, S1_BLOCKS) for due, g in pending if due <= x]
        pending = [(due, g) for due, g in pending if due > x]
        for block in range(used, min(until, S1_BLOCKS * KV_HEADS)):
            g, i = divmod(block, S1_BLOCKS)
            events.append(("block", g, i))
            if i == S1_BLOCKS - 1 and g == 0:
                events.append(("max", 0, S1_BLOCKS))
            elif i == S1_BLOCKS - 1:
                pending.append((x + 2, g))
            used = block + 1
        for event in events:
            blocks = used_blocks(order) + (event[0] == "block")
            at.setdefault(x, []).append((len(order),) + event)
            order.append(event + (blocks,))
    return order, at


def used_blocks(order):
    return order[-1][3] if order else 0


class Names:
    pass


def semaphores(nc, stack):
    def sem(name):
        return stack.enter_context(nc.semaphore(name))

    setup = Names()
    setup.small = sem("small_loaded")
    setup.proj_w = sem("proj_weights_loaded")
    setup.ffn_w = [sem("w1_staged"), sem("w2_staged")]
    setup.const = sem("constants_set")
    setup.vec = sem("setup_vector_chain")
    setup.abs_sum = sem("abs_sum_ready")
    setup.abs_tot = sem("abs_total_ready")
    setup.w1_read = sem("w1_stage_read")
    gather = [sem(f"gathered{t}") for t in range(TB)]
    first = sem("batch_first")
    batch = Names()
    batch.gather = gather
    batch.x_row = sem("x_row_loaded")
    batch.idx = sem("indices_copied")
    batch.hot = sem("one_hot_ready")
    batch.delta = sem("delta_in_psum")
    batch.h0 = sem("h0_ready")
    batch.h0_stored = sem("h0_stored")
    batch.p_vec = sem("project_vector_chain")
    batch.p_var = sem("variance_ready")
    batch.p_rstd = sem("rstd_ready")
    batch.p_norm = sem("normalised_ready")
    batch.x_tr = sem("x_transposes_in_psum")
    batch.x_t = sem("x_t_ready")
    batch.v_ps = sem("v_in_psum")
    batch.v_sb = sem("v_ready")
    batch.v_const = sem("v_ones_set")
    batch.qk_ps = sem("qk_in_psum")
    batch.qk_hi = sem("qk_high_ready")
    batch.qk_r1 = sem("qk_remainder_ready")
    batch.qk_mid = sem("qk_middle_ready")
    batch.qk_lo = sem("qk_low_ready")
    batch.part_st = [sem(f"qk_parts_stored{i}") for i in range(2)]
    batch.qk_load = [sem(f"qk_parts_loaded{i}") for i in range(QK_SLOTS)]
    batch.ones = sem("score_ones_set")
    batch.s1 = sem("stage1_in_psum")
    batch.s1_read = sem("stage1_read")
    batch.a_vec = sem("attend_vector_chain")
    batch.negmax = sem("negmax_ready")
    batch.mrow = sem("max_rows_ready")
    batch.mrow_st = sem("max_rows_stored")
    batch.mrow_ld = sem("max_rows_loaded")
    batch.s2 = sem("stage2_in_psum")
    batch.exp = sem("exp_ready")
    batch.pv = sem("pv_done")
    batch.o = sem("outputs_ready")
    batch.sum_st = sem("sums_stored")
    batch.sum_ld = sem("sums_loaded")
    batch.rec = sem("reciprocals_ready")
    batch.rec_st = sem("reciprocals_stored")
    batch.rec_ld = sem("reciprocals_loaded")
    batch.on = sem("outputs_normalised")
    batch.at = sem("attn_t_landed")
    batch.f_h = [sem(f"h0_loaded{t}") for t in range(TB)]
    batch.wo = sem("wo_in_psum")
    batch.h1 = sem("h1_ready")
    batch.h1_b2 = sem("h1_plus_b2_ready")
    batch.f_vec = sem("ffn_vector_chain")
    batch.f_pool = sem("ffn_pool_chain")
    batch.g_stats = sem("g_stats_ready")
    batch.y_max = sem("y_absmax_ready")
    batch.f_var = sem("h1_variance_ready")
    batch.f_r0 = sem("h1_rstd_ready")
    batch.x2 = sem("x2_ready")
    batch.x2_ss = sem("x2_squares_ready")
    batch.x2_r = sem("x2_rms_ready")
    batch.xq = sem("xq_ready")
    batch.xq_tr = sem("xq_transposes_in_psum")
    batch.xq_t = sem("xq_t_ready")
    batch.u_ps = sem("u_in_psum")
    batch.u = sem("u_ready")
    batch.tanh = sem("tanh_ready")
    batch.silu = sem("silu_ready")
    batch.gelu = sem("gelu_ready")
    batch.g_var = sem("g_variance_ready")
    batch.y = sem("y_ready")
    batch.y_ss = sem("y_squares_ready")
    batch.y_r = sem("y_rms_ready")
    batch.y_qs = sem("y_scale_ready")
    batch.y_shift = sem("y_shifted_ready")
    batch.yq = sem("yq_ready")
    batch.yq_tr = sem("yq_transposes_in_psum")
    batch.yq_t = sem("yq_t_ready")
    batch.o_ps = sem("ffn_out_in_psum")
    batch.f_o = sem("ffn_out_ready")
    batch.out_st = [sem(f"out_stored{i}") for i in range(4)]
    last = sem("batch_last")
    return setup, batch, range(first.num, last.num + 1)


def rows_of(weights):
    return weights.rearrange("(c p) n -> p c n", p=P)


def set_up(nc, S, M, A):
    with ExitStack() as ctx:
        def sb(name, shape, dt=F32):
            return ctx.enter_context(nc.sbuf_tensor(name, shape, dt))

        xc_i = sb("xc_i", [P, NT], I32)
        xc_f = sb("xc_f", [P, NT])
        xc_n = sb("xc_n", [P, NT])
        t_i = sb("t_i", [P, 1], I32)
        t_n = sb("t_n", [P, 1])
        dl = sb("dl", [P, D])
        dl_bf = sb("dl_bf", [P, D], BF16)
        dl_r1 = sb("dl_r1", [P, D])
        dl_r2 = sb("dl_r2", [P, D])
        stage = sb("stage", [P, DC * INNER])
        abs_part = sb("abs_part", [P, 16])
        abs_sum = sb("abs_sum", [P, 2])
        abs_tot = sb("abs_tot", [P, 2])
        w_scale = sb("w_scale", [P, 2])
        block = ctx.enter_context(nc.Block())

        @block.sync
        def _(sp):
            sp.dma_start(rows_of_stage(stage, DC), rows_of(A.w1t)).then_inc(S.ffn_w[0], 16)
            sp.dma_start(xc_i[:], A.x_col).then_inc(S.small, 16)
            for half in range(2):
                rows = slice(half * N_TRAIN, (half + 1) * N_TRAIN)
                sp.dma_start(t_i[rows, :], A.tokens).then_inc(S.small, 16)
                sp.dma_start(dl[rows, :], A.delta_t).then_inc(S.small, 16)
            for dst, src in ((M.wq, A.wq), (M.wk, A.wk), (M.wv, A.wv), (M.wo, A.wo)):
                sp.dma_start(dst[:], rows_of(src)).then_inc(S.proj_w, 16)
            for dst, src in ((M.b1, A.b1), (M.ln_g, A.ln_g), (M.ln_b, A.ln_b), (M.b2, A.b2)):
                sp.dma_start(dst[:], src.partition_broadcast(P)).then_inc(S.proj_w, 16)
            sp.wait_ge(S.w1_read, 1)
            sp.dma_start(rows_of_stage(stage, IC), rows_of(A.w2t)).then_inc(S.ffn_w[1], 16)
            sp.wait_ge(S.proj_w, 8 * 16)

        @block.gpsimd
        def _(pool):
            pool.memset(M.ident[:], 0.0).then_inc(S.const, 1)
            pool.memset(M.neg_half[:], -0.5).then_inc(S.const, 1)
            pool.memset(M.round_c[:], ROUND).then_inc(S.const, 1)
            pool.wait_ge(S.const, 3)
            pool.affine_select(out=M.ident[:], in_=M.ident[:], compare_op=ALU.not_equal, fill=1.0, base=0,
                               pattern=[[-1, P]], channel_multiplier=1).then_inc(S.const, 1)
            for w in range(2):
                pool.wait_ge(S.abs_sum, w + 1)
                pool.partition_all_reduce(abs_tot[:, w:w + 1], abs_sum[:, w:w + 1], P,
                                          bass.bass_isa.ReduceOp.add).then_inc(S.abs_tot, 1)

        @block.vector
        def _(dve):
            n = [0]

            def link(ins):
                n[0] += 1
                ins.then_inc(S.vec, 1)
                dve.wait_ge(S.vec, n[0])

            dve.wait_ge(S.const, 4)
            link(dve.tensor_copy(M.ident_bf[:], M.ident[:]))
            dve.wait_ge(S.small, 5 * 16)

            link(dve.tensor_copy(xc_f[:], xc_i[:]))
            link(dve.tensor_scalar(xc_n[:], xc_f[:], 0.0, float(VOCAB), ALU.is_lt, ALU.mult))
            link(dve.tensor_tensor(xc_f[:], xc_f[:], xc_n[:], ALU.add))
            link(dve.tensor_scalar(xc_f[:], xc_f[:], 0.0, float(VOCAB - 1), ALU.max, ALU.min))
            link(dve.tensor_copy(M.idx_all[:], xc_f[:]))
            link(dve.tensor_copy(M.tok[:], t_i[:]))
            link(dve.tensor_scalar(t_n[:], M.tok[:], 0.0, float(VOCAB), ALU.is_lt, ALU.mult))
            link(dve.tensor_tensor(M.tok[:], M.tok[:], t_n[:], ALU.add))
            lower, upper = slice(0, N_TRAIN), slice(N_TRAIN, P)
            link(dve.tensor_copy(dl_bf[:], dl[:]))
            link(dve.tensor_tensor(dl_r1[:], dl[:], dl_bf[:], ALU.subtract))
            link(dve.tensor_copy(M.d_hm[lower, :], dl_bf[lower, :]))
            link(dve.tensor_copy(M.d_hm[upper, :], dl_r1[upper, :]))
            link(dve.tensor_copy(dl_bf[:], dl_r1[:]))
            link(dve.tensor_tensor(dl_r2[:], dl_r1[:], dl_bf[:], ALU.subtract))
            link(dve.memset(M.d_lo[:], 0.0))
            link(dve.tensor_copy(M.d_lo[lower, :], dl_r2[lower, :]))

            for w, dst in enumerate((M.w1q, M.w2q)):
                dve.wait_ge(S.ffn_w[w], 16)
                link(dve.tensor_reduce(abs_part[:], stage[:].rearrange("p (c n) -> p c n", c=16), AX,
                                       ALU.add, apply_absolute_value=True))
                dve.tensor_reduce(abs_sum[:, w:w + 1], abs_part[:], AX, ALU.add).then_inc(S.abs_sum, 1)
                dve.wait_ge(S.abs_tot, w + 1)
                link(dve.tensor_scalar(M.w_mean[:, w:w + 1], abs_tot[:, w:w + 1], 1.0 / (D * INNER), 1e-5,
                                       ALU.mult, ALU.max))
                link(dve.reciprocal(w_scale[:, w:w + 1], M.w_mean[:, w:w + 1]))
                link(dve.tensor_scalar(M.w_dq[:, w:w + 1], M.w_mean[:, w:w + 1], 1.0 / 127.0, None, ALU.mult))
                link(dve.tensor_scalar(stage[:], stage[:], w_scale[:, w:w + 1], 1.0, ALU.mult, ALU.min))
                link(dve.tensor_scalar(stage[:], stage[:], -1.0, ROUND, ALU.max, ALU.add))
                last = dve.tensor_scalar(dst[:].rearrange("p c n -> p (c n)"), stage[:], ROUND, None,
                                         ALU.subtract)
                last.then_inc(S.w1_read, 1)


def rows_of_stage(stage, chunks):
    return stage[:].rearrange("p (c n) -> p c n", c=chunks)


def attention_memory(nc, ctx, S1, tag):
    T = Names()
    T.q6 = [ctx.enter_context(nc.sbuf_tensor(f"q6_{i}" + tag, [SCORE_ROWS, REP, SEQ], BF16)) for i in range(QK_SLOTS)]
    T.k6 = [ctx.enter_context(nc.sbuf_tensor(f"k6_{i}" + tag, [SCORE_ROWS, SEQ], BF16)) for i in range(QK_SLOTS)]
    T.half_max = ctx.enter_context(nc.sbuf_tensor("half_max" + tag, [P, 2, S1_BLOCKS], F32))
    T.neg_max = ctx.enter_context(nc.sbuf_tensor("neg_max" + tag, [P, REP * TB], F32))
    T.neg_max_bf = ctx.enter_context(nc.sbuf_tensor("neg_max_bf" + tag, [P, MAX_ROWS * REP * TB], BF16))
    T.max_rows = ctx.enter_context(nc.sbuf_tensor("max_rows" + tag, [MAX_ROWS * REP * TB, P], BF16))
    T.ps_s1 = ctx.enter_context(nc.psum_tensor("ps_s1" + tag, [P, 2, BANK], F32))
    T.order, T.at = S1
    return T


def stage1_sync(sp, S, A, T):
    steps = Names()

    def load_qk(g):
        slot = g % QK_SLOTS
        if g >= QK_SLOTS:
            sp.wait_ge(S.s2, GROUP_ITEMS * (g - QK_SLOTS + 1))
        m, r0 = g // 2, (g % 2) * REP * HD
        for first, count in K_RUNS:
            rows = slice(first * HD, (first + count) * HD)
            sp.dma_start(T.k6[slot][rows], A.k_dram[0:count, g * HD:(g + 1) * HD, :]).then_inc(S.qk_load[slot], 16)
        for i, part in enumerate(Q_PARTS):
            src = A.q_dram[part, m, r0:r0 + REP * HD, :].rearrange("(j d) t -> d j t", j=REP)
            sp.dma_start(T.q6[slot][i * HD:(i + 1) * HD], src).then_inc(S.qk_load[slot], 16)

    def place_max(g):
        sp.wait_ge(S.mrow, g + 1)
        sp.dma_start(A.max_dram.rearrange("r (a t) -> (r a) t", t=P), T.max_rows[:]).then_inc(S.mrow_st, 16)
        sp.wait_ge(S.mrow_st, 16 * (g + 1))
        sp.dma_start(T.q6[g % QK_SLOTS][PART_ROWS:SCORE_ROWS].rearrange("r j t -> r (j t)"),
                     A.max_dram).then_inc(S.mrow_ld, 16)

    steps.load_qk, steps.place_max = load_qk, place_max
    return steps


def stage1_vector(dve, S, T, link):
    def stage1_max(use, g, i):
        dve.wait_ge(S.s1, use + 1)
        dve.tensor_reduce(T.half_max[:, g % 2, i:i + 1], T.ps_s1[:, use % 2, :], AX, ALU.max).then_inc(S.s1_read, 1)

    def negate(g):
        dve.wait_ge(S.s1_read, (g + 1) * S1_BLOCKS)
        link(dve.tensor_reduce(T.neg_max[:], T.half_max[:, g % 2, :].rearrange("p (a h) -> p a h", h=QH), AX,
                               ALU.max, negate=True))
        link(dve.tensor_copy(T.neg_max_bf[:, 0:REP * TB], T.neg_max[:]))
        dve.tensor_tensor(T.neg_max_bf[:, REP * TB:], T.neg_max[:], T.neg_max_bf[:, 0:REP * TB],
                          ALU.subtract).then_inc(S.negmax, 1)

    def copy_max_rows(use, g):
        dve.wait_ge(S.s1, use + 1)
        if g >= 1:
            dve.wait_ge(S.mrow_st, 16 * g)
        dve.tensor_copy(T.max_rows[:], T.ps_s1[:, use % 2, :].bitcast(BF16)[0:MAX_ROWS * REP * TB, 0:P],
                        ).then_inc(S.mrow, 1)

    def run(use, kind, g, i):
        if kind == "max":
            copy_max_rows(use, g)
            return
        stage1_max(use, g, i)
        if i == S1_BLOCKS - 1:
            negate(g)

    return run


def stage1_tensor(pe, S, M, T):
    def run(use, kind, g, i):
        if use >= 2:
            last_kind, last_g, _, blocks = T.order[use - 2]
            if last_kind == "max":
                pe.wait_ge(S.mrow, last_g + 1)
            else:
                pe.wait_ge(S.s1_read, blocks)
        bank, slot = T.ps_s1[:, use % 2, :], g % QK_SLOTS
        if kind == "max":
            pe.wait_ge(S.negmax, g + 1)
            pe.transpose(bank.bitcast(BF16)[0:MAX_ROWS * REP * TB, 0:P], T.neg_max_bf[:],
                         M.ident_bf[:]).then_inc(S.s1, 1)
            return
        if i == 0:
            pe.wait_ge(S.qk_load[slot], QK_LOADS * (g // QK_SLOTS + 1))
        j, t, half = i // (TB * QH), i // QH % TB, i % QH
        pe.matmul(bank, T.q6[slot][0:PART_ROWS, j, t * P:(t + 1) * P],
                  T.k6[slot][0:PART_ROWS, half * BANK:(half + 1) * BANK], start=True, stop=True).then_inc(S.s1, 1)

    return run


def output_sync(sp, S, A, M, first_token, earlier):
    steps = Names()

    def spread_sums(g):
        n = g + earlier
        sp.dma_start(A.sum_dram.rearrange("(j t) -> j t", j=REP), M.o[0:P:VW, g % 2, :]).then_inc(S.sum_st, 16)
        sp.wait_ge(S.sum_st, 16 * (n + 1))
        sp.dma_start(M.sums[:], A.sum_dram.rearrange("(p n) -> p n", p=P)).then_inc(S.sum_ld, 16)

    def place_reciprocals(g):
        n = g + earlier
        sp.wait_ge(S.rec, n + 1)
        sp.dma_start(A.rec_dram.rearrange("(p n) -> p n", p=P), M.rec[:]).then_inc(S.rec_st, 16)
        sp.wait_ge(S.rec_st, 16 * (n + 1))
        if n >= 1:
            sp.wait_ge(S.on, n)
        for j in range(REP):
            sp.dma_start(M.rec_rows[j * VW:(j + 1) * VW, :],
                         A.rec_dram[j * SEQ:(j + 1) * SEQ].partition_broadcast(VW)).then_inc(S.rec_ld, 16)

    def place_outputs(g):
        sp.wait_ge(S.on, g + earlier + 1)
        for j in range(REP):
            row = (g * REP + j) * HD
            sp.dma_start(A.attn_dram[row:row + HD, bass.ds(first_token, SEQ)],
                         M.on[j * VW + 1:j * VW + 1 + HD, :]).then_inc(S.at, 16)

    steps.spread_sums, steps.place_reciprocals, steps.place_outputs = spread_sums, place_reciprocals, place_outputs
    return steps


def normalise_outputs(pool, S, M, g, n):
    pool.wait_ge(S.rec_ld, 16 * REP * (n + 1))
    if n >= 1:
        pool.wait_ge(S.at, 16 * REP * n)
    pool.tensor_tensor(M.on[:], M.o[:, g % 2, :], M.rec_rows[:], ALU.mult).then_inc(S.on, 1)


def reciprocals(dve, S, M, n):
    dve.wait_ge(S.sum_ld, 16 * (n + 1))
    if n >= 1:
        dve.wait_ge(S.rec_st, 16 * n)
    dve.reciprocal(M.rec[:], M.sums[:]).then_inc(S.rec, 1)


def project(nc, S, M, A, T, b, tag, with_tail):
    with ExitStack() as ctx:
        def sb(name, shape, dt=F32):
            return ctx.enter_context(nc.sbuf_tensor(name + tag, shape, dt))

        def ps(name, shape, dt=F32):
            return ctx.enter_context(nc.psum_tensor(name + tag, shape, dt))

        x_i = sb("x_i", [P, SEQ], I32)
        x_f = sb("x_f", [P, SEQ])
        x_n = sb("x_n", [P, SEQ])
        hot = sb("hot", [P, SEQ], BF16)
        h = sb("h", [P, TB, D])
        stats = sb("p_stats", [P, TB, 6])
        mv = sb("p_mv", [P, TB, 2])
        veps = sb("p_veps", [P, TB])
        rstd = sb("p_rstd_sb", [P, TB])
        xn = sb("xn", [P, 2, D])
        x_t = sb("x_t", [P, DC, SEQ])
        r1 = sb("r1", [P, 2, BANK])
        parts = sb("parts", [P, 2, 3, BANK], BF16)
        ps_d = T.ps_s1
        ps_t = ps("ps_t", [P, 2, BANK])
        ps_v = ps("ps_v", [P, BANK])
        ps_q = ps("ps_q", [P, 2, BANK])
        block = ctx.enter_context(nc.Block())
        qk_items = [(0, 0), (0, HC), (0, 1), (0, 2), (1, 0), (1, HC), (0, 3), (1, 1), (1, 2), (1, 3)]
        GROUP0_ITEMS = 6
        first_tile = TB // QH + 1
        beside_tiles = TB + 1 - first_tile

        stage1_uses = T.at[-1]

        @block.sync
        def _(sp):
            tail = output_sync(sp, S, A, M, b * SEQ - SEQ, 1 - KV_HEADS)
            if with_tail:
                tail.spread_sums(KV_HEADS - 1)
            sp.dma_start(x_i[:], A.x_row[bass.ds(b * SEQ, SEQ)].partition_broadcast(P)).then_inc(S.x_row, 16)
            for t in range(TB):
                sp.wait_ge(S.h0, t + 1)
                sp.dma_start(A.h_dram[bass.ds(b * SEQ + t * P, P), :], h[:, t, :]).then_inc(S.h0_stored, 16)
                if with_tail and t == 0:
                    tail.place_reciprocals(KV_HEADS - 1)
                if with_tail and t == 3:
                    tail.place_outputs(KV_HEADS - 1)
            stage1 = stage1_sync(sp, S, A, T)
            for n, (half, m) in enumerate(qk_items):
                sp.wait_ge(S.qk_lo, n + 1)
                cols = slice(half * BANK, (half + 1) * BANK)
                dst = A.q_dram[:, m, :, cols] if m < HC else A.k_dram[:, :, cols]
                sp.dma_start(dst.rearrange("s p t -> p s t"), parts[:, n % 2]).then_inc(S.part_st[n % 2], 16)
                if n == GROUP0_ITEMS - 1:
                    for i in range(2):
                        sp.wait_ge(S.part_st[i], GROUP0_ITEMS // 2 * 16)
                    stage1.load_qk(0)
            stage1.load_qk(1)
            stage1.place_max(0)
            sp.wait_ge(S.h0_stored, TB * 16)
            for i in range(2):
                sp.wait_ge(S.part_st[i], len(qk_items) // 2 * 16)
            if with_tail:
                sp.wait_ge(S.at, 16 * REP)
            sp.wait_ge(S.mrow_ld, 16)

        @block.gpsimd
        def _(pool):
            pool.tensor_copy(M.idx_b[:], M.idx_all[:, bass.ds(b * TB, TB)]).then_inc(S.idx, 1)
            pool.wait_ge(S.idx, 1)
            for t in range(TB):
                pool.indirect_dma_start(out=h[:, t, :], out_offset=None, in_=A.W,
                                        in_offset=bass.IndirectOffsetOnAxis(ap=M.idx_b[:, t:t + 1], axis=0),
                                        ).then_inc(S.gather[t], 16)
            pool.memset(M.v[:], 0.0).then_inc(S.v_const, 1)
            pool.wait_ge(S.v_const, 1)
            pool.memset(M.v[:, :, :, 0:1], 1.0).then_inc(S.v_const, 1)
            def low_part(n):
                pool.wait_ge(S.qk_mid, n + 1)
                if n >= 2:
                    pool.wait_ge(S.part_st[n % 2], n // 2 * 16)
                pool.tensor_tensor(parts[:, n % 2, 2, :], r1[:, n % 2, :], parts[:, n % 2, 1, :],
                                   ALU.subtract).then_inc(S.qk_lo, 1)

            for t in range(TB):
                pool.wait_ge(S.p_var, t + 1)
                pool.tensor_tensor(rstd[:, t:t + 1], veps[:, t:t + 1], M.neg_half[:], ALU.pow).then_inc(S.p_rstd, 1)
                if with_tail and t == 2:
                    normalise_outputs(pool, S, M, KV_HEADS - 1, 0)
                if t >= first_tile + 2:
                    low_part(t - first_tile - 2)
            for n in range(beside_tiles - 3, len(qk_items)):
                low_part(n)

        @block.vector
        def _(dve):
            n = [0]

            def link(ins):
                n[0] += 1
                ins.then_inc(S.p_vec, 1)
                dve.wait_ge(S.p_vec, n[0])

            dve.wait_ge(S.x_row, 16)
            link(dve.tensor_copy(x_f[:], x_i[:]))
            link(dve.tensor_scalar(x_n[:], x_f[:], 0.0, float(VOCAB), ALU.is_lt, ALU.mult))
            link(dve.tensor_tensor(x_f[:], x_f[:], x_n[:], ALU.add))
            link(dve.tensor_scalar(x_f[:], x_f[:], 0.0, float(VOCAB - 1), ALU.max, ALU.min))
            dve.tensor_scalar(hot[:], x_f[:], M.tok[:], None, ALU.is_equal).then_inc(S.hot, 1)

            def embed(t):
                dve.wait_ge(S.gather[t], b * 16 + 16)
                dve.wait_ge(S.delta, t + 1)
                dve.tensor_tensor(h[:, t, :], h[:, t, :], ps_d[:, t % 2, :], ALU.add).then_inc(S.h0, 1)
                dve.wait_ge(S.h0, t + 1)
                link(dve.bn_stats(stats[:, t, :], h[:, t, :]))
                link(dve.bn_aggr(mv[:, t, :], stats[:, t, :]))
                dve.tensor_scalar(veps[:, t:t + 1], mv[:, t, 1:2], EPS, None, ALU.add).then_inc(S.p_var, 1)

            def normalise(t):
                dve.wait_ge(S.p_rstd, t + 1)
                if t >= 2:
                    dve.wait_ge(S.x_tr, t - 1)
                dve.tensor_scalar(xn[:, t % 2, :], h[:, t, :], mv[:, t, 0:1], rstd[:, t:t + 1],
                                  ALU.subtract, ALU.mult).then_inc(S.p_norm, 1)

            def remainder(i):
                scale = HD ** -0.5 if qk_items[i][1] < HC else 1.0
                dve.wait_ge(S.qk_hi, i + 1)
                if i >= 2:
                    dve.wait_ge(S.qk_lo, i - 1)
                dve.scalar_tensor_tensor(out=r1[:, i % 2, :], in0=ps_q[:, i % 2, :], scalar=scale,
                                         in1=parts[:, i % 2, 0, :], op0=ALU.mult,
                                         op1=ALU.subtract).then_inc(S.qk_r1, 1)

            embed(0)
            embed(1)
            for t in range(TB + 1):
                if t < TB:
                    normalise(t)
                if t + 2 < TB:
                    embed(t + 2)
                if with_tail and t == 0:
                    reciprocals(dve, S, M, 0)
                if t >= first_tile + 2:
                    remainder(t - first_tile - 2)
            for i in range(beside_tiles - 2, len(qk_items)):
                remainder(i)
            stage1 = stage1_vector(dve, S, T, link)
            for use in stage1_uses:
                stage1(*use)

        @block.scalar
        def _(act):
            def copy_x_t(t):
                act.wait_ge(S.x_tr, t + 1)
                act.activation(x_t[:, :, t * P:(t + 1) * P],
                               ps_t[:, t % 2, :].rearrange("p (c t) -> p c t", c=DC), ACT.Copy).then_inc(S.x_t, 1)

            def copy_v(t):
                act.wait_ge(S.v_ps, t + 1)
                if t == 0:
                    act.wait_ge(S.v_const, 2)
                act.activation(M.v[:, t, :, 1:1 + HD],
                               ps_v[:, 0:KV_HEADS * HD].rearrange("p (g d) -> p g d", g=KV_HEADS),
                               ACT.Copy).then_inc(S.v_sb, 1)

            def split(i):
                scale = HD ** -0.5 if qk_items[i][1] < HC else 1.0
                act.wait_ge(S.qk_ps, i + 1)
                if i >= 2:
                    act.wait_ge(S.part_st[i % 2], i // 2 * 16)
                act.activation(parts[:, i % 2, 0, :], ps_q[:, i % 2, :], ACT.Copy, scale=scale).then_inc(S.qk_hi, 1)
                act.wait_ge(S.qk_r1, i + 1)
                act.activation(parts[:, i % 2, 1, :], r1[:, i % 2, :], ACT.Copy).then_inc(S.qk_mid, 1)

            for t in range(TB + 1):
                if t < TB:
                    copy_x_t(t)
                if t >= 1:
                    copy_v(t - 1)
                if t > first_tile:
                    split(t - first_tile - 1)
            for i in range(beside_tiles - 1, len(qk_items)):
                split(i)

        @block.tensor
        def _(pe):
            def add_delta(t):
                if t >= 2:
                    pe.wait_ge(S.h0, t - 1)
                pe.matmul(ps_d[:, t % 2, :], hot[:, t * P:(t + 1) * P], M.d_hm[:], start=True, stop=False)
                pe.matmul(ps_d[:, t % 2, :], hot[:, t * P:(t + 1) * P], M.d_lo[:], start=False,
                          stop=True).then_inc(S.delta, 1)

            def transposes(t):
                pe.wait_ge(S.p_norm, t + 1)
                if t >= 2:
                    pe.wait_ge(S.x_t, t - 1)
                for c in range(DC):
                    last = pe.transpose(ps_t[:, t % 2, c * P:(c + 1) * P], xn[:, t % 2, c * P:(c + 1) * P],
                                        M.ident[:])
                last.then_inc(S.x_tr, 1)

            def values(t):
                pe.wait_ge(S.x_t, t + 1)
                if t >= 1:
                    pe.wait_ge(S.v_sb, t)
                for c in range(DC):
                    last = pe.matmul(ps_v[:, 0:KV_HEADS * HD], x_t[:, c, t * P:(t + 1) * P], M.wv[:, c, :],
                                     start=(c == 0), stop=(c == DC - 1))
                last.then_inc(S.v_ps, 1)

            def queries_keys(i):
                half, m = qk_items[i]
                w = M.wq[:, :, m * P:(m + 1) * P] if m < HC else M.wk[:]
                if i >= 2:
                    pe.wait_ge(S.qk_r1, i - 1)
                for c in range(DC):
                    last = pe.matmul(ps_q[:, i % 2, :], w[:, c, :], x_t[:, c, half * BANK:(half + 1) * BANK],
                                     start=(c == 0), stop=(c == DC - 1))
                last.then_inc(S.qk_ps, 1)

            pe.wait_ge(S.hot, 1)
            add_delta(0)
            add_delta(1)
            for t in range(TB + 1):
                if t + 2 < TB:
                    add_delta(t + 2)
                if t < TB:
                    transposes(t)
                if t >= 1:
                    values(t - 1)
                if t >= first_tile:
                    queries_keys(t - first_tile)
            for i in range(beside_tiles, len(qk_items)):
                queries_keys(i)
            stage1 = stage1_tensor(pe, S, M, T)
            for use in stage1_uses:
                stage1(*use)


def attend(nc, S, M, A, T, b, tag, with_ffn):
    with ExitStack() as ctx:
        def sb(name, shape, dt=F32):
            return ctx.enter_context(nc.sbuf_tensor(name + tag, shape, dt))

        def ps(name, shape, dt=F32):
            return ctx.enter_context(nc.psum_tensor(name + tag, shape, dt))

        probs = sb("probs", [P, 2, REP, BANK])
        ps_s2 = ps("ps_s2", [P, 2, 2, BANK])
        ps_o = ps("ps_o", [P, BANK])
        F = None
        earlier = 1 if with_ffn else 0
        if with_ffn:
            banks = ps("ffn_banks", [P, 1, BANK])
            order = [use[:3] for x in range(ITEMS) for use in ffn_uses_at(x) if use[3] == 0]
            F = ffn_memory(sb, banks, plan_banks(order, {kind: (0,) for kind in ("wo", "xt", "u", "yt", "f2")}),
                           slots=FFN_SLOTS_BESIDE)
        block = ctx.enter_context(nc.Block())

        def beside(schedule, x):
            return [t for t in range(TB) if x == schedule + FFN_PERIOD * t] if with_ffn else []

        @block.sync
        def _(sp):
            stage1 = stage1_sync(sp, S, A, T)
            outputs = output_sync(sp, S, A, M, b * SEQ, earlier)
            if with_ffn:
                ffn = ffn_sync(sp, S, A, F, b * SEQ - SEQ)
            if with_ffn:
                ffn.load(0)
            for x in range(ITEMS):
                g, y = x // GROUP_ITEMS, x % GROUP_ITEMS
                if y == 1 and g + 2 < KV_HEADS:
                    stage1.load_qk(g + 2)
                if y == 3 and g >= 1:
                    sp.wait_ge(S.o, QH * g)
                    outputs.spread_sums(g - 1)
                if y == 7 and g >= 1:
                    outputs.place_reciprocals(g - 1)
                if y == 12 and g >= 1:
                    outputs.place_outputs(g - 1)
                for t in beside(AT_LOAD, x):
                    ffn.load(t)
                for t in beside(AT_FINISH, x):
                    ffn.store(t)
                for _, kind, group, _ in T.at.get(x, ()):
                    if kind == "max":
                        stage1.place_max(group)
            sp.wait_ge(S.at, 16 * REP * (KV_HEADS - 1 + earlier))
            if with_ffn:
                ffn.wait_stores()

        @block.gpsimd
        def _(pool):
            for slot in range(QK_SLOTS):
                pool.memset(T.k6[slot][PART_ROWS:SCORE_ROWS, :], 1.0).then_inc(S.ones, 1)
            if with_ffn:
                ffn = ffn_gpsimd(pool, S, M, F)
            for x in range(ITEMS):
                if x >= GROUP_ITEMS and x % GROUP_ITEMS == 10:
                    g = x // GROUP_ITEMS - 1
                    normalise_outputs(pool, S, M, g, g + earlier)
                for t in beside(AT_STATS, x):
                    ffn.rstd_h1(t)
                for t in beside(AT_SQUARE_X2, x):
                    ffn.rms_x2(t)
                for t in beside(AT_NORM + 2, x):
                    ffn.add_b2(t)
                for t in beside(AT_SILU, x):
                    ffn.silu(t)
                for t in beside(AT_STATS_G + UC, x):
                    ffn.scale_g(t)
                for t in beside(AT_SQUARE_Y, x):
                    ffn.rms_y(t)

        @block.vector
        def _(dve):
            n = [0]

            def link(ins):
                n[0] += 1
                ins.then_inc(S.a_vec, 1)
                dve.wait_ge(S.a_vec, n[0])

            stage1 = stage1_vector(dve, S, T, link)
            if with_ffn:
                ffn = ffn_vector(dve, S, M, F, link)
            for x in range(ITEMS):
                for use in T.at.get(x, ()):
                    stage1(*use)
                if x >= GROUP_ITEMS and x % GROUP_ITEMS == 6:
                    reciprocals(dve, S, M, x // GROUP_ITEMS - 1 + earlier)
                for t in beside(AT_RESIDUAL, x):
                    ffn.residual(t)
                for t in beside(AT_STATS, x):
                    ffn.stats_h1(t)
                for t in beside(AT_NORM, x):
                    ffn.norm_x2(t)
                for t in beside(AT_NORM + 1, x):
                    ffn.max_x2(t)
                for t in beside(AT_QUANT_X, x):
                    ffn.scale_x2(t)
                for t in beside(AT_QUANT_X + 1, x):
                    ffn.quantise_x2(t)
                for c in range(UC):
                    for t in beside(AT_U + 2 * c + 1, x):
                        ffn.dequantise_u(t, c)
                    for t in beside(AT_STATS_G + c, x):
                        ffn.stats_g(t, c)
                    for t in beside(AT_MAX_Y + c, x):
                        ffn.max_y(t, c)
                for t in beside(AT_STATS_G + UC, x):
                    ffn.variance_g(t)
                for t in beside(AT_SCALE_Y, x):
                    ffn.scale_y(t)
                for t in beside(AT_QUANT_Y, x):
                    ffn.quantise_y(t)
                for t in beside(AT_FINISH, x):
                    ffn.finish(t)

        @block.scalar
        def _(act):
            def outputs(seg):
                g, half = seg // QH, seg % QH
                act.wait_ge(S.pv, TB * (seg + 1))
                if g >= 2:
                    act.wait_ge(S.on, g - 1 + earlier)
                act.activation(M.o[:, g % 2, half * BANK:(half + 1) * BANK], ps_o[:], ACT.Copy).then_inc(S.o, 1)

            def exponentials(x):
                tile, pair = x // 2, x % 2
                if tile >= 2 and pair == 0:
                    act.wait_ge(S.pv, tile - 1)
                act.wait_ge(S.s2, x + 1)
                act.activation(probs[:, tile % 2, 2 * pair:2 * pair + 2, :], ps_s2[:, x % 2, :, :],
                               ACT.Exp).then_inc(S.exp, 1)

            if with_ffn:
                ffn = ffn_scalar(act, S, M, F)
            for x in range(ITEMS):
                exponentials(x)
                for t in beside(AT_SQUARE_X2, x):
                    ffn.square_x2(t)
                for t in beside(AT_XT + 1, x):
                    ffn.copy_xq_t(t)
                for t in beside(AT_TANH, x):
                    ffn.tanh(t)
                for t in beside(AT_GELU, x):
                    ffn.gelu(t)
                for t in beside(AT_SQUARE_Y, x):
                    ffn.square_y(t)
                for t in beside(AT_ROUND_Y, x):
                    ffn.round_y(t)
                for half in range(2):
                    for t in beside(AT_YT + 2 * half + 1, x):
                        ffn.copy_yq_t(t, half)
                if x >= SEG_ITEMS and x % SEG_ITEMS == 1:
                    outputs(x // SEG_ITEMS - 1)
            outputs(KV_HEADS * QH - 1)

        @block.tensor
        def _(pe):
            stage1 = stage1_tensor(pe, S, M, T)

            def stage2(x):
                g, half, kt, pair = x // GROUP_ITEMS, x // SEG_ITEMS % QH, x // 2 % TB, x % 2
                if x % GROUP_ITEMS == 0:
                    pe.wait_ge(S.mrow_ld, 16 * (g + 1))
                if x >= 2:
                    pe.wait_ge(S.exp, x - 1)
                slot = g % QK_SLOTS
                for i in range(2):
                    last = pe.matmul(ps_s2[:, x % 2, i, :], T.k6[slot][:, kt * P:(kt + 1) * P],
                                     T.q6[slot][:, 2 * pair + i, half * BANK:(half + 1) * BANK],
                                     start=True, stop=True)
                last.then_inc(S.s2, 1)

            def weigh(tile):
                g, kt = tile // TB // QH, tile % TB
                pe.wait_ge(S.exp, 2 * (tile + 1))
                if kt == 0 and tile >= TB:
                    pe.wait_ge(S.o, tile // TB)
                for j in range(REP):
                    last = pe.matmul(ps_o[j * VW:(j + 1) * VW, :], M.v[:, kt, g, :], probs[:, tile % 2, j, :],
                                     start=(kt == 0), stop=(kt == TB - 1), skip_group_check=True)
                last.then_inc(S.pv, 1)

            if with_ffn:
                ffn = ffn_tensor(pe, S, M, F)
            pe.wait_ge(S.ones, QK_SLOTS)
            for x in range(ITEMS):
                uses = T.at.get(x, ())
                for use in uses[:1]:
                    stage1(*use)
                stage2(x)
                for use in uses[1:]:
                    stage1(*use)
                if with_ffn:
                    for piece in ffn_uses_at(x):
                        ffn.run(*piece)
                if x % 2 == 1 and x > 1:
                    weigh(x // 2 - 1)
            weigh(ITEMS // 2 - 1)


FFN_PERIOD = 26
AT_LOAD = -18
AT_WO = 0
AT_RESIDUAL = 7
AT_STATS = 8
AT_NORM = 10
AT_SQUARE_X2 = 11
AT_QUANT_X = 13
AT_XT = 16
AT_U = 18
AT_TANH = 26
AT_SILU = 27
AT_GELU = 31
AT_STATS_G = 35
AT_MAX_Y = 47
AT_SQUARE_Y = 47
AT_SCALE_Y = 51
AT_ROUND_Y = 52
AT_QUANT_Y = 54
AT_YT = 60
AT_F2 = 64
AT_FINISH = 67
FFN_SLOTS_BESIDE = dict(h1=4, at=2, x2=1, xq=1, u=2, yq=1)
FFN_SLOTS_ALONE = dict(h1=8, at=3, x2=3, xq=2, u=5, yq=2)


def ffn_share(x):
    y = x % FFN_PERIOD
    if y == (AT_GELU + 2) % FFN_PERIOD:
        return 6
    if y in ((AT_TANH + 2) % FFN_PERIOD, (AT_SQUARE_Y + 2) % FFN_PERIOD, (AT_ROUND_Y + 2) % FFN_PERIOD):
        return 3
    return 1.7


def ffn_uses_at(x):
    pieces = []
    for t in range(TB):
        at = x - FFN_PERIOD * t
        if at - AT_WO in range(0, 2 * HC, 2):
            pieces.append(("wo", t, 0, (at - AT_WO) // 2))
        if at == AT_XT:
            pieces.append(("xt", t, 0, 0))
        if at - AT_U in range(0, 2 * UC, 2):
            pieces.append(("u", t, (at - AT_U) // 2, 0))
        if at - AT_YT in (0, 2):
            pieces.append(("yt", t, (at - AT_YT) // 2, 0))
        if at - AT_F2 in (0, 1):
            pieces.append(("f2", t, 0, at - AT_F2))
    return pieces


def plan_banks(order, rings):
    bank, before, last, count = {}, {}, {}, {}
    for use in order:
        ring = rings[use[0]]
        k = ring[count.get(use[0], 0) % len(ring)]
        count[use[0]] = count.get(use[0], 0) + 1
        bank[use], before[use], last[k] = k, last.get(k), use
    return bank, before


def read_of(S, use):
    kind, t, n = use
    return {"wo": (S.h1, t + 1), "xt": (S.xq_t, t + 1), "u": (S.u, t * UC + n + 1),
            "yt": (S.yq_t, 2 * t + n + 1), "f2": (S.f_o, t + 1)}[kind]


def ffn_memory(sb, banks, plan, slots):
    F = Names()
    F.slots, F.banks = slots, banks
    F.bank, F.before = plan
    F.h1 = sb("h1", [P, slots["h1"], D])
    F.at = sb("at", [P, slots["at"], HC, P])
    F.x2 = sb("x2", [P, slots["x2"], D])
    F.xq = sb("xq", [P, slots["xq"], D], BF16)
    F.xq_t = sb("xq_t", [P, slots["xq"], D], BF16)
    F.u = sb("u", [P, slots["u"], INNER])
    F.th = sb("th", [P, INNER])
    F.yq = sb("yq", [P, slots["yq"], INNER], BF16)
    F.yq_t = sb("yq_t", [P, slots["yq"], INNER], BF16)
    F.fo = sb("fo", [P, 2, D])
    F.st = sb("f_st", [P, TB, 6])
    F.mv = sb("f_mv", [P, TB, 2])
    F.gst = sb("f_gst", [P, TB, UC * 6])
    F.gmv = sb("f_gmv", [P, TB, 2])
    F.yc = sb("f_yc", [P, TB, UC])
    F.veps, F.r0, F.ss, F.mx = (sb("c_" + n, [P, TB]) for n in ("veps", "r0", "ss", "mx"))
    F.ms, F.r1, F.am, F.rc = (sb("c_" + n, [P, TB]) for n in ("ms", "r1", "am", "rc"))
    F.qs, F.a1, F.gveps, F.gr = (sb("c_" + n, [P, TB]) for n in ("qs", "a1", "gveps", "gr"))
    F.gnm = sb("c_gnm", [P, TB])
    F.yss, F.ymx, F.yms, F.yr = (sb("c_" + n, [P, TB]) for n in ("yss", "ymx", "yms", "yr"))
    F.yam, F.yrc, F.yqs, F.a2 = (sb("c_" + n, [P, TB]) for n in ("yam", "yrc", "yqs", "a2"))
    return F


def col(c, t):
    return c[:, t:t + 1]


def ffn_sync(sp, S, A, F, first_token):
    steps = Names()

    def load(t):
        hs, ats = F.slots["h1"], F.slots["at"]
        if t >= hs:
            sp.wait_ge(S.f_o, t - hs + 1)
        sp.dma_start(F.h1[:, t % hs, :], A.h_dram[bass.ds(first_token + t * P, P), :]).then_inc(S.f_h[t], 16)
        if t >= ats:
            sp.wait_ge(S.wo, t - ats + 1)
        sp.dma_start(F.at[:, t % ats], A.attn_dram[:, bass.ds(first_token + t * P, P)].rearrange(
            "(c p) t -> p c t", p=P)).then_inc(S.f_h[t], 16)

    def store(t):
        sp.wait_ge(S.f_o, t + 1)
        sp.dma_start(A.out[bass.ds(first_token + t * P, P), :], F.fo[:, t % 2, :]).then_inc(S.out_st[t % 4], 16)

    def wait_stores():
        for i in range(4):
            sp.wait_ge(S.out_st[i], TB // 4 * 16)

    steps.load, steps.store, steps.wait_stores = load, store, wait_stores
    return steps


def ffn_gpsimd(pool, S, M, F):
    steps = Names()
    n = [0]

    def link(ins):
        n[0] += 1
        ins.then_inc(S.f_pool, 1)
        pool.wait_ge(S.f_pool, n[0])

    def rstd_h1(t):
        pool.wait_ge(S.f_var, t + 1)
        pool.tensor_tensor(col(F.r0, t), col(F.veps, t), M.neg_half[:], ALU.pow).then_inc(S.f_r0, 1)

    def rms_x2(t):
        pool.wait_ge(S.x2_ss, t + 1)
        link(pool.tensor_scalar(col(F.ms, t), col(F.ss, t), 1.0 / D, EPS, ALU.mult, ALU.add))
        pool.tensor_tensor(col(F.r1, t), col(F.ms, t), M.neg_half[:], ALU.pow).then_inc(S.x2_r, 1)

    def add_b2(t):
        h = F.h1[:, t % F.slots["h1"], :]
        pool.wait_ge(S.x2, t + 1)
        pool.tensor_tensor(h, h, M.b2[:], ALU.add).then_inc(S.h1_b2, 1)

    def silu(t):
        u = F.u[:, t % F.slots["u"], :]
        pool.wait_ge(S.tanh, t + 1)
        link(pool.tensor_scalar(F.th[:], F.th[:], 1.0, 1.0, ALU.add, ALU.mult))
        pool.tensor_tensor(u, u, F.th[:], ALU.mult).then_inc(S.silu, 1)

    def scale_g(t):
        u = F.u[:, t % F.slots["u"], :]
        pool.wait_ge(S.g_var, 2 * (t + 1))
        link(pool.tensor_tensor(col(F.gr, t), col(F.gveps, t), M.neg_half[:], ALU.pow))
        link(pool.tensor_scalar(u, u, col(F.gnm, t), col(F.gr, t), ALU.add, ALU.mult))
        link(pool.tensor_tensor(u, u, M.ln_g[:], ALU.mult))
        pool.tensor_tensor(u, u, M.ln_b[:], ALU.add).then_inc(S.y, 1)

    def rms_y(t):
        pool.wait_ge(S.y_ss, t + 1)
        link(pool.tensor_scalar(col(F.yms, t), col(F.yss, t), 1.0 / INNER, EPS, ALU.mult, ALU.add))
        pool.tensor_tensor(col(F.yr, t), col(F.yms, t), M.neg_half[:], ALU.pow).then_inc(S.y_r, 1)

    steps.rstd_h1, steps.rms_x2, steps.add_b2, steps.silu = rstd_h1, rms_x2, add_b2, silu
    steps.scale_g, steps.rms_y = scale_g, rms_y
    return steps


def ffn_vector(dve, S, M, F, link):
    steps = Names()
    hs, xs, qs, us, ys = (F.slots[k] for k in ("h1", "x2", "xq", "u", "yq"))

    def chunk(c):
        return slice(c * BANK, (c + 1) * BANK)

    def residual(t):
        dve.wait_ge(S.wo, t + 1)
        h = F.h1[:, t % hs, :]
        dve.tensor_tensor(h, F.banks[:, F.bank["wo", t, 0], :], h, ALU.add).then_inc(S.h1, 1)

    def stats_h1(t):
        dve.wait_ge(S.h1, t + 1)
        link(dve.bn_stats(F.st[:, t, :], F.h1[:, t % hs, :]))
        link(dve.bn_aggr(F.mv[:, t, :], F.st[:, t, :]))
        dve.tensor_scalar(col(F.veps, t), F.mv[:, t, 1:2], EPS, None, ALU.add).then_inc(S.f_var, 1)

    def norm_x2(t):
        dve.wait_ge(S.f_r0, t + 1)
        if t >= xs:
            dve.wait_ge(S.x2_ss, t - xs + 1)
        dve.tensor_scalar(F.x2[:, t % xs, :], F.h1[:, t % hs, :], F.mv[:, t, 0:1], col(F.r0, t),
                          ALU.subtract, ALU.mult).then_inc(S.x2, 1)

    def max_x2(t):
        dve.wait_ge(S.x2, t + 1)
        link(dve.tensor_reduce(col(F.mx, t), F.x2[:, t % xs, :], AX, ALU.max, apply_absolute_value=True))

    def scales(am, rc, qsc, a, mx, r, w, t):
        link(dve.tensor_scalar(col(am, t), col(mx, t), col(r, t), 1e-5, ALU.mult, ALU.max))
        link(dve.reciprocal(col(rc, t), col(am, t)))
        link(dve.tensor_scalar(col(a, t), col(am, t), M.w_dq[:, w:w + 1], None, ALU.mult))
        return dve.tensor_scalar(col(qsc, t), col(rc, t), 127.0, col(r, t), ALU.mult, ALU.mult)

    def scale_x2(t):
        dve.wait_ge(S.x2_r, t + 1)
        link(scales(F.am, F.rc, F.qs, F.a1, F.mx, F.r1, 0, t))

    def quantise_x2(t):
        x2 = F.x2[:, t % xs, :]
        link(dve.tensor_scalar(x2, x2, col(F.qs, t), ROUND, ALU.mult, ALU.add))
        dve.tensor_scalar(F.xq[:, t % qs, :], x2, ROUND, 127.0, ALU.subtract, ALU.min).then_inc(S.xq, 1)

    def dequantise_u(t, c):
        dve.wait_ge(S.u_ps, t * UC + c + 1)
        if t >= us and c == 0:
            dve.wait_ge(S.yq, t - us + 1)
        dve.scalar_tensor_tensor(out=F.u[:, t % us, chunk(c)], in0=F.banks[:, F.bank["u", t, c], :],
                                 scalar=col(F.a1, t), in1=M.b1[:, chunk(c)], op0=ALU.mult,
                                 op1=ALU.add).then_inc(S.u, 1)

    def silu(t):
        u = F.u[:, t % us, :]
        dve.wait_ge(S.tanh, t + 1)
        dve.scalar_tensor_tensor(out=u, in0=F.th[:], scalar=1.0, in1=u, op0=ALU.add,
                                 op1=ALU.mult).then_inc(S.silu, 1)

    def stats_g(t, c):
        dve.wait_ge(S.gelu, t + 1)
        dve.bn_stats(F.gst[:, t, 6 * c:6 * c + 6], F.u[:, t % us, chunk(c)]).then_inc(S.g_stats, 1)

    def variance_g(t):
        dve.wait_ge(S.g_stats, UC * (t + 1))
        link(dve.bn_aggr(F.gmv[:, t, :], F.gst[:, t, :]))
        dve.tensor_scalar(col(F.gnm, t), F.gmv[:, t, 0:1], -1.0, None, ALU.mult).then_inc(S.g_var, 1)
        dve.tensor_scalar(col(F.gveps, t), F.gmv[:, t, 1:2], EPS, None, ALU.add).then_inc(S.g_var, 1)

    def max_y(t, c):
        dve.wait_ge(S.y, t + 1)
        dve.tensor_reduce(F.yc[:, t, c:c + 1], F.u[:, t % us, chunk(c)], AX, ALU.max,
                          apply_absolute_value=True).then_inc(S.y_max, 1)

    def scale_y(t):
        dve.wait_ge(S.y_max, UC * (t + 1))
        link(dve.tensor_reduce(col(F.ymx, t), F.yc[:, t, :], AX, ALU.max))
        dve.wait_ge(S.y_r, t + 1)
        scales(F.yam, F.yrc, F.yqs, F.a2, F.ymx, F.yr, 1, t).then_inc(S.y_qs, 1)

    def quantise_y(t):
        dve.wait_ge(S.y_shift, t + 1)
        dve.tensor_scalar(F.yq[:, t % ys, :], F.u[:, t % us, :], ROUND, 127.0, ALU.subtract,
                          ALU.min).then_inc(S.yq, 1)

    def finish(t):
        dve.wait_ge(S.o_ps, t + 1)
        dve.wait_ge(S.h1_b2, t + 1)
        if t >= 2:
            dve.wait_ge(S.out_st[(t - 2) % 4], 16 * ((t - 2) // 4 + 1))
        dve.scalar_tensor_tensor(out=F.fo[:, t % 2, :], in0=F.banks[:, F.bank["f2", t, 0], :],
                                 scalar=col(F.a2, t), in1=F.h1[:, t % hs, :], op0=ALU.mult,
                                 op1=ALU.add).then_inc(S.f_o, 1)

    steps.residual, steps.stats_h1, steps.norm_x2, steps.max_x2 = residual, stats_h1, norm_x2, max_x2
    steps.scale_x2, steps.quantise_x2, steps.dequantise_u = scale_x2, quantise_x2, dequantise_u
    steps.silu, steps.stats_g, steps.variance_g, steps.max_y = silu, stats_g, variance_g, max_y
    steps.scale_y, steps.quantise_y, steps.finish = scale_y, quantise_y, finish
    return steps


def ffn_scalar(act, S, M, F):
    steps = Names()
    xs, qs, us, ys = (F.slots[k] for k in ("x2", "xq", "u", "yq"))

    def square_x2(t):
        act.wait_ge(S.x2, t + 1)
        if t >= qs:
            act.wait_ge(S.xq_tr, t - qs + 1)
        act.activation(F.xq[:, t % qs, :], F.x2[:, t % xs, :], ACT.Square, accum_out=col(F.ss, t)).then_inc(S.x2_ss, 1)

    def copy_xq_t(t):
        act.wait_ge(S.xq_tr, t + 1)
        if t >= qs:
            act.wait_ge(S.u_ps, UC * (t - qs + 1))
        act.activation(F.xq_t[:, t % qs, :], F.banks[:, F.bank["xt", t, 0], :].bitcast(BF16)[:, 0:D],
                       ACT.Copy).then_inc(S.xq_t, 1)

    def tanh(t):
        act.wait_ge(S.u, UC * (t + 1))
        if t >= 1:
            act.wait_ge(S.silu, t)
        act.activation(F.th[:], F.u[:, t % us, :], ACT.Tanh, scale=0.5).then_inc(S.tanh, 1)

    def gelu(t):
        u = F.u[:, t % us, :]
        act.wait_ge(S.silu, t + 1)
        act.activation(u, u, ACT.Gelu, scale=0.5).then_inc(S.gelu, 1)

    def square_y(t):
        act.wait_ge(S.y, t + 1)
        if t >= ys:
            act.wait_ge(S.yq_tr, 2 * (t - ys + 1))
        act.activation(F.yq[:, t % ys, :], F.u[:, t % us, :], ACT.Square, accum_out=col(F.yss, t)).then_inc(S.y_ss, 1)

    def round_y(t):
        u = F.u[:, t % us, :]
        act.wait_ge(S.y_qs, t + 1)
        act.activation(u, u, ACT.Identity, bias=M.round_c[:], scale=col(F.yqs, t)).then_inc(S.y_shift, 1)

    def copy_yq_t(t, half):
        act.wait_ge(S.yq_tr, 2 * t + half + 1)
        if t >= ys and half == 0:
            act.wait_ge(S.o_ps, t - ys + 1)
        act.activation(F.yq_t[:, t % ys, half * 2 * BANK:(half + 1) * 2 * BANK],
                       F.banks[:, F.bank["yt", t, half], :].bitcast(BF16), ACT.Copy).then_inc(S.yq_t, 1)

    steps.square_x2, steps.copy_xq_t, steps.tanh, steps.gelu = square_x2, copy_xq_t, tanh, gelu
    steps.square_y, steps.round_y, steps.copy_yq_t = square_y, round_y, copy_yq_t
    return steps


def ffn_tensor(pe, S, M, F):
    steps = Names()
    ats, qs, ys = (F.slots[k] for k in ("at", "xq", "yq"))

    def bank(use):
        if F.before[use] is not None:
            pe.wait_ge(*read_of(S, F.before[use]))
        return F.banks[:, F.bank[use], :]

    def project_out(t, c):
        if c == 0:
            bank(("wo", t, 0))
            pe.wait_ge(S.f_h[t], 32)
        last = pe.matmul(F.banks[:, F.bank["wo", t, 0], :], F.at[:, t % ats, c, :], M.wo[:, c, :],
                         start=(c == 0), stop=(c == HC - 1))
        if c == HC - 1:
            last.then_inc(S.wo, 1)

    def transpose_xq(t):
        out = bank(("xt", t, 0)).bitcast(BF16)
        pe.wait_ge(S.xq, t + 1)
        for c in range(DC):
            last = pe.transpose(out[:, c * P:(c + 1) * P], F.xq[:, t % qs, c * P:(c + 1) * P], M.ident_bf[:])
        last.then_inc(S.xq_tr, 1)

    def product_1(t, n):
        out = bank(("u", t, n))
        pe.wait_ge(S.xq_t, t + 1)
        for c in range(DC):
            last = pe.matmul(out, F.xq_t[:, t % qs, c * P:(c + 1) * P], M.w1q[:, c, n * BANK:(n + 1) * BANK],
                             start=(c == 0), stop=(c == DC - 1))
        last.then_inc(S.u_ps, 1)

    def transpose_yq(t, half):
        out = bank(("yt", t, half)).bitcast(BF16)
        pe.wait_ge(S.yq, t + 1)
        for c in range(IC // 2):
            ic = half * IC // 2 + c
            last = pe.transpose(out[:, c * P:(c + 1) * P], F.yq[:, t % ys, ic * P:(ic + 1) * P], M.ident_bf[:])
        last.then_inc(S.yq_tr, 1)

    def product_2(t, half):
        if half == 0:
            bank(("f2", t, 0))
        pe.wait_ge(S.yq_t, 2 * t + half + 1)
        for c in range(half * IC // 2, (half + 1) * IC // 2):
            last = pe.matmul(F.banks[:, F.bank["f2", t, 0], :], F.yq_t[:, t % ys, c * P:(c + 1) * P],
                             M.w2q[:, c, :], start=(c == 0), stop=(c == IC - 1), skip_group_check=True)
        if half == 1:
            last.then_inc(S.o_ps, 1)

    def run(kind, t, n, piece):
        if kind == "wo":
            project_out(t, piece)
        elif kind == "xt":
            transpose_xq(t)
        elif kind == "u":
            product_1(t, n)
        elif kind == "yt":
            transpose_yq(t, n)
        else:
            product_2(t, piece)

    steps.run = run
    return steps


def feed_forward(nc, S, M, A, b, tag):
    with ExitStack() as ctx:
        def sb(name, shape, dt=F32):
            return ctx.enter_context(nc.sbuf_tensor(name + tag, shape, dt))

        def steps(*stages):
            return [(stage, s - lag) for s in range(TB + max(lag for _, lag in stages))
                    for stage, lag in stages if 0 <= s - lag < TB]

        banks = ctx.enter_context(nc.psum_tensor("ffn_banks" + tag, [P, 8, BANK], F32))
        kinds = steps(("wo", 0), ("xt", 1), ("u", 1), ("yt", 4), ("f2", 4))
        order = [(kind, t, n) for kind, t in kinds for n in range({"u": UC, "yt": 2}.get(kind, 1))]
        F = ffn_memory(sb, banks, plan_banks(order, {"wo": (0,), "xt": (1,), "u": (2, 3, 4), "yt": (5, 6),
                                                     "f2": (7,)}), slots=FFN_SLOTS_ALONE)
        block = ctx.enter_context(nc.Block())

        @block.sync
        def _(sp):
            tail = output_sync(sp, S, A, M, b * SEQ, 1 - KV_HEADS)
            tail.spread_sums(KV_HEADS - 1)
            tail.place_reciprocals(KV_HEADS - 1)
            tail.place_outputs(KV_HEADS - 1)
            sp.wait_ge(S.at, 16 * REP)
            ffn = ffn_sync(sp, S, A, F, b * SEQ)
            for stage, t in steps((ffn.load, 0), (ffn.store, 5)):
                stage(t)
            ffn.wait_stores()

        @block.gpsimd
        def _(pool):
            normalise_outputs(pool, S, M, KV_HEADS - 1, 0)
            ffn = ffn_gpsimd(pool, S, M, F)
            for stage, t in steps((ffn.rms_x2, 1), (ffn.rms_y, 4), (ffn.rstd_h1, 0), (ffn.add_b2, 1),
                                  (ffn.scale_g, 2)):
                stage(t)

        @block.vector
        def _(dve):
            n = [0]

            def link(ins):
                n[0] += 1
                ins.then_inc(S.f_vec, 1)
                dve.wait_ge(S.f_vec, n[0])

            reciprocals(dve, S, M, 0)
            ffn = ffn_vector(dve, S, M, F, link)

            def chunks(*per_chunk):
                def run(t):
                    for stage in per_chunk:
                        for c in range(UC):
                            stage(t, c)
                return run

            for stage, t in steps((ffn.scale_x2, 1), (ffn.quantise_x2, 1), (ffn.scale_y, 4), (ffn.residual, 0),
                                  (ffn.stats_h1, 0), (chunks(ffn.stats_g), 2), (ffn.variance_g, 2),
                                  (chunks(ffn.dequantise_u), 1), (ffn.norm_x2, 0), (ffn.quantise_y, 4),
                                  (ffn.max_x2, 0), (chunks(ffn.max_y), 3), (ffn.silu, 1), (ffn.finish, 5)):
                stage(t)

        @block.scalar
        def _(act):
            ffn = ffn_scalar(act, S, M, F)

            def copy_yq_t(t):
                for half in range(2):
                    ffn.copy_yq_t(t, half)

            for stage, t in steps((ffn.copy_xq_t, 1), (ffn.round_y, 4), (ffn.square_x2, 0), (ffn.tanh, 1),
                                  (ffn.square_y, 3), (copy_yq_t, 4), (ffn.gelu, 1)):
                stage(t)

        @block.tensor
        def _(pe):
            ffn = ffn_tensor(pe, S, M, F)
            for kind, t, n in order:
                for piece in range({"wo": HC, "f2": 2}.get(kind, 1)):
                    ffn.run(kind, t, n, piece)


def lm_tower(nc, x_row, x_col, W, delta_t, tokens, wq, wk, wv, wo, w1t, b1, ln_g, ln_b, w2t, b2, out):
    with ExitStack() as ctx:
        setup, batch, batch_range = semaphores(nc, ctx)

        def sb(name, shape, dt=F32):
            return ctx.enter_context(nc.sbuf_tensor(name, shape, dt))

        def dram(name, shape, dt=F32):
            return nc.dram_tensor(name, shape, dt, kind="Internal").ap()

        A = Names()
        A.x_row = x_row
        A.x_col = x_col
        A.W = W
        A.delta_t = delta_t
        A.tokens = tokens
        A.wq = wq
        A.wk = wk
        A.wv = wv
        A.wo = wo
        A.w1t = w1t
        A.b1 = b1
        A.ln_g = ln_g
        A.ln_b = ln_b
        A.w2t = w2t
        A.b2 = b2
        A.out = out
        A.attn_dram = dram("attn_dram", [HEADS * HD, TOKENS])
        A.h_dram = dram("h_dram", [TOKENS, D])
        A.q_dram = dram("q_dram", [3, HC, P, SEQ], BF16)
        A.k_dram = dram("k_dram", [3, P, SEQ], BF16)
        A.max_dram = dram("max_dram", [MAX_ROWS, REP * SEQ], BF16)
        A.sum_dram = dram("sum_dram", [REP * SEQ])
        A.rec_dram = dram("rec_dram", [REP * SEQ])
        M = Names()
        M.ident = sb("ident", [P, P])
        M.ident_bf = sb("ident_bf", [P, P], BF16)
        M.neg_half = sb("neg_half", [P, 1])
        M.round_c = sb("round_c", [P, 1])
        M.idx_all = sb("idx_all", [P, NT], U32)
        M.idx_b = sb("idx_b", [P, TB], U32)
        M.tok = sb("tok", [P, 1])
        M.d_hm = sb("d_hm", [P, D], BF16)
        M.d_lo = sb("d_lo", [P, D], BF16)
        M.wq = sb("wq_sb", [P, DC, HEADS * HD])
        M.wk = sb("wk_sb", [P, DC, KV_HEADS * HD])
        M.wv = sb("wv_sb", [P, DC, KV_HEADS * HD])
        M.wo = sb("wo_sb", [P, HC, D])
        M.b1 = sb("b1_sb", [P, INNER])
        M.ln_g = sb("ln_g_sb", [P, INNER])
        M.ln_b = sb("ln_b_sb", [P, INNER])
        M.b2 = sb("b2_sb", [P, D])
        M.w1q = sb("w1q", [P, DC, INNER], BF16)
        M.w2q = sb("w2q", [P, IC, D], BF16)
        M.w_mean = sb("w_mean", [P, 2])
        M.w_dq = sb("w_dq", [P, 2])
        M.v = sb("v", [P, TB, KV_HEADS, VW])

        M.o = sb("o", [P, 2, SEQ])
        M.on = sb("on", [P, SEQ])
        M.sums = sb("sums", [P, REP * SEQ // P])
        M.rec = sb("rec", [P, REP * SEQ // P])
        M.rec_rows = sb("rec_rows", [P, SEQ])

        def attention(b, tag, later):
            stage1 = plan_stage1(ffn_share if later else lambda x: 1)
            with ExitStack() as shared:
                T = attention_memory(nc, shared, stage1, tag)
                project(nc, batch, M, A, T, b, tag, with_tail=later)
                attend(nc, batch, M, A, T, b, tag, with_ffn=later)
            nc.all_engine_barrier(sems_to_clear=batch_range)

        set_up(nc, setup, M, A)
        attention(0, "_first", later=False)
        with nc.Fori(1, BATCH) as b:
            attention(b, "_loop", later=True)
        feed_forward(nc, batch, M, A, BATCH - 1, "_last")


def kernel(**inputs):
    import numpy as _np
    import concourse.bacc as _bacc
    from concourse import mybir as _mybir
    from concourse.bass_utils import run_bass_kernel_spmd as _run

    a = {k: _np.asarray(v) for k, v in inputs.items()}
    x = a["x"]
    n_train, dim = a["L0_tok_token_indices"].shape[0], a["L0_tok_W"].shape[1]
    laid_out = {
        "x_row": x.reshape(-1),
        "x_col": x.reshape(-1, 128).T,
        "W": a["L0_tok_W"],
        "delta_t": a["L0_tok_delta_values"].reshape(dim, n_train).T,
        "tokens": a["L0_tok_token_indices"].reshape(n_train, 1),
        "wq": a["L0_attn_Wq"], "wk": a["L0_attn_Wk"], "wv": a["L0_attn_Wv"], "wo": a["L0_attn_Wo"],
        "w1t": a["L0_ffn_w1"].T, "b1": a["L0_ffn_b1"], "ln_g": a["L0_ffn_ln_g"], "ln_b": a["L0_ffn_ln_b"],
        "w2t": a["L0_ffn_w2"].T, "b2": a["L0_ffn_b2"],
    }
    nc = _bacc.Bacc("TRN2", target_bir_lowering=False, num_devices=1)
    arrays, args = {}, []
    for name, v in laid_out.items():
        v = _np.ascontiguousarray(v)
        arrays[f"in_{name}"] = v
        args.append(nc.dram_tensor(f"in_{name}", v.shape, _mybir.dt.from_np(v.dtype), kind="ExternalInput").ap())
    out = nc.dram_tensor("out_0", (x.size, dim), _mybir.dt.from_np(_np.dtype("float32")), kind="ExternalOutput").ap()
    lm_tower(nc, *args, out)
    r = _run(nc, [arrays], core_ids=[0])
    return r.results[0]["out_0"].reshape(*x.shape, dim)
```

```python
from contextlib import ExitStack

import concourse.bass as bass
from concourse import mybir

F32 = mybir.dt.float32
BF16 = mybir.dt.bfloat16
I32 = mybir.dt.int32
U32 = mybir.dt.uint32
ALU = mybir.AluOpType
ACT = mybir.ActivationFunctionType
AX = mybir.AxisListType.X

P = 128
BATCH, SEQ = 4, 1024
TOKENS = BATCH * SEQ
VOCAB, D = 32000, 512
N_TRAIN = 64
HEADS, KV_HEADS, HD = 32, 8, 16
REP = HEADS // KV_HEADS
INNER = 2048
EPS = 1e-5
ROUND = 1.5 * 2.0 ** 23

DC = D // P
TB = SEQ // P
NT = TOKENS // P
IC = INNER // P
HC = HEADS * HD // P
BANK = 512
QH = SEQ // BANK
UC = INNER // BANK

Q_PARTS = (0, 0, 0, 1, 1, 2)
K_PARTS = (0, 1, 2, 0, 1, 0)
PART_ROWS = len(Q_PARTS) * HD
MAX_ROWS = 2
SCORE_ROWS = PART_ROWS + MAX_ROWS
VW = 32
QK_SLOTS = 3
K_RUNS = ((0, 3), (3, 2), (5, 1))
QK_LOADS = (len(Q_PARTS) + len(K_RUNS)) * 16

SEG_ITEMS = TB * REP // 2
GROUP_ITEMS = QH * SEG_ITEMS
ITEMS = KV_HEADS * GROUP_ITEMS
S1_BLOCKS = REP * TB * QH
S1_LEAD = 4


def plan_stage1(share):
    last = (KV_HEADS - 1) * GROUP_ITEMS - S1_LEAD
    rate = S1_BLOCKS * (KV_HEADS - 1) / (sum(share(x) for x in range(last)) or 1)
    done, total = [], 0.0
    for x in range(last):
        total += rate * share(x)
        done.append(total)
    ahead = max(S1_BLOCKS * g - done[g * GROUP_ITEMS - S1_LEAD - 1] for g in range(1, KV_HEADS))
    order, at, used = [], {}, 0
    pending = []
    for x in range(-1, last + 3):
        until = S1_BLOCKS * KV_HEADS if x >= last else int(S1_BLOCKS + ahead + (done[x] if x >= 0 else 0) + 0.999)
        events = [("max", g, S1_BLOCKS) for due, g in pending if due <= x]
        pending = [(due, g) for due, g in pending if due > x]
        for block in range(used, min(until, S1_BLOCKS * KV_HEADS)):
            g, i = divmod(block, S1_BLOCKS)
            events.append(("block", g, i))
            if i == S1_BLOCKS - 1 and g == 0:
                events.append(("max", 0, S1_BLOCKS))
            elif i == S1_BLOCKS - 1:
                pending.append((x + 2, g))
            used = block + 1
        for event in events:
            blocks = used_blocks(order) + (event[0] == "block")
            at.setdefault(x, []).append((len(order),) + event)
            order.append(event + (blocks,))
    return order, at


def used_blocks(order):
    return order[-1][3] if order else 0


class Names:
    pass


def semaphores(nc, stack):
    def sem(name):
        return stack.enter_context(nc.semaphore(name))

    setup = Names()
    setup.small = sem("small_loaded")
    setup.proj_w = sem("proj_weights_loaded")
    setup.ffn_w = [sem("w1_staged"), sem("w2_staged")]
    setup.rows = sem("token_rows_ready")
    setup.late_w = sem("later_weights_loaded")
    setup.const = sem("constants_set")
    setup.vec = sem("setup_vector_chain")
    setup.abs_sum = sem("abs_sum_ready")
    setup.abs_tot = sem("abs_total_ready")
    setup.mean = sem("mean_ready")
    setup.rounded = sem("weights_rounded")
    setup.clipped = sem("weights_clipped")
    gather = [sem(f"gathered{t}") for t in range(TB)]
    first = sem("batch_first")
    batch = Names()
    batch.gather = gather
    batch.x_row = sem("x_row_loaded")
    batch.idx = sem("indices_copied")
    batch.hot = sem("one_hot_ready")
    batch.delta = sem("delta_in_psum")
    batch.h0 = sem("h0_ready")
    batch.h0_stored = sem("h0_stored")
    batch.p_vec = sem("project_vector_chain")
    batch.p_var = sem("variance_ready")
    batch.p_rstd = sem("rstd_ready")
    batch.p_norm = sem("normalised_ready")
    batch.x_tr = sem("x_transposes_in_psum")
    batch.x_t = sem("x_t_ready")
    batch.v_ps = sem("v_in_psum")
    batch.v_sb = sem("v_ready")
    batch.v_const = sem("v_ones_set")
    batch.qk_ps = sem("qk_in_psum")
    batch.qk_hi = sem("qk_high_ready")
    batch.qk_r1 = sem("qk_remainder_ready")
    batch.qk_mid = sem("qk_middle_ready")
    batch.qk_lo = sem("qk_low_ready")
    batch.part_st = [sem(f"qk_parts_stored{i}") for i in range(2)]
    batch.qk_load = [sem(f"qk_parts_loaded{i}") for i in range(QK_SLOTS)]
    batch.g0_load = [sem(n) for n in ("first_halves_loaded", "k_second_half_loaded", "q_second_half_loaded")]
    batch.ones = sem("score_ones_set")
    batch.s1 = sem("stage1_in_psum")
    batch.s1_read = sem("stage1_read")
    batch.a_vec = sem("attend_vector_chain")
    batch.negmax = sem("negmax_ready")
    batch.mrow = sem("max_rows_ready")
    batch.mrow_st = sem("max_rows_stored")
    batch.mrow_ld = sem("max_rows_loaded")
    batch.s2 = sem("stage2_in_psum")
    batch.exp = sem("exp_ready")
    batch.pv = sem("pv_done")
    batch.o = sem("outputs_ready")
    batch.sum_st = sem("sums_stored")
    batch.sum_ld = sem("sums_loaded")
    batch.rec = sem("reciprocals_ready")
    batch.rec_st = sem("reciprocals_stored")
    batch.rec_ld = sem("reciprocals_loaded")
    batch.on = sem("outputs_normalised")
    batch.at = sem("attn_t_landed")
    batch.f_h = [sem(f"h0_loaded{t}") for t in range(TB)]
    batch.wo = sem("wo_in_psum")
    batch.h1 = sem("h1_ready")
    batch.h1_b2 = sem("h1_plus_b2_ready")
    batch.f_vec = sem("ffn_vector_chain")
    batch.f_pool = sem("ffn_pool_chain")
    batch.g_stats = sem("g_stats_ready")
    batch.y_max = sem("y_absmax_ready")
    batch.f_var = sem("h1_variance_ready")
    batch.f_r0 = sem("h1_rstd_ready")
    batch.x2 = sem("x2_ready")
    batch.x2_ss = sem("x2_squares_ready")
    batch.x2_r = sem("x2_rms_ready")
    batch.xq = sem("xq_ready")
    batch.xq_tr = sem("xq_transposes_in_psum")
    batch.xq_t = sem("xq_t_ready")
    batch.u_ps = sem("u_in_psum")
    batch.u = sem("u_ready")
    batch.tanh = sem("tanh_ready")
    batch.silu = sem("silu_ready")
    batch.gelu = sem("gelu_ready")
    batch.g_var = sem("g_variance_ready")
    batch.y = sem("y_ready")
    batch.y_ss = sem("y_squares_ready")
    batch.y_r = sem("y_rms_ready")
    batch.y_qs = sem("y_scale_ready")
    batch.y_shift = sem("y_shifted_ready")
    batch.yq = sem("yq_ready")
    batch.yq_tr = sem("yq_transposes_in_psum")
    batch.yq_t = sem("yq_t_ready")
    batch.o_ps = sem("ffn_out_in_psum")
    batch.f_o = sem("ffn_out_ready")
    batch.out_st = [sem(f"out_stored{i}") for i in range(4)]
    last = sem("batch_last")
    return setup, batch, range(first.num, last.num + 1)


def rows_of(weights):
    return weights.rearrange("(c p) n -> p c n", p=P)


def set_up(nc, S, M, A):
    with ExitStack() as ctx:
        def sb(name, shape, dt=F32):
            return ctx.enter_context(nc.sbuf_tensor(name, shape, dt))

        xc_i = sb("xc_i", [P, NT], I32)
        xc_f = sb("xc_f", [P, NT])
        xc_n = sb("xc_n", [P, NT])
        xr_i = sb("xr_i", [NT, P], I32)
        xr_f = sb("xr_f", [NT, P])
        xr_n = sb("xr_n", [NT, P])
        t_i = sb("t_i", [P, 1], I32)
        t_n = sb("t_n", [P, 1])
        dl = sb("dl", [P, D])
        dl_bf = sb("dl_bf", [P, D], BF16)
        dl_r1 = sb("dl_r1", [P, D])
        dl_r2 = sb("dl_r2", [P, D])
        block = ctx.enter_context(nc.Block())

        @block.sync
        def _(sp):
            sp.dma_start(xc_i[:], A.x_col).then_inc(S.small, 16)
            sp.dma_start(xr_i[:], A.x_row.rearrange("(t p) -> t p", p=P)).then_inc(S.small, 16)
            for half in range(2):
                rows = slice(half * N_TRAIN, (half + 1) * N_TRAIN)
                sp.dma_start(t_i[rows, :], A.tokens).then_inc(S.small, 16)
                sp.dma_start(dl[rows, :], A.delta_t).then_inc(S.small, 16)
            for dst, src in ((M.wv, A.wv), (M.wk, A.wk), (M.wq, A.wq)):
                sp.dma_start(dst[:], rows_of(src)).then_inc(S.proj_w, 16)
            sp.wait_ge(S.rows, 1)
            sp.dma_start(A.rows_dram.rearrange("(t p) -> t p", p=P), xr_f[:]).then_inc(S.proj_w, 16)
            sp.wait_ge(S.proj_w, 4 * 16)

        @block.gpsimd
        def _(pool):
            pool.memset(M.ident[:], 0.0).then_inc(S.const, 1)
            pool.memset(M.neg_half[:], -0.5).then_inc(S.const, 1)
            pool.memset(M.round_c[:], ROUND).then_inc(S.const, 1)
            pool.wait_ge(S.const, 3)
            pool.affine_select(out=M.ident[:], in_=M.ident[:], compare_op=ALU.not_equal, fill=1.0, base=0,
                               pattern=[[-1, P]], channel_multiplier=1).then_inc(S.const, 1)

        @block.vector
        def _(dve):
            n = [0]

            def link(ins):
                n[0] += 1
                ins.then_inc(S.vec, 1)
                dve.wait_ge(S.vec, n[0])

            dve.wait_ge(S.const, 4)
            link(dve.tensor_copy(M.ident_bf[:], M.ident[:]))
            dve.wait_ge(S.small, 6 * 16)

            for ids, f, negative in ((xr_i, xr_f, xr_n), (xc_i, xc_f, xc_n)):
                link(dve.tensor_copy(f[:], ids[:]))
                link(dve.tensor_scalar(negative[:], f[:], 0.0, float(VOCAB), ALU.is_lt, ALU.mult))
                link(dve.tensor_tensor(f[:], f[:], negative[:], ALU.add))
                last = dve.tensor_scalar(f[:], f[:], 0.0, float(VOCAB - 1), ALU.max, ALU.min)
                if f is xr_f:
                    last.then_inc(S.rows, 1)
                else:
                    link(last)
            link(dve.tensor_copy(M.idx_all[:], xc_f[:]))
            link(dve.tensor_copy(M.tok[:], t_i[:]))
            link(dve.tensor_scalar(t_n[:], M.tok[:], 0.0, float(VOCAB), ALU.is_lt, ALU.mult))
            link(dve.tensor_tensor(M.tok[:], M.tok[:], t_n[:], ALU.add))
            lower, upper = slice(0, N_TRAIN), slice(N_TRAIN, P)
            link(dve.tensor_copy(dl_bf[:], dl[:]))
            link(dve.tensor_tensor(dl_r1[:], dl[:], dl_bf[:], ALU.subtract))
            link(dve.tensor_copy(M.d_hm[lower, :], dl_bf[lower, :]))
            link(dve.tensor_copy(M.d_hm[upper, :], dl_r1[upper, :]))
            link(dve.tensor_copy(dl_bf[:], dl_r1[:]))
            link(dve.tensor_tensor(dl_r2[:], dl_r1[:], dl_bf[:], ALU.subtract))
            link(dve.memset(M.d_lo[:], 0.0))
            link(dve.tensor_copy(M.d_lo[lower, :], dl_r2[lower, :]))


def rows_of_stage(stage, chunks):
    return stage[:].rearrange("p (c n) -> p c n", c=chunks)


WEIGHT_START, WEIGHT_PERIOD = 8, 128
WEIGHT_CHUNKS = 16
WEIGHT_STEP = 3
AT_W_ABS = 0
AT_W_MEAN = 56
AT_W_ROUND = 58
AT_W_CLIP = 60


def weight_memory(sb):
    Q = Names()
    Q.stage = sb("stage", [P, DC * INNER])
    Q.abs_part = sb("abs_part", [P, WEIGHT_CHUNKS])
    Q.abs_sum = sb("abs_sum", [P, 2])
    Q.abs_tot = sb("abs_tot", [P, 2])
    Q.w_scale = sb("w_scale", [P, 2])
    Q.chunk = [Q.stage[:, c * DC * INNER // WEIGHT_CHUNKS:(c + 1) * DC * INNER // WEIGHT_CHUNKS]
               for c in range(WEIGHT_CHUNKS)]
    return Q


def weights_at(x, at, step=WEIGHT_STEP, count=WEIGHT_CHUNKS):
    y = [(w, x - WEIGHT_START - WEIGHT_PERIOD * w - at) for w in range(2)]
    return [(w, d // step) for w, d in y if 0 <= d < step * count and d % step == 0]


def weights_sync(sp, W, A, Q):
    def load(w):
        if w == 1:
            sp.wait_ge(W.clipped, WEIGHT_CHUNKS)
        src, chunks = ((A.w1t, DC), (A.w2t, IC))[w]
        sp.dma_start(rows_of_stage(Q.stage, chunks), rows_of(src)).then_inc(W.ffn_w[w], 16)

    return load


def weights_gpsimd(pool, W, Q):
    steps = Names()

    def total(w):
        pool.wait_ge(W.abs_sum, w + 1)
        pool.partition_all_reduce(Q.abs_tot[:, w:w + 1], Q.abs_sum[:, w:w + 1], P,
                                  bass.bass_isa.ReduceOp.add).then_inc(W.abs_tot, 1)

    def round_chunk(w, c):
        pool.wait_ge(W.mean, w + 1)
        pool.tensor_scalar(Q.chunk[c], Q.chunk[c], Q.w_scale[:, w:w + 1], ROUND, ALU.mult,
                           ALU.add).then_inc(W.rounded, 1)

    steps.total, steps.round_chunk = total, round_chunk
    return steps


def weights_vector(dve, W, M, Q, link):
    steps = Names()

    def abs_chunk(w, c):
        dve.wait_ge(W.ffn_w[w], 16)
        link(dve.tensor_reduce(Q.abs_part[:, c:c + 1], Q.chunk[c], AX, ALU.add, apply_absolute_value=True))
        if c == WEIGHT_CHUNKS - 1:
            dve.tensor_reduce(Q.abs_sum[:, w:w + 1], Q.abs_part[:], AX, ALU.add).then_inc(W.abs_sum, 1)

    def mean(w):
        dve.wait_ge(W.abs_tot, w + 1)
        link(dve.tensor_scalar(M.w_mean[:, w:w + 1], Q.abs_tot[:, w:w + 1], 1.0 / (D * INNER), 1e-5,
                               ALU.mult, ALU.max))
        link(dve.tensor_scalar(M.w_dq[:, w:w + 1], M.w_mean[:, w:w + 1], 1.0 / 127.0, None, ALU.mult))
        dve.reciprocal(Q.w_scale[:, w:w + 1], M.w_mean[:, w:w + 1]).then_inc(W.mean, 1)

    def clip_chunk(w, c):
        dve.wait_ge(W.rounded, WEIGHT_CHUNKS * w + c + 1)
        link(dve.tensor_scalar(Q.chunk[c], Q.chunk[c], ROUND, 1.0, ALU.subtract, ALU.min))
        n = DC * INNER // WEIGHT_CHUNKS
        dst = (M.w1q, M.w2q)[w][:].rearrange("p c n -> p (c n)")
        dve.tensor_scalar(dst[:, c * n:(c + 1) * n], Q.chunk[c], -1.0, None, ALU.max).then_inc(W.clipped, 1)

    steps.abs_chunk, steps.mean, steps.clip_chunk = abs_chunk, mean, clip_chunk
    return steps


def attention_memory(nc, ctx, S1, tag):
    T = Names()
    T.q6 = [ctx.enter_context(nc.sbuf_tensor(f"q6_{i}" + tag, [SCORE_ROWS, REP, SEQ], BF16)) for i in range(QK_SLOTS)]
    T.k6 = [ctx.enter_context(nc.sbuf_tensor(f"k6_{i}" + tag, [SCORE_ROWS, SEQ], BF16)) for i in range(QK_SLOTS)]
    T.half_max = ctx.enter_context(nc.sbuf_tensor("half_max" + tag, [P, 2, S1_BLOCKS], F32))
    T.neg_max = ctx.enter_context(nc.sbuf_tensor("neg_max" + tag, [P, REP * TB], F32))
    T.neg_max_bf = ctx.enter_context(nc.sbuf_tensor("neg_max_bf" + tag, [P, MAX_ROWS * REP * TB], BF16))
    T.max_rows = ctx.enter_context(nc.sbuf_tensor("max_rows" + tag, [MAX_ROWS * REP * TB, P], BF16))
    T.ps_s1 = ctx.enter_context(nc.psum_tensor("ps_s1" + tag, [P, 2, BANK], F32))
    T.order, T.at = S1
    return T


def stage1_block(i):
    quarter, k = divmod(i, S1_BLOCKS // QH ** 2)
    j, t = divmod(k, TB // QH)
    return j, quarter // QH * (TB // QH) + t, quarter % QH


def stage1_sync(sp, S, A, T):
    steps = Names()

    def load_q(g, cols, signal):
        m, r0 = g // 2, (g % 2) * REP * HD
        for i, part in enumerate(Q_PARTS):
            src = A.q_dram[part, m, r0:r0 + REP * HD, cols].rearrange("(j d) t -> d j t", j=REP)
            sp.dma_start(T.q6[g % QK_SLOTS][i * HD:(i + 1) * HD, :, cols], src).then_inc(signal, 16)

    def load_k(g, cols, signal):
        for first, count in K_RUNS:
            rows = slice(first * HD, (first + count) * HD)
            sp.dma_start(T.k6[g % QK_SLOTS][rows, cols], A.k_dram[0:count, g * HD:(g + 1) * HD, cols],
                         ).then_inc(signal, 16)

    def load_group0(step):
        if step == 0:
            load_q(0, slice(0, BANK), S.g0_load[0])
            load_k(0, slice(0, BANK), S.g0_load[0])
        elif step == 1:
            load_k(0, slice(BANK, SEQ), S.g0_load[1])
        else:
            load_q(0, slice(BANK, SEQ), S.g0_load[2])

    def load_qk(g):
        slot = g % QK_SLOTS
        if g >= QK_SLOTS:
            sp.wait_ge(S.s2, GROUP_ITEMS * (g - QK_SLOTS + 1))
        load_q(g, slice(0, SEQ), S.qk_load[slot])
        load_k(g, slice(0, SEQ), S.qk_load[slot])

    def place_max(g):
        sp.wait_ge(S.mrow, g + 1)
        sp.dma_start(A.max_dram.rearrange("r (a t) -> (r a) t", t=P), T.max_rows[:]).then_inc(S.mrow_st, 16)
        sp.wait_ge(S.mrow_st, 16 * (g + 1))
        sp.dma_start(T.q6[g % QK_SLOTS][PART_ROWS:SCORE_ROWS].rearrange("r j t -> r (j t)"),
                     A.max_dram).then_inc(S.mrow_ld, 16)

    steps.load_group0, steps.load_qk, steps.place_max = load_group0, load_qk, place_max
    return steps


def stage1_vector(dve, S, T, link):
    def stage1_max(use, g, i):
        dve.wait_ge(S.s1, use + 1)
        j, t, half = stage1_block(i)
        column = (j * TB + t) * QH + half
        dve.tensor_reduce(T.half_max[:, g % 2, column:column + 1], T.ps_s1[:, use % 2, :], AX,
                          ALU.max).then_inc(S.s1_read, 1)

    def negate(g):
        dve.wait_ge(S.s1_read, (g + 1) * S1_BLOCKS)
        link(dve.tensor_reduce(T.neg_max[:], T.half_max[:, g % 2, :].rearrange("p (a h) -> p a h", h=QH), AX,
                               ALU.max, negate=True))
        link(dve.tensor_copy(T.neg_max_bf[:, 0:REP * TB], T.neg_max[:]))
        dve.tensor_tensor(T.neg_max_bf[:, REP * TB:], T.neg_max[:], T.neg_max_bf[:, 0:REP * TB],
                          ALU.subtract).then_inc(S.negmax, 1)

    def copy_max_rows(use, g):
        dve.wait_ge(S.s1, use + 1)
        if g >= 1:
            dve.wait_ge(S.mrow_st, 16 * g)
        dve.tensor_copy(T.max_rows[:], T.ps_s1[:, use % 2, :].bitcast(BF16)[0:MAX_ROWS * REP * TB, 0:P],
                        ).then_inc(S.mrow, 1)

    def run(use, kind, g, i):
        if kind == "max":
            copy_max_rows(use, g)
            return
        stage1_max(use, g, i)
        if i == S1_BLOCKS - 1:
            negate(g)

    return run


def stage1_tensor(pe, S, M, T):
    def run(use, kind, g, i):
        if use >= 2:
            last_kind, last_g, _, blocks = T.order[use - 2]
            if last_kind == "max":
                pe.wait_ge(S.mrow, last_g + 1)
            else:
                pe.wait_ge(S.s1_read, blocks)
        bank, slot = T.ps_s1[:, use % 2, :], g % QK_SLOTS
        if kind == "max":
            pe.wait_ge(S.negmax, g + 1)
            pe.transpose(bank.bitcast(BF16)[0:MAX_ROWS * REP * TB, 0:P], T.neg_max_bf[:],
                         M.ident_bf[:]).then_inc(S.s1, 1)
            return
        if g == 0 and i % (S1_BLOCKS // QH ** 2) == 0 and i < S1_BLOCKS * 3 // 4:
            quarter = i // (S1_BLOCKS // QH ** 2)
            pe.wait_ge(S.g0_load[quarter], (QK_LOADS, 16 * len(K_RUNS), 16 * len(Q_PARTS))[quarter])
        elif g > 0 and i == 0:
            pe.wait_ge(S.qk_load[slot], QK_LOADS * (g // QK_SLOTS + (slot > 0)))
        j, t, half = stage1_block(i)
        pe.matmul(bank, T.q6[slot][0:PART_ROWS, j, t * P:(t + 1) * P],
                  T.k6[slot][0:PART_ROWS, half * BANK:(half + 1) * BANK], start=True, stop=True).then_inc(S.s1, 1)

    return run


WHOLE = slice(0, SEQ)
FIRST_HALF, SECOND_HALF = slice(0, SEQ // 2), slice(SEQ // 2, SEQ)


def output_sync(sp, S, A, M, first_token):
    steps = Names()

    def spread_sums(g, queries, n):
        count = REP * (queries.stop - queries.start)
        sp.dma_start(A.sum_dram[0:count].rearrange("(j t) -> j t", j=REP), M.o[0:P:VW, g % 2, queries],
                     ).then_inc(S.sum_st, 16)
        sp.wait_ge(S.sum_st, 16 * (n + 1))
        sp.dma_start(M.sums[:, 0:count // P], A.sum_dram[0:count].rearrange("(p n) -> p n", p=P)).then_inc(S.sum_ld, 16)

    def place_reciprocals(queries, n):
        width = queries.stop - queries.start
        sp.wait_ge(S.rec, n + 1)
        sp.dma_start(A.rec_dram[0:REP * width].rearrange("(p n) -> p n", p=P), M.rec[:, 0:REP * width // P],
                     ).then_inc(S.rec_st, 16)
        sp.wait_ge(S.rec_st, 16 * (n + 1))
        if n >= 1:
            sp.wait_ge(S.on, n)
        for j in range(REP):
            sp.dma_start(M.rec_rows[j * VW:(j + 1) * VW, queries],
                         A.rec_dram[j * width:(j + 1) * width].partition_broadcast(VW)).then_inc(S.rec_ld, 16)

    def place_outputs(g, queries, n):
        sp.wait_ge(S.on, n + 1)
        for j in range(REP):
            row = (g * REP + j) * HD
            sp.dma_start(A.attn_dram[row:row + HD, bass.ds(first_token + queries.start, queries.stop - queries.start)],
                         M.on[j * VW + 1:j * VW + 1 + HD, queries]).then_inc(S.at, 16)

    steps.spread_sums, steps.place_reciprocals, steps.place_outputs = spread_sums, place_reciprocals, place_outputs
    return steps


def normalise_outputs(pool, S, M, g, queries, n):
    pool.wait_ge(S.rec_ld, 16 * REP * (n + 1))
    if n >= 1:
        pool.wait_ge(S.at, 16 * REP * n)
    pool.tensor_tensor(M.on[:, queries], M.o[:, g % 2, queries], M.rec_rows[:, queries], ALU.mult).then_inc(S.on, 1)


def reciprocals(dve, S, M, queries, n):
    columns = REP * (queries.stop - queries.start) // P
    dve.wait_ge(S.sum_ld, 16 * (n + 1))
    if n >= 1:
        dve.wait_ge(S.rec_st, 16 * n)
    dve.reciprocal(M.rec[:, 0:columns], M.sums[:, 0:columns]).then_inc(S.rec, 1)


def output_round(x):
    if x % GROUP_ITEMS == 0 and x > 0:
        return x // GROUP_ITEMS - 1, WHOLE
    if x == ITEMS - SEG_ITEMS:
        return KV_HEADS - 1, FIRST_HALF
    return None


def project(nc, S, M, A, T, b, tag, with_tail):
    with ExitStack() as ctx:
        def sb(name, shape, dt=F32):
            return ctx.enter_context(nc.sbuf_tensor(name + tag, shape, dt))

        def ps(name, shape, dt=F32):
            return ctx.enter_context(nc.psum_tensor(name + tag, shape, dt))

        x_f = sb("x_f", [P, SEQ])
        hot = sb("hot", [P, SEQ], BF16)
        h = sb("h", [P, TB, D])
        stats = sb("p_stats", [P, TB, 6])
        mv = sb("p_mv", [P, TB, 2])
        veps = sb("p_veps", [P, TB])
        rstd = sb("p_rstd_sb", [P, TB])
        xn = sb("xn", [P, 2, D])
        x_t = sb("x_t", [P, DC, SEQ])
        r1 = sb("r1", [P, 2, BANK])
        parts = sb("parts", [P, 2, 3, BANK], BF16)
        ps_d = T.ps_s1
        ps_t = ps("ps_t", [P, 2, BANK])
        ps_v = ps("ps_v", [P, BANK])
        ps_q = ps("ps_q", [P, 2, BANK])
        block = ctx.enter_context(nc.Block())
        qk_items = [(0, 0), (0, HC), (0, 1), (0, 2), (1, HC), (1, 0), (0, 3), (1, 1), (1, 2), (1, 3)]
        LOAD_AFTER = (1, 4, 5)
        first_tile = TB // QH
        beside_tiles = TB + 1 - first_tile

        first_mixed = LOAD_AFTER[1] + 1
        stage1_uses = T.at[-1]
        mixed = {2 * n + 1: (first_mixed + n // DC, n % DC) for n in range(DC * (len(qk_items) - first_mixed))}

        @block.sync
        def _(sp):
            tail = output_sync(sp, S, A, M, b * SEQ - SEQ)
            sp.dma_start(x_f[:], A.rows_dram[bass.ds(b * SEQ, SEQ)].partition_broadcast(P)).then_inc(S.x_row, 16)
            if with_tail:
                tail.spread_sums(KV_HEADS - 1, SECOND_HALF, 0)
            for t in range(TB):
                sp.wait_ge(S.h0, t + 1)
                sp.dma_start(A.h_dram[bass.ds(b * SEQ + t * P, P), :], h[:, t, :]).then_inc(S.h0_stored, 16)
                if with_tail and t == 0:
                    tail.place_reciprocals(SECOND_HALF, 0)
                if with_tail and t == TB - 1:
                    tail.place_outputs(KV_HEADS - 1, SECOND_HALF, 0)
            stage1 = stage1_sync(sp, S, A, T)
            for n, (half, m) in enumerate(qk_items):
                sp.wait_ge(S.qk_lo, n + 1)
                cols = slice(half * BANK, (half + 1) * BANK)
                dst = A.q_dram[:, m, :, cols] if m < HC else A.k_dram[:, :, cols]
                sp.dma_start(dst.rearrange("s p t -> p s t"), parts[:, n % 2]).then_inc(S.part_st[n % 2], 16)
                if n in LOAD_AFTER:
                    for i in range(2):
                        sp.wait_ge(S.part_st[i], (n + 2 - i) // 2 * 16)
                    stage1.load_group0(LOAD_AFTER.index(n))
            stage1.load_qk(1)
            stage1.place_max(0)
            sp.wait_ge(S.h0_stored, TB * 16)
            for i in range(2):
                sp.wait_ge(S.part_st[i], len(qk_items) // 2 * 16)
            if with_tail:
                sp.wait_ge(S.at, 16 * REP)
            sp.wait_ge(S.mrow_ld, 16)

        @block.gpsimd
        def _(pool):
            pool.tensor_copy(M.idx_b[:], M.idx_all[:, bass.ds(b * TB, TB)]).then_inc(S.idx, 1)
            pool.wait_ge(S.idx, 1)
            for t in range(TB):
                pool.indirect_dma_start(out=h[:, t, :], out_offset=None, in_=A.W,
                                        in_offset=bass.IndirectOffsetOnAxis(ap=M.idx_b[:, t:t + 1], axis=0),
                                        ).then_inc(S.gather[t], 16)
            pool.memset(M.v[:], 0.0).then_inc(S.v_const, 1)
            pool.wait_ge(S.v_const, 1)
            pool.memset(M.v[:, :, :, 0:1], 1.0).then_inc(S.v_const, 1)
            def low_part(n):
                pool.wait_ge(S.qk_mid, n + 1)
                if n >= 2:
                    pool.wait_ge(S.part_st[n % 2], n // 2 * 16)
                pool.tensor_tensor(parts[:, n % 2, 2, :], r1[:, n % 2, :], parts[:, n % 2, 1, :],
                                   ALU.subtract).then_inc(S.qk_lo, 1)

            for t in range(TB):
                pool.wait_ge(S.p_var, t + 1)
                pool.tensor_tensor(rstd[:, t:t + 1], veps[:, t:t + 1], M.neg_half[:], ALU.pow).then_inc(S.p_rstd, 1)
                if with_tail and t == TB - 2:
                    normalise_outputs(pool, S, M, KV_HEADS - 1, SECOND_HALF, 0)
                if t >= first_tile + 2:
                    low_part(t - first_tile - 2)
            for n in range(beside_tiles - 3, len(qk_items)):
                low_part(n)
            pool.wait_ge(S.qk_lo, len(qk_items))
            for slot in range(QK_SLOTS):
                pool.memset(T.k6[slot][PART_ROWS:SCORE_ROWS, :], 1.0).then_inc(S.ones, 1)

        @block.vector
        def _(dve):
            n = [0]

            def link(ins):
                n[0] += 1
                ins.then_inc(S.p_vec, 1)
                dve.wait_ge(S.p_vec, n[0])

            dve.wait_ge(S.x_row, 16)
            dve.tensor_scalar(hot[:], x_f[:], M.tok[:], None, ALU.is_equal).then_inc(S.hot, 1)

            def embed(t):
                dve.wait_ge(S.gather[t], b * 16 + 16)
                dve.wait_ge(S.delta, t + 1)
                dve.tensor_tensor(h[:, t, :], h[:, t, :], ps_d[:, t % 2, :], ALU.add).then_inc(S.h0, 1)
                dve.wait_ge(S.h0, t + 1)
                link(dve.bn_stats(stats[:, t, :], h[:, t, :]))
                link(dve.bn_aggr(mv[:, t, :], stats[:, t, :]))
                dve.tensor_scalar(veps[:, t:t + 1], mv[:, t, 1:2], EPS, None, ALU.add).then_inc(S.p_var, 1)

            def normalise(t):
                dve.wait_ge(S.p_rstd, t + 1)
                if t >= 2:
                    dve.wait_ge(S.x_tr, t - 1)
                dve.tensor_scalar(xn[:, t % 2, :], h[:, t, :], mv[:, t, 0:1], rstd[:, t:t + 1],
                                  ALU.subtract, ALU.mult).then_inc(S.p_norm, 1)

            def remainder(i):
                scale = HD ** -0.5 if qk_items[i][1] < HC else 1.0
                dve.wait_ge(S.qk_hi, i + 1)
                if i >= 2:
                    dve.wait_ge(S.qk_lo, i - 1)
                dve.scalar_tensor_tensor(out=r1[:, i % 2, :], in0=ps_q[:, i % 2, :], scalar=scale,
                                         in1=parts[:, i % 2, 0, :], op0=ALU.mult,
                                         op1=ALU.subtract).then_inc(S.qk_r1, 1)

            embed(0)
            embed(1)
            for t in range(TB + 1):
                if t < TB:
                    normalise(t)
                if t + 2 < TB:
                    embed(t + 2)
                if with_tail and t == 0:
                    reciprocals(dve, S, M, SECOND_HALF, 0)
                if t >= first_tile + 2:
                    remainder(t - first_tile - 2)
            for i in range(beside_tiles - 2, first_mixed):
                remainder(i)
            stage1 = stage1_vector(dve, S, T, link)
            for x, use in enumerate(stage1_uses):
                stage1(*use)
                i, c = mixed.get(x - 2, (0, 0))
                if c == DC - 1:
                    remainder(i)

        @block.scalar
        def _(act):
            def copy_x_t(t):
                act.wait_ge(S.x_tr, t + 1)
                act.activation(x_t[:, :, t * P:(t + 1) * P],
                               ps_t[:, t % 2, :].rearrange("p (c t) -> p c t", c=DC), ACT.Copy).then_inc(S.x_t, 1)

            def copy_v(t):
                act.wait_ge(S.v_ps, t + 1)
                if t == 0:
                    act.wait_ge(S.v_const, 2)
                act.activation(M.v[:, t, :, 1:1 + HD],
                               ps_v[:, 0:KV_HEADS * HD].rearrange("p (g d) -> p g d", g=KV_HEADS),
                               ACT.Copy).then_inc(S.v_sb, 1)

            def split(i):
                scale = HD ** -0.5 if qk_items[i][1] < HC else 1.0
                act.wait_ge(S.qk_ps, i + 1)
                if i >= 2:
                    act.wait_ge(S.part_st[i % 2], i // 2 * 16)
                act.activation(parts[:, i % 2, 0, :], ps_q[:, i % 2, :], ACT.Copy, scale=scale).then_inc(S.qk_hi, 1)
                act.wait_ge(S.qk_r1, i + 1)
                act.activation(parts[:, i % 2, 1, :], r1[:, i % 2, :], ACT.Copy).then_inc(S.qk_mid, 1)

            for t in range(TB + 1):
                if t < TB:
                    copy_x_t(t)
                if t >= 1:
                    copy_v(t - 1)
                if t > first_tile:
                    split(t - first_tile - 1)
            for i in range(beside_tiles - 1, len(qk_items)):
                split(i)

        @block.tensor
        def _(pe):
            def add_delta(t):
                if t >= 2:
                    pe.wait_ge(S.h0, t - 1)
                pe.matmul(ps_d[:, t % 2, :], hot[:, t * P:(t + 1) * P], M.d_hm[:], start=True, stop=False)
                pe.matmul(ps_d[:, t % 2, :], hot[:, t * P:(t + 1) * P], M.d_lo[:], start=False,
                          stop=True).then_inc(S.delta, 1)

            def transposes(t):
                pe.wait_ge(S.p_norm, t + 1)
                if t >= 2:
                    pe.wait_ge(S.x_t, t - 1)
                for c in range(DC):
                    last = pe.transpose(ps_t[:, t % 2, c * P:(c + 1) * P], xn[:, t % 2, c * P:(c + 1) * P],
                                        M.ident[:])
                last.then_inc(S.x_tr, 1)

            def values(t):
                pe.wait_ge(S.x_t, t + 1)
                if t >= 1:
                    pe.wait_ge(S.v_sb, t)
                for c in range(DC):
                    last = pe.matmul(ps_v[:, 0:KV_HEADS * HD], x_t[:, c, t * P:(t + 1) * P], M.wv[:, c, :],
                                     start=(c == 0), stop=(c == DC - 1))
                last.then_inc(S.v_ps, 1)

            def queries_keys(i, chunks=range(DC)):
                half, m = qk_items[i]
                w = M.wq[:, :, m * P:(m + 1) * P] if m < HC else M.wk[:]
                for c in chunks:
                    if c == 0 and i >= 2:
                        pe.wait_ge(S.qk_r1, i - 1)
                    last = pe.matmul(ps_q[:, i % 2, :], w[:, c, :], x_t[:, c, half * BANK:(half + 1) * BANK],
                                     start=(c == 0), stop=(c == DC - 1), skip_group_check=True)
                    if c == DC - 1:
                        last.then_inc(S.qk_ps, 1)

            pe.wait_ge(S.hot, 1)
            add_delta(0)
            add_delta(1)
            for t in range(TB + 1):
                if t + 2 < TB:
                    add_delta(t + 2)
                if t < TB:
                    transposes(t)
                if t >= 1:
                    values(t - 1)
                if t >= first_tile:
                    queries_keys(t - first_tile)
            for i in range(beside_tiles, first_mixed):
                queries_keys(i)
            stage1 = stage1_tensor(pe, S, M, T)
            for x, use in enumerate(stage1_uses):
                stage1(*use)
                if x in mixed:
                    i, c = mixed[x]
                    queries_keys(i, [c])


def attend(nc, S, W, M, A, T, b, tag, with_ffn):
    with ExitStack() as ctx:
        def sb(name, shape, dt=F32):
            return ctx.enter_context(nc.sbuf_tensor(name + tag, shape, dt))

        def ps(name, shape, dt=F32):
            return ctx.enter_context(nc.psum_tensor(name + tag, shape, dt))

        probs = sb("probs", [P, 2, REP, BANK])
        ps_s2 = ps("ps_s2", [P, 2, 2, BANK])
        ps_o = ps("ps_o", [P, BANK])
        F, Q = None, None
        earlier = 1 if with_ffn else 0
        if with_ffn:
            banks = ps("ffn_banks", [P, 1, BANK])
            order = [use[:3] for x in range(ITEMS) for use in ffn_uses_at(x) if use[3] == 0]
            F = ffn_memory(sb, banks, plan_banks(order, {kind: (0,) for kind in ("wo", "xt", "u", "yt", "f2")}),
                           slots=FFN_SLOTS_BESIDE)
        else:
            Q = weight_memory(sb)
        block = ctx.enter_context(nc.Block())

        def outputs_at(x, at):
            found = output_round(x - at)
            return [found + (earlier + found[0],)] if found else []

        def beside(schedule, x):
            return [t for t in range(TB) if x == schedule + FFN_PERIOD * t] if with_ffn else []

        @block.sync
        def _(sp):
            stage1 = stage1_sync(sp, S, A, T)
            outputs = output_sync(sp, S, A, M, b * SEQ)
            if with_ffn:
                ffn = ffn_sync(sp, S, A, F, b * SEQ - SEQ)
            if with_ffn:
                ffn.load(0)
            else:
                load_weight = weights_sync(sp, W, A, Q)
                load_weight(0)
                sp.dma_start(M.wo[:], rows_of(A.wo)).then_inc(W.late_w, 16)
                for dst, src in ((M.b1, A.b1), (M.ln_g, A.ln_g), (M.ln_b, A.ln_b), (M.b2, A.b2)):
                    sp.dma_start(dst[:], src.partition_broadcast(P)).then_inc(W.late_w, 16)
            for x in range(ITEMS):
                g, y = x // GROUP_ITEMS, x % GROUP_ITEMS
                if y == 1 and g + 2 < KV_HEADS:
                    stage1.load_qk(g + 2)
                for done, queries, rounds in outputs_at(x, 3):
                    sp.wait_ge(S.o, QH * done + queries.stop // BANK)
                    outputs.spread_sums(done, queries, rounds)
                for _, queries, rounds in outputs_at(x, 7):
                    outputs.place_reciprocals(queries, rounds)
                for done, queries, rounds in outputs_at(x, 12):
                    outputs.place_outputs(done, queries, rounds)
                if not with_ffn and x == WEIGHT_START + AT_W_CLIP + WEIGHT_STEP * WEIGHT_CHUNKS:
                    load_weight(1)
                for t in beside(AT_LOAD, x):
                    ffn.load(t)
                for t in beside(AT_FINISH, x):
                    ffn.store(t)
                for _, kind, group, _ in T.at.get(x, ()):
                    if kind == "max":
                        stage1.place_max(group)
            sp.wait_ge(S.at, 16 * REP * (KV_HEADS + earlier))
            if with_ffn:
                ffn.wait_stores()
            else:
                sp.wait_ge(W.late_w, 5 * 16)

        @block.gpsimd
        def _(pool):
            if with_ffn:
                ffn = ffn_gpsimd(pool, S, M, F)
            else:
                weights = weights_gpsimd(pool, W, Q)
            for x in range(ITEMS):
                if not with_ffn:
                    for w, _ in weights_at(x, AT_W_ABS + WEIGHT_STEP * WEIGHT_CHUNKS, count=1):
                        weights.total(w)
                    for w, c in weights_at(x, AT_W_ROUND):
                        weights.round_chunk(w, c)
                for done, queries, rounds in outputs_at(x, 10):
                    normalise_outputs(pool, S, M, done, queries, rounds)
                for t in beside(AT_STATS, x):
                    ffn.rstd_h1(t)
                for t in beside(AT_SQUARE_X2, x):
                    ffn.rms_x2(t)
                for t in beside(AT_NORM + 2, x):
                    ffn.add_b2(t)
                for t in beside(AT_SILU, x):
                    ffn.silu(t)
                for t in beside(AT_STATS_G + UC, x):
                    ffn.scale_g(t)
                for t in beside(AT_SQUARE_Y, x):
                    ffn.rms_y(t)

        @block.vector
        def _(dve):
            n = [0]

            def link(ins):
                n[0] += 1
                ins.then_inc(S.a_vec, 1)
                dve.wait_ge(S.a_vec, n[0])

            stage1 = stage1_vector(dve, S, T, link)
            if with_ffn:
                ffn = ffn_vector(dve, S, M, F, link)
            else:
                weights = weights_vector(dve, W, M, Q, link)
            for x in range(ITEMS):
                for use in T.at.get(x, ()):
                    stage1(*use)
                for _, queries, rounds in outputs_at(x, 6):
                    reciprocals(dve, S, M, queries, rounds)
                if not with_ffn:
                    for w, c in weights_at(x, AT_W_ABS):
                        weights.abs_chunk(w, c)
                    for w, _ in weights_at(x, AT_W_MEAN, count=1):
                        weights.mean(w)
                    for w, c in weights_at(x, AT_W_CLIP):
                        weights.clip_chunk(w, c)
                for t in beside(AT_RESIDUAL, x):
                    ffn.residual(t)
                for t in beside(AT_STATS, x):
                    ffn.stats_h1(t)
                for t in beside(AT_NORM, x):
                    ffn.norm_x2(t)
                for t in beside(AT_NORM + 1, x):
                    ffn.max_x2(t)
                for t in beside(AT_QUANT_X, x):
                    ffn.scale_x2(t)
                for t in beside(AT_QUANT_X + 1, x):
                    ffn.quantise_x2(t)
                for c in range(UC):
                    for t in beside(AT_U + 2 * c + 1, x):
                        ffn.dequantise_u(t, c)
                    for t in beside(AT_STATS_G + c, x):
                        ffn.stats_g(t, c)
                    for t in beside(AT_MAX_Y + c, x):
                        ffn.max_y(t, c)
                for t in beside(AT_STATS_G + UC, x):
                    ffn.variance_g(t)
                for t in beside(AT_SCALE_Y, x):
                    ffn.scale_y(t)
                for t in beside(AT_QUANT_Y, x):
                    ffn.quantise_y(t)
                for t in beside(AT_FINISH, x):
                    ffn.finish(t)

        @block.scalar
        def _(act):
            def outputs(seg):
                g, half = seg // QH, seg % QH
                act.wait_ge(S.pv, TB * (seg + 1))
                if g >= 2:
                    act.wait_ge(S.on, g - 1 + earlier)
                act.activation(M.o[:, g % 2, half * BANK:(half + 1) * BANK], ps_o[:], ACT.Copy).then_inc(S.o, 1)

            def exponentials(x):
                tile, pair = x // 2, x % 2
                if tile >= 2 and pair == 0:
                    act.wait_ge(S.pv, tile - 1)
                act.wait_ge(S.s2, x + 1)
                act.activation(probs[:, tile % 2, 2 * pair:2 * pair + 2, :], ps_s2[:, x % 2, :, :],
                               ACT.Exp).then_inc(S.exp, 1)

            if with_ffn:
                ffn = ffn_scalar(act, S, M, F)
            for x in range(ITEMS):
                exponentials(x)
                for t in beside(AT_SQUARE_X2, x):
                    ffn.square_x2(t)
                for t in beside(AT_XT + 1, x):
                    ffn.copy_xq_t(t)
                for t in beside(AT_TANH, x):
                    ffn.tanh(t)
                for t in beside(AT_GELU, x):
                    ffn.gelu(t)
                for t in beside(AT_SQUARE_Y, x):
                    ffn.square_y(t)
                for t in beside(AT_ROUND_Y, x):
                    ffn.round_y(t)
                for half in range(2):
                    for t in beside(AT_YT + 2 * half + 1, x):
                        ffn.copy_yq_t(t, half)
                if x >= SEG_ITEMS and x % SEG_ITEMS == 1:
                    outputs(x // SEG_ITEMS - 1)
            outputs(KV_HEADS * QH - 1)

        @block.tensor
        def _(pe):
            stage1 = stage1_tensor(pe, S, M, T)

            def stage2(x):
                g, half, kt, pair = x // GROUP_ITEMS, x // SEG_ITEMS % QH, x // 2 % TB, x % 2
                if x % GROUP_ITEMS == 0:
                    pe.wait_ge(S.mrow_ld, 16 * (g + 1))
                if x >= 2:
                    pe.wait_ge(S.exp, x - 1)
                slot = g % QK_SLOTS
                for i in range(2):
                    last = pe.matmul(ps_s2[:, x % 2, i, :], T.k6[slot][:, kt * P:(kt + 1) * P],
                                     T.q6[slot][:, 2 * pair + i, half * BANK:(half + 1) * BANK],
                                     start=True, stop=True)
                last.then_inc(S.s2, 1)

            def weigh(tile):
                g, kt = tile // TB // QH, tile % TB
                pe.wait_ge(S.exp, 2 * (tile + 1))
                if kt == 0 and tile >= TB:
                    pe.wait_ge(S.o, tile // TB)
                for j in range(REP):
                    last = pe.matmul(ps_o[j * VW:(j + 1) * VW, :], M.v[:, kt, g, :], probs[:, tile % 2, j, :],
                                     start=(kt == 0), stop=(kt == TB - 1), skip_group_check=True)
                last.then_inc(S.pv, 1)

            if with_ffn:
                ffn = ffn_tensor(pe, S, M, F)
            pe.wait_ge(S.ones, QK_SLOTS)
            for x in range(ITEMS):
                uses = T.at.get(x, ())
                for use in uses[:1]:
                    stage1(*use)
                stage2(x)
                for use in uses[1:]:
                    stage1(*use)
                if with_ffn:
                    for piece in ffn_uses_at(x):
                        ffn.run(*piece)
                if x % 2 == 1 and x > 1:
                    weigh(x // 2 - 1)
            weigh(ITEMS // 2 - 1)


FFN_PERIOD = 26
AT_LOAD = -18
AT_WO = 0
AT_RESIDUAL = 7
AT_STATS = 8
AT_NORM = 10
AT_SQUARE_X2 = 11
AT_QUANT_X = 13
AT_XT = 16
AT_U = 18
AT_TANH = 25
AT_SILU = 27
AT_GELU = 31
AT_STATS_G = 35
AT_MAX_Y = 47
AT_SQUARE_Y = 47
AT_SCALE_Y = 51
AT_ROUND_Y = 53
AT_QUANT_Y = 55
AT_YT = 60
AT_F2 = 64
AT_FINISH = 67
FFN_SLOTS_BESIDE = dict(h1=4, at=2, x2=1, xq=1, u=2, yq=1)
FFN_SLOTS_ALONE = dict(h1=8, at=3, x2=3, xq=2, u=5, yq=2)


def ffn_share(x):
    y = x % FFN_PERIOD
    if y == (AT_GELU + 2) % FFN_PERIOD:
        return 5
    return 1.7


def ffn_uses_at(x):
    pieces = []
    for t in range(TB):
        at = x - FFN_PERIOD * t
        if at - AT_WO in range(0, 2 * HC, 2):
            pieces.append(("wo", t, 0, (at - AT_WO) // 2))
        if at == AT_XT:
            pieces.append(("xt", t, 0, 0))
        if at - AT_U in range(0, 2 * UC, 2):
            pieces.append(("u", t, (at - AT_U) // 2, 0))
        if at - AT_YT in (0, 2):
            pieces.append(("yt", t, (at - AT_YT) // 2, 0))
        if at - AT_F2 in (0, 2):
            pieces.append(("f2", t, 0, (at - AT_F2) // 2))
    return pieces


def plan_banks(order, rings):
    bank, before, last, count = {}, {}, {}, {}
    for use in order:
        ring = rings[use[0]]
        k = ring[count.get(use[0], 0) % len(ring)]
        count[use[0]] = count.get(use[0], 0) + 1
        bank[use], before[use], last[k] = k, last.get(k), use
    return bank, before


def read_of(S, use):
    kind, t, n = use
    return {"wo": (S.h1, t + 1), "xt": (S.xq_t, t + 1), "u": (S.u, t * UC + n + 1),
            "yt": (S.yq_t, 2 * t + n + 1), "f2": (S.f_o, t + 1)}[kind]


def ffn_memory(sb, banks, plan, slots):
    F = Names()
    F.slots, F.banks = slots, banks
    F.bank, F.before = plan
    F.h1 = sb("h1", [P, slots["h1"], D])
    F.at = sb("at", [P, slots["at"], HC, P])
    F.x2 = sb("x2", [P, slots["x2"], D])
    F.xq = sb("xq", [P, slots["xq"], D], BF16)
    F.xq_t = sb("xq_t", [P, slots["xq"], D], BF16)
    F.u = sb("u", [P, slots["u"], INNER])
    F.th = sb("th", [P, INNER])
    F.yq = sb("yq", [P, slots["yq"], INNER], BF16)
    F.yq_t = sb("yq_t", [P, slots["yq"], INNER], BF16)
    F.fo = sb("fo", [P, 2, D])
    F.st = sb("f_st", [P, TB, 6])
    F.mv = sb("f_mv", [P, TB, 2])
    F.gst = sb("f_gst", [P, TB, UC * 6])
    F.gmv = sb("f_gmv", [P, TB, 2])
    F.yc = sb("f_yc", [P, TB, UC])
    F.veps, F.r0, F.ss, F.mx = (sb("c_" + n, [P, TB]) for n in ("veps", "r0", "ss", "mx"))
    F.ms, F.r1, F.am, F.rc = (sb("c_" + n, [P, TB]) for n in ("ms", "r1", "am", "rc"))
    F.qs, F.a1, F.gveps, F.gr = (sb("c_" + n, [P, TB]) for n in ("qs", "a1", "gveps", "gr"))
    F.gnm = sb("c_gnm", [P, TB])
    F.yss, F.ymx, F.yms, F.yr = (sb("c_" + n, [P, TB]) for n in ("yss", "ymx", "yms", "yr"))
    F.yam, F.yrc, F.yqs, F.a2 = (sb("c_" + n, [P, TB]) for n in ("yam", "yrc", "yqs", "a2"))
    return F


def col(c, t):
    return c[:, t:t + 1]


def ffn_sync(sp, S, A, F, first_token):
    steps = Names()

    def load(t):
        hs, ats = F.slots["h1"], F.slots["at"]
        if t >= hs:
            sp.wait_ge(S.f_o, t - hs + 1)
        sp.dma_start(F.h1[:, t % hs, :], A.h_dram[bass.ds(first_token + t * P, P), :]).then_inc(S.f_h[t], 16)
        if t >= ats:
            sp.wait_ge(S.wo, t - ats + 1)
        sp.dma_start(F.at[:, t % ats], A.attn_dram[:, bass.ds(first_token + t * P, P)].rearrange(
            "(c p) t -> p c t", p=P)).then_inc(S.f_h[t], 16)

    def store(t):
        sp.wait_ge(S.f_o, t + 1)
        sp.dma_start(A.out[bass.ds(first_token + t * P, P), :], F.fo[:, t % 2, :]).then_inc(S.out_st[t % 4], 16)

    def wait_stores():
        for i in range(4):
            sp.wait_ge(S.out_st[i], TB // 4 * 16)

    steps.load, steps.store, steps.wait_stores = load, store, wait_stores
    return steps


def ffn_gpsimd(pool, S, M, F):
    steps = Names()
    n = [0]

    def link(ins):
        n[0] += 1
        ins.then_inc(S.f_pool, 1)
        pool.wait_ge(S.f_pool, n[0])

    def rstd_h1(t):
        pool.wait_ge(S.f_var, t + 1)
        pool.tensor_tensor(col(F.r0, t), col(F.veps, t), M.neg_half[:], ALU.pow).then_inc(S.f_r0, 1)

    def rms_x2(t):
        pool.wait_ge(S.x2_ss, t + 1)
        link(pool.tensor_scalar(col(F.ms, t), col(F.ss, t), 1.0 / D, EPS, ALU.mult, ALU.add))
        pool.tensor_tensor(col(F.r1, t), col(F.ms, t), M.neg_half[:], ALU.pow).then_inc(S.x2_r, 1)

    def add_b2(t):
        h = F.h1[:, t % F.slots["h1"], :]
        pool.wait_ge(S.x2, t + 1)
        pool.tensor_tensor(h, h, M.b2[:], ALU.add).then_inc(S.h1_b2, 1)

    def silu(t):
        u = F.u[:, t % F.slots["u"], :]
        pool.wait_ge(S.tanh, t + 1)
        link(pool.tensor_scalar(F.th[:], F.th[:], 1.0, 1.0, ALU.add, ALU.mult))
        pool.tensor_tensor(u, u, F.th[:], ALU.mult).then_inc(S.silu, 1)

    def scale_g(t):
        u = F.u[:, t % F.slots["u"], :]
        pool.wait_ge(S.g_var, 2 * (t + 1))
        link(pool.tensor_tensor(col(F.gr, t), col(F.gveps, t), M.neg_half[:], ALU.pow))
        link(pool.tensor_scalar(u, u, col(F.gnm, t), col(F.gr, t), ALU.add, ALU.mult))
        link(pool.tensor_tensor(u, u, M.ln_g[:], ALU.mult))
        pool.tensor_tensor(u, u, M.ln_b[:], ALU.add).then_inc(S.y, 1)

    def rms_y(t):
        pool.wait_ge(S.y_ss, t + 1)
        link(pool.tensor_scalar(col(F.yms, t), col(F.yss, t), 1.0 / INNER, EPS, ALU.mult, ALU.add))
        pool.tensor_tensor(col(F.yr, t), col(F.yms, t), M.neg_half[:], ALU.pow).then_inc(S.y_r, 1)

    steps.rstd_h1, steps.rms_x2, steps.add_b2, steps.silu = rstd_h1, rms_x2, add_b2, silu
    steps.scale_g, steps.rms_y = scale_g, rms_y
    return steps


def ffn_vector(dve, S, M, F, link):
    steps = Names()
    hs, xs, qs, us, ys = (F.slots[k] for k in ("h1", "x2", "xq", "u", "yq"))

    def chunk(c):
        return slice(c * BANK, (c + 1) * BANK)

    def residual(t):
        dve.wait_ge(S.wo, t + 1)
        h = F.h1[:, t % hs, :]
        dve.tensor_tensor(h, F.banks[:, F.bank["wo", t, 0], :], h, ALU.add).then_inc(S.h1, 1)

    def stats_h1(t):
        dve.wait_ge(S.h1, t + 1)
        link(dve.bn_stats(F.st[:, t, :], F.h1[:, t % hs, :]))
        link(dve.bn_aggr(F.mv[:, t, :], F.st[:, t, :]))
        dve.tensor_scalar(col(F.veps, t), F.mv[:, t, 1:2], EPS, None, ALU.add).then_inc(S.f_var, 1)

    def norm_x2(t):
        dve.wait_ge(S.f_r0, t + 1)
        if t >= xs:
            dve.wait_ge(S.x2_ss, t - xs + 1)
        dve.tensor_scalar(F.x2[:, t % xs, :], F.h1[:, t % hs, :], F.mv[:, t, 0:1], col(F.r0, t),
                          ALU.subtract, ALU.mult).then_inc(S.x2, 1)

    def max_x2(t):
        dve.wait_ge(S.x2, t + 1)
        link(dve.tensor_reduce(col(F.mx, t), F.x2[:, t % xs, :], AX, ALU.max, apply_absolute_value=True))

    def scales(am, rc, qsc, a, mx, r, w, t):
        link(dve.tensor_scalar(col(am, t), col(mx, t), col(r, t), 1e-5, ALU.mult, ALU.max))
        link(dve.reciprocal(col(rc, t), col(am, t)))
        link(dve.tensor_scalar(col(a, t), col(am, t), M.w_dq[:, w:w + 1], None, ALU.mult))
        return dve.tensor_scalar(col(qsc, t), col(rc, t), 127.0, col(r, t), ALU.mult, ALU.mult)

    def scale_x2(t):
        dve.wait_ge(S.x2_r, t + 1)
        link(scales(F.am, F.rc, F.qs, F.a1, F.mx, F.r1, 0, t))

    def quantise_x2(t):
        x2 = F.x2[:, t % xs, :]
        link(dve.tensor_scalar(x2, x2, col(F.qs, t), ROUND, ALU.mult, ALU.add))
        dve.tensor_scalar(F.xq[:, t % qs, :], x2, ROUND, 127.0, ALU.subtract, ALU.min).then_inc(S.xq, 1)

    def dequantise_u(t, c):
        dve.wait_ge(S.u_ps, t * UC + c + 1)
        if t >= us and c == 0:
            dve.wait_ge(S.yq, t - us + 1)
        dve.scalar_tensor_tensor(out=F.u[:, t % us, chunk(c)], in0=F.banks[:, F.bank["u", t, c], :],
                                 scalar=col(F.a1, t), in1=M.b1[:, chunk(c)], op0=ALU.mult,
                                 op1=ALU.add).then_inc(S.u, 1)

    def silu(t):
        u = F.u[:, t % us, :]
        dve.wait_ge(S.tanh, t + 1)
        dve.scalar_tensor_tensor(out=u, in0=F.th[:], scalar=1.0, in1=u, op0=ALU.add,
                                 op1=ALU.mult).then_inc(S.silu, 1)

    def stats_g(t, c):
        dve.wait_ge(S.gelu, t + 1)
        dve.bn_stats(F.gst[:, t, 6 * c:6 * c + 6], F.u[:, t % us, chunk(c)]).then_inc(S.g_stats, 1)

    def variance_g(t):
        dve.wait_ge(S.g_stats, UC * (t + 1))
        link(dve.bn_aggr(F.gmv[:, t, :], F.gst[:, t, :]))
        dve.tensor_scalar(col(F.gnm, t), F.gmv[:, t, 0:1], -1.0, None, ALU.mult).then_inc(S.g_var, 1)
        dve.tensor_scalar(col(F.gveps, t), F.gmv[:, t, 1:2], EPS, None, ALU.add).then_inc(S.g_var, 1)

    def max_y(t, c):
        dve.wait_ge(S.y, t + 1)
        dve.tensor_reduce(F.yc[:, t, c:c + 1], F.u[:, t % us, chunk(c)], AX, ALU.max,
                          apply_absolute_value=True).then_inc(S.y_max, 1)

    def scale_y(t):
        dve.wait_ge(S.y_max, UC * (t + 1))
        link(dve.tensor_reduce(col(F.ymx, t), F.yc[:, t, :], AX, ALU.max))
        dve.wait_ge(S.y_r, t + 1)
        scales(F.yam, F.yrc, F.yqs, F.a2, F.ymx, F.yr, 1, t).then_inc(S.y_qs, 1)

    def quantise_y(t):
        dve.wait_ge(S.y_shift, t + 1)
        dve.tensor_scalar(F.yq[:, t % ys, :], F.u[:, t % us, :], ROUND, 127.0, ALU.subtract,
                          ALU.min).then_inc(S.yq, 1)

    def finish(t):
        dve.wait_ge(S.o_ps, t + 1)
        dve.wait_ge(S.h1_b2, t + 1)
        if t >= 2:
            dve.wait_ge(S.out_st[(t - 2) % 4], 16 * ((t - 2) // 4 + 1))
        dve.scalar_tensor_tensor(out=F.fo[:, t % 2, :], in0=F.banks[:, F.bank["f2", t, 0], :],
                                 scalar=col(F.a2, t), in1=F.h1[:, t % hs, :], op0=ALU.mult,
                                 op1=ALU.add).then_inc(S.f_o, 1)

    steps.residual, steps.stats_h1, steps.norm_x2, steps.max_x2 = residual, stats_h1, norm_x2, max_x2
    steps.scale_x2, steps.quantise_x2, steps.dequantise_u = scale_x2, quantise_x2, dequantise_u
    steps.silu, steps.stats_g, steps.variance_g, steps.max_y = silu, stats_g, variance_g, max_y
    steps.scale_y, steps.quantise_y, steps.finish = scale_y, quantise_y, finish
    return steps


def ffn_scalar(act, S, M, F):
    steps = Names()
    xs, qs, us, ys = (F.slots[k] for k in ("x2", "xq", "u", "yq"))

    def square_x2(t):
        act.wait_ge(S.x2, t + 1)
        if t >= qs:
            act.wait_ge(S.xq_tr, t - qs + 1)
        act.activation(F.xq[:, t % qs, :], F.x2[:, t % xs, :], ACT.Square, accum_out=col(F.ss, t)).then_inc(S.x2_ss, 1)

    def copy_xq_t(t):
        act.wait_ge(S.xq_tr, t + 1)
        if t >= qs:
            act.wait_ge(S.u_ps, UC * (t - qs + 1))
        act.activation(F.xq_t[:, t % qs, :], F.banks[:, F.bank["xt", t, 0], :].bitcast(BF16)[:, 0:D],
                       ACT.Copy).then_inc(S.xq_t, 1)

    def tanh(t):
        act.wait_ge(S.u, UC * (t + 1))
        if t >= 1:
            act.wait_ge(S.silu, t)
        act.activation(F.th[:], F.u[:, t % us, :], ACT.Tanh, scale=0.5).then_inc(S.tanh, 1)

    def gelu(t):
        u = F.u[:, t % us, :]
        act.wait_ge(S.silu, t + 1)
        act.activation(u, u, ACT.Gelu, scale=0.5).then_inc(S.gelu, 1)

    def square_y(t):
        act.wait_ge(S.y, t + 1)
        if t >= ys:
            act.wait_ge(S.yq_tr, 2 * (t - ys + 1))
        act.activation(F.yq[:, t % ys, :], F.u[:, t % us, :], ACT.Square, accum_out=col(F.yss, t)).then_inc(S.y_ss, 1)

    def round_y(t):
        u = F.u[:, t % us, :]
        act.wait_ge(S.y_qs, t + 1)
        act.activation(u, u, ACT.Identity, bias=M.round_c[:], scale=col(F.yqs, t)).then_inc(S.y_shift, 1)

    def copy_yq_t(t, half):
        act.wait_ge(S.yq_tr, 2 * t + half + 1)
        if t >= ys and half == 0:
            act.wait_ge(S.o_ps, t - ys + 1)
        act.activation(F.yq_t[:, t % ys, half * 2 * BANK:(half + 1) * 2 * BANK],
                       F.banks[:, F.bank["yt", t, half], :].bitcast(BF16), ACT.Copy).then_inc(S.yq_t, 1)

    steps.square_x2, steps.copy_xq_t, steps.tanh, steps.gelu = square_x2, copy_xq_t, tanh, gelu
    steps.square_y, steps.round_y, steps.copy_yq_t = square_y, round_y, copy_yq_t
    return steps


def ffn_tensor(pe, S, M, F):
    steps = Names()
    ats, qs, ys = (F.slots[k] for k in ("at", "xq", "yq"))

    def bank(use):
        if F.before[use] is not None:
            pe.wait_ge(*read_of(S, F.before[use]))
        return F.banks[:, F.bank[use], :]

    def project_out(t, c):
        if c == 0:
            bank(("wo", t, 0))
            pe.wait_ge(S.f_h[t], 32)
        last = pe.matmul(F.banks[:, F.bank["wo", t, 0], :], F.at[:, t % ats, c, :], M.wo[:, c, :],
                         start=(c == 0), stop=(c == HC - 1))
        if c == HC - 1:
            last.then_inc(S.wo, 1)

    def transpose_xq(t):
        out = bank(("xt", t, 0)).bitcast(BF16)
        pe.wait_ge(S.xq, t + 1)
        for c in range(DC):
            last = pe.transpose(out[:, c * P:(c + 1) * P], F.xq[:, t % qs, c * P:(c + 1) * P], M.ident_bf[:])
        last.then_inc(S.xq_tr, 1)

    def product_1(t, n):
        out = bank(("u", t, n))
        pe.wait_ge(S.xq_t, t + 1)
        for c in range(DC):
            last = pe.matmul(out, F.xq_t[:, t % qs, c * P:(c + 1) * P], M.w1q[:, c, n * BANK:(n + 1) * BANK],
                             start=(c == 0), stop=(c == DC - 1))
        last.then_inc(S.u_ps, 1)

    def transpose_yq(t, half):
        out = bank(("yt", t, half)).bitcast(BF16)
        pe.wait_ge(S.yq, t + 1)
        for c in range(IC // 2):
            ic = half * IC // 2 + c
            last = pe.transpose(out[:, c * P:(c + 1) * P], F.yq[:, t % ys, ic * P:(ic + 1) * P], M.ident_bf[:])
        last.then_inc(S.yq_tr, 1)

    def product_2(t, half):
        if half == 0:
            bank(("f2", t, 0))
        pe.wait_ge(S.yq_t, 2 * t + half + 1)
        for c in range(half * IC // 2, (half + 1) * IC // 2):
            last = pe.matmul(F.banks[:, F.bank["f2", t, 0], :], F.yq_t[:, t % ys, c * P:(c + 1) * P],
                             M.w2q[:, c, :], start=(c == 0), stop=(c == IC - 1), skip_group_check=True)
        if half == 1:
            last.then_inc(S.o_ps, 1)

    def run(kind, t, n, piece):
        if kind == "wo":
            project_out(t, piece)
        elif kind == "xt":
            transpose_xq(t)
        elif kind == "u":
            product_1(t, n)
        elif kind == "yt":
            transpose_yq(t, n)
        else:
            product_2(t, piece)

    steps.run = run
    return steps


def feed_forward(nc, S, M, A, b, tag):
    with ExitStack() as ctx:
        def sb(name, shape, dt=F32):
            return ctx.enter_context(nc.sbuf_tensor(name + tag, shape, dt))

        def steps(*stages):
            return [(stage, s - lag) for s in range(TB + max(lag for _, lag in stages))
                    for stage, lag in stages if 0 <= s - lag < TB]

        banks = ctx.enter_context(nc.psum_tensor("ffn_banks" + tag, [P, 8, BANK], F32))
        kinds = steps(("wo", 0), ("xt", 1), ("u", 1), ("yt", 4), ("f2", 4))
        order = [(kind, t, n) for kind, t in kinds for n in range({"u": UC, "yt": 2}.get(kind, 1))]
        F = ffn_memory(sb, banks, plan_banks(order, {"wo": (0,), "xt": (1,), "u": (2, 3, 4), "yt": (5, 6),
                                                     "f2": (7,)}), slots=FFN_SLOTS_ALONE)
        block = ctx.enter_context(nc.Block())

        @block.sync
        def _(sp):
            tail = output_sync(sp, S, A, M, b * SEQ)
            tail.spread_sums(KV_HEADS - 1, SECOND_HALF, 0)
            ffn = ffn_sync(sp, S, A, F, b * SEQ)
            for stage, t in steps((ffn.load, 0), (ffn.store, 5)):
                stage(t)
                if stage is ffn.load and t == 0:
                    tail.place_reciprocals(SECOND_HALF, 0)
                if stage is ffn.load and t == 2:
                    tail.place_outputs(KV_HEADS - 1, SECOND_HALF, 0)
                    sp.wait_ge(S.at, 16 * REP)
            ffn.wait_stores()

        @block.gpsimd
        def _(pool):
            normalise_outputs(pool, S, M, KV_HEADS - 1, SECOND_HALF, 0)
            ffn = ffn_gpsimd(pool, S, M, F)
            for stage, t in steps((ffn.rstd_h1, 0), (ffn.rms_x2, 0), (ffn.scale_g, 2), (ffn.add_b2, 1),
                                  (ffn.rms_y, 3)):
                stage(t)

        @block.vector
        def _(dve):
            n = [0]

            def link(ins):
                n[0] += 1
                ins.then_inc(S.f_vec, 1)
                dve.wait_ge(S.f_vec, n[0])

            reciprocals(dve, S, M, SECOND_HALF, 0)
            ffn = ffn_vector(dve, S, M, F, link)

            def chunks(*per_chunk):
                def run(t):
                    for stage in per_chunk:
                        for c in range(UC):
                            stage(t, c)
                return run

            for stage, t in steps((ffn.scale_x2, 1), (ffn.quantise_x2, 1), (chunks(ffn.stats_g), 2),
                                  (ffn.variance_g, 2),
                                  (ffn.residual, 0), (ffn.stats_h1, 0), (ffn.norm_x2, 0),
                                  (ffn.scale_y, 4), (chunks(ffn.dequantise_u), 1), (ffn.quantise_y, 4),
                                  (chunks(ffn.max_y), 3), (ffn.silu, 1), (ffn.finish, 5), (ffn.max_x2, 0)):
                stage(t)

        @block.scalar
        def _(act):
            ffn = ffn_scalar(act, S, M, F)

            def copy_yq_t(t):
                for half in range(2):
                    ffn.copy_yq_t(t, half)

            for stage, t in steps((ffn.copy_xq_t, 1), (ffn.square_x2, 0), (ffn.round_y, 4), (ffn.tanh, 1),
                                  (ffn.square_y, 3), (copy_yq_t, 4), (ffn.gelu, 1)):
                stage(t)

        @block.tensor
        def _(pe):
            ffn = ffn_tensor(pe, S, M, F)
            for kind, t, n in order:
                for piece in range({"wo": HC, "f2": 2}.get(kind, 1)):
                    ffn.run(kind, t, n, piece)


def lm_tower(nc, x_row, x_col, W, delta_t, tokens, wq, wk, wv, wo, w1t, b1, ln_g, ln_b, w2t, b2, out):
    with ExitStack() as ctx:
        setup, batch, batch_range = semaphores(nc, ctx)

        def sb(name, shape, dt=F32):
            return ctx.enter_context(nc.sbuf_tensor(name, shape, dt))

        def dram(name, shape, dt=F32):
            return nc.dram_tensor(name, shape, dt, kind="Internal").ap()

        A = Names()
        A.x_row = x_row
        A.x_col = x_col
        A.W = W
        A.delta_t = delta_t
        A.tokens = tokens
        A.wq = wq
        A.wk = wk
        A.wv = wv
        A.wo = wo
        A.w1t = w1t
        A.b1 = b1
        A.ln_g = ln_g
        A.ln_b = ln_b
        A.w2t = w2t
        A.b2 = b2
        A.out = out
        A.attn_dram = dram("attn_dram", [HEADS * HD, TOKENS])
        A.rows_dram = dram("rows_dram", [TOKENS])
        A.h_dram = dram("h_dram", [TOKENS, D])
        A.q_dram = dram("q_dram", [3, HC, P, SEQ], BF16)
        A.k_dram = dram("k_dram", [3, P, SEQ], BF16)
        A.max_dram = dram("max_dram", [MAX_ROWS, REP * SEQ], BF16)
        A.sum_dram = dram("sum_dram", [REP * SEQ])
        A.rec_dram = dram("rec_dram", [REP * SEQ])
        M = Names()
        M.ident = sb("ident", [P, P])
        M.ident_bf = sb("ident_bf", [P, P], BF16)
        M.neg_half = sb("neg_half", [P, 1])
        M.round_c = sb("round_c", [P, 1])
        M.idx_all = sb("idx_all", [P, NT], U32)
        M.idx_b = sb("idx_b", [P, TB], U32)
        M.tok = sb("tok", [P, 1])
        M.d_hm = sb("d_hm", [P, D], BF16)
        M.d_lo = sb("d_lo", [P, D], BF16)
        M.wq = sb("wq_sb", [P, DC, HEADS * HD])
        M.wk = sb("wk_sb", [P, DC, KV_HEADS * HD])
        M.wv = sb("wv_sb", [P, DC, KV_HEADS * HD])
        M.wo = sb("wo_sb", [P, HC, D])
        M.b1 = sb("b1_sb", [P, INNER])
        M.ln_g = sb("ln_g_sb", [P, INNER])
        M.ln_b = sb("ln_b_sb", [P, INNER])
        M.b2 = sb("b2_sb", [P, D])
        M.w1q = sb("w1q", [P, DC, INNER], BF16)
        M.w2q = sb("w2q", [P, IC, D], BF16)
        M.w_mean = sb("w_mean", [P, 2])
        M.w_dq = sb("w_dq", [P, 2])
        M.v = sb("v", [P, TB, KV_HEADS, VW])

        M.o = sb("o", [P, 2, SEQ])
        M.on = sb("on", [P, SEQ])
        M.sums = sb("sums", [P, REP * SEQ // P])
        M.rec = sb("rec", [P, REP * SEQ // P])
        M.rec_rows = sb("rec_rows", [P, SEQ])

        def attention(b, tag, later):
            stage1 = plan_stage1(ffn_share if later else lambda x: 1)
            with ExitStack() as shared:
                T = attention_memory(nc, shared, stage1, tag)
                project(nc, batch, M, A, T, b, tag, with_tail=later)
                attend(nc, batch, setup, M, A, T, b, tag, with_ffn=later)
            nc.all_engine_barrier(sems_to_clear=batch_range)

        set_up(nc, setup, M, A)
        attention(0, "_first", later=False)
        with nc.Fori(1, BATCH) as b:
            attention(b, "_loop", later=True)
        feed_forward(nc, batch, M, A, BATCH - 1, "_last")


def kernel(**inputs):
    import numpy as _np
    import concourse.bacc as _bacc
    from concourse import mybir as _mybir
    from concourse.bass_utils import run_bass_kernel_spmd as _run

    a = {k: _np.asarray(v) for k, v in inputs.items()}
    x = a["x"]
    n_train, dim = a["L0_tok_token_indices"].shape[0], a["L0_tok_W"].shape[1]
    laid_out = {
        "x_row": x.reshape(-1),
        "x_col": x.reshape(-1, 128).T,
        "W": a["L0_tok_W"],
        "delta_t": a["L0_tok_delta_values"].reshape(dim, n_train).T,
        "tokens": a["L0_tok_token_indices"].reshape(n_train, 1),
        "wq": a["L0_attn_Wq"], "wk": a["L0_attn_Wk"], "wv": a["L0_attn_Wv"], "wo": a["L0_attn_Wo"],
        "w1t": a["L0_ffn_w1"].T, "b1": a["L0_ffn_b1"], "ln_g": a["L0_ffn_ln_g"], "ln_b": a["L0_ffn_ln_b"],
        "w2t": a["L0_ffn_w2"].T, "b2": a["L0_ffn_b2"],
    }
    nc = _bacc.Bacc("TRN2", target_bir_lowering=False, num_devices=1)
    arrays, args = {}, []
    for name, v in laid_out.items():
        v = _np.ascontiguousarray(v)
        arrays[f"in_{name}"] = v
        args.append(nc.dram_tensor(f"in_{name}", v.shape, _mybir.dt.from_np(v.dtype), kind="ExternalInput").ap())
    out = nc.dram_tensor("out_0", (x.size, dim), _mybir.dt.from_np(_np.dtype("float32")), kind="ExternalOutput").ap()
    lm_tower(nc, *args, out)
    r = _run(nc, [arrays], core_ids=[0])
    return r.results[0]["out_0"].reshape(*x.shape, dim)
```
